# Optimizing a Trainium2 kernel written in Bass

```python
import numpy as np
import jax
import jax.numpy as jnp

def _softmax(x, axis=-1):
    return jax.nn.softmax(x, axis=axis)

def _gelu(x):
    return jax.nn.gelu(x, approximate=True)

def _silu(x):
    return jax.nn.silu(x)

def _sigmoid(x):
    return jax.nn.sigmoid(x)

def _layernorm(x, axis=-1, eps=1e-05):
    m = jnp.mean(x, axis=axis, keepdims=True)
    v = jnp.var(x, axis=axis, keepdims=True)
    return (x - m) / jnp.sqrt(v + eps)

def _scatter_add(tgt, idx, src, axis=0):
    return tgt.at[idx].add(src)

def _segment_sum(src, seg, n):
    return jax.ops.segment_sum(src, seg, n)
kernel_name = 'mk_hybrid_d1_jaxref_r8_dca770'

def setup_inputs(seed: int=0):
    np.random.seed(seed)
    _w = jnp.asarray

    def _L0_attn_a_setup():
        import jax, jax.numpy as jnp
        import numpy as np
        B, S, D = (2, 256, 256)
        H = 16
        Q_LORA, KV_LORA = (192, 64)
        ROPE_DIM, NOPE_DIM, V_DIM = (64, 64, 128)
        Q_HEAD_DIM = NOPE_DIM + ROPE_DIM
        ROPE_THETA, ROPE_RATIO = (10000.0, 1.0)

        def _rope_tables(seq_len):
            half = ROPE_DIM // 2
            inv_freq = ROPE_RATIO / ROPE_THETA ** (jnp.arange(half, dtype=jnp.float32) * 2.0 / ROPE_DIM)
            freqs = jnp.arange(seq_len, dtype=jnp.float32)[:, None] * inv_freq[None, :]
            return (jnp.cos(freqs), jnp.sin(freqs))

        def _apply_rope(x, cos, sin):
            x_even = x[..., 0::2]
            x_odd = x[..., 1::2]
            r_even = x_even * cos - x_odd * sin
            r_odd = x_odd * cos + x_even * sin
            return jnp.stack([r_even, r_odd], axis=-1).reshape(x.shape)
        key = jax.random.key(seed)
        ks = jax.random.split(key, 6)
        std = 0.02
        return {'hidden_states': jax.random.normal(ks[0], (B, S, D), jnp.float32), 'Wqa': jax.random.normal(ks[1], (D, Q_LORA), jnp.float32) * std, 'Wqb': jax.random.normal(ks[2], (Q_LORA, H * Q_HEAD_DIM), jnp.float32) * std, 'Wkva': jax.random.normal(ks[3], (D, KV_LORA + ROPE_DIM), jnp.float32) * std, 'Wkvb': jax.random.normal(ks[4], (KV_LORA, H * (NOPE_DIM + V_DIM)), jnp.float32) * std, 'Wo': jax.random.normal(ks[5], (H * V_DIM, D), jnp.float32) * std}
    _L0_attn_a_in = _L0_attn_a_setup()

    def _L0_attn_b_setup():
        import jax, jax.numpy as jnp
        import numpy as np
        from jax import lax
        B, L, D = (2, 256, 256)
        H, DK, DV, K = (16, 128, 128, 4)
        Q_DIM = H * DK
        V_DIM = H * DV

        def silu(x):
            return x * jax.nn.sigmoid(x)

        def causal_dwconv(x, w, b):
            Kk = w.shape[1]
            xp = jnp.pad(x, ((0, 0), (Kk - 1, 0), (0, 0)))
            kern = w.T[:, None, :]
            y = lax.conv_general_dilated(xp, kern, window_strides=(1,), padding='VALID', dimension_numbers=('NWC', 'WIO', 'NWC'), feature_group_count=w.shape[0])
            return y + b

        def layernorm(x, w, b, eps=1e-05):
            m = jnp.mean(x, axis=-1, keepdims=True)
            var = jnp.mean((x - m) ** 2, axis=-1, keepdims=True)
            return (x - m) * lax.rsqrt(var + eps) * w + b
        key = jax.random.key(seed)
        ks = jax.random.split(key, 16)
        s = 0.02
        f32 = jnp.float32
        return {'hidden_states': jax.random.normal(ks[0], (B, L, D), f32), 'Wq': jax.random.normal(ks[1], (D, Q_DIM), f32) * s, 'Wk': jax.random.normal(ks[2], (D, Q_DIM), f32) * s, 'Wv': jax.random.normal(ks[3], (D, V_DIM), f32) * s, 'Wb': jax.random.normal(ks[4], (D, H), f32) * s, 'bb': jnp.full((H,), -2.0, f32), 'Wg': jax.random.normal(ks[5], (D, V_DIM), f32) * s, 'Wo': jax.random.normal(ks[6], (V_DIM, D), f32) * s, 'qconv_w': jax.random.normal(ks[7], (Q_DIM, K), f32) * 0.5, 'qconv_b': jnp.zeros((Q_DIM,), f32), 'kconv_w': jax.random.normal(ks[8], (Q_DIM, K), f32) * 0.5, 'kconv_b': jnp.zeros((Q_DIM,), f32), 'qn_w': jnp.ones((DK,), f32), 'qn_b': jnp.zeros((DK,), f32), 'kn_w': jnp.ones((DK,), f32), 'kn_b': jnp.zeros((DK,), f32)}
    _L0_attn_b_in = _L0_attn_b_setup()

    def _L0_ffn_setup():
        import jax, jax.numpy as jnp
        import numpy as np
        B, S, H, E, K, I = (2, 128, 256, 32, 8, 96)
        key = jax.random.key(seed)
        ks = jax.random.split(key, 5)
        scaled = lambda k, shp, fan: jax.random.normal(k, shp, jnp.float32) * fan ** (-0.5)
        return {'hidden_states': jax.random.normal(ks[0], (B, S, H), jnp.float32), 'router_w': scaled(ks[1], (E, H), H), 'w_gate': scaled(ks[2], (E, H, I), H), 'w_up': scaled(ks[3], (E, H, I), H), 'w_down': scaled(ks[4], (E, I, H), I)}
    _L0_ffn_in = _L0_ffn_setup()
    _d = {'L0_attn_a_hidden_states': _L0_attn_a_in['hidden_states'], 'L0_attn_a_Wqa': _L0_attn_a_in['Wqa'], 'L0_attn_a_Wqb': _L0_attn_a_in['Wqb'], 'L0_attn_a_Wkva': _L0_attn_a_in['Wkva'], 'L0_attn_a_Wkvb': _L0_attn_a_in['Wkvb'], 'L0_attn_a_Wo': _L0_attn_a_in['Wo'], 'L0_attn_b_Wq': _L0_attn_b_in['Wq'], 'L0_attn_b_Wk': _L0_attn_b_in['Wk'], 'L0_attn_b_Wv': _L0_attn_b_in['Wv'], 'L0_attn_b_Wb': _L0_attn_b_in['Wb'], 'L0_attn_b_bb': _L0_attn_b_in['bb'], 'L0_attn_b_Wg': _L0_attn_b_in['Wg'], 'L0_attn_b_Wo': _L0_attn_b_in['Wo'], 'L0_attn_b_qconv_w': _L0_attn_b_in['qconv_w'], 'L0_attn_b_qconv_b': _L0_attn_b_in['qconv_b'], 'L0_attn_b_kconv_w': _L0_attn_b_in['kconv_w'], 'L0_attn_b_kconv_b': _L0_attn_b_in['kconv_b'], 'L0_attn_b_qn_w': _L0_attn_b_in['qn_w'], 'L0_attn_b_qn_b': _L0_attn_b_in['qn_b'], 'L0_attn_b_kn_w': _L0_attn_b_in['kn_w'], 'L0_attn_b_kn_b': _L0_attn_b_in['kn_b'], 'L0_ffn_router_w': _L0_ffn_in['router_w'], 'L0_ffn_w_gate': _L0_ffn_in['w_gate'], 'L0_ffn_w_up': _L0_ffn_in['w_up'], 'L0_ffn_w_down': _L0_ffn_in['w_down']}
    _x0 = _d['L0_attn_a_hidden_states']
    _d['L0_attn_a_hidden_states'] = jax.random.normal(jax.random.fold_in(jax.random.key(seed), 1), (1, 1024, 256), dtype=_x0.dtype)
    del _x0
    return _d

def reference(L0_attn_a_hidden_states, L0_attn_a_Wqa, L0_attn_a_Wqb, L0_attn_a_Wkva, L0_attn_a_Wkvb, L0_attn_a_Wo, L0_attn_b_Wq, L0_attn_b_Wk, L0_attn_b_Wv, L0_attn_b_Wb, L0_attn_b_bb, L0_attn_b_Wg, L0_attn_b_Wo, L0_attn_b_qconv_w, L0_attn_b_qconv_b, L0_attn_b_kconv_w, L0_attn_b_kconv_b, L0_attn_b_qn_w, L0_attn_b_qn_b, L0_attn_b_kn_w, L0_attn_b_kn_b, L0_ffn_router_w, L0_ffn_w_gate, L0_ffn_w_up, L0_ffn_w_down):

    def _L0_attn_a_ref(hidden_states, Wqa, Wqb, Wkva, Wkvb, Wo):
        import jax, jax.numpy as jnp
        import numpy as np
        B, S, D = (2, 256, 256)
        H = 16
        Q_LORA, KV_LORA = (192, 64)
        ROPE_DIM, NOPE_DIM, V_DIM = (64, 64, 128)
        Q_HEAD_DIM = NOPE_DIM + ROPE_DIM
        ROPE_THETA, ROPE_RATIO = (10000.0, 1.0)

        def _rope_tables(seq_len):
            half = ROPE_DIM // 2
            inv_freq = ROPE_RATIO / ROPE_THETA ** (jnp.arange(half, dtype=jnp.float32) * 2.0 / ROPE_DIM)
            freqs = jnp.arange(seq_len, dtype=jnp.float32)[:, None] * inv_freq[None, :]
            return (jnp.cos(freqs), jnp.sin(freqs))

        def _apply_rope(x, cos, sin):
            x_even = x[..., 0::2]
            x_odd = x[..., 1::2]
            r_even = x_even * cos - x_odd * sin
            r_odd = x_odd * cos + x_even * sin
            return jnp.stack([r_even, r_odd], axis=-1).reshape(x.shape)
        b, s, _ = hidden_states.shape
        scale = Q_HEAD_DIM ** (-0.5)
        q_latent = hidden_states @ Wqa
        q = (q_latent @ Wqb).reshape(b, s, H, Q_HEAD_DIM)
        q = jnp.transpose(q, (0, 2, 1, 3))
        q_nope, q_pe = (q[..., :NOPE_DIM], q[..., NOPE_DIM:])
        kv_comp = hidden_states @ Wkva
        c_kv, k_pe = (kv_comp[..., :KV_LORA], kv_comp[..., KV_LORA:])
        cos, sin = _rope_tables(s)
        q_pe = _apply_rope(q_pe, cos, sin)
        k_pe = _apply_rope(k_pe, cos, sin)
        kv = (c_kv @ Wkvb).reshape(b, s, H, NOPE_DIM + V_DIM)
        kv = jnp.transpose(kv, (0, 2, 1, 3))
        k_nope, v = (kv[..., :NOPE_DIM], kv[..., NOPE_DIM:])
        k_pe_b = jnp.broadcast_to(k_pe[:, None], (b, H, s, ROPE_DIM))
        q_full = jnp.concatenate([q_nope, q_pe], axis=-1)
        k_full = jnp.concatenate([k_nope, k_pe_b], axis=-1)
        scores = jnp.einsum('bhqd,bhkd->bhqk', q_full, k_full) * scale
        causal = jnp.tril(jnp.ones((s, s), dtype=bool))
        scores = jnp.where(causal[None, None], scores, jnp.finfo(scores.dtype).min)
        probs = jax.nn.softmax(scores, axis=-1)
        attn = jnp.einsum('bhqk,bhkd->bhqd', probs, v)
        out = jnp.transpose(attn, (0, 2, 1, 3)).reshape(b, s, H * V_DIM)
        return out @ Wo

    def _L0_attn_b_ref(hidden_states, Wq, Wk, Wv, Wb, bb, Wg, Wo, qconv_w, qconv_b, kconv_w, kconv_b, qn_w, qn_b, kn_w, kn_b):
        import jax, jax.numpy as jnp
        import numpy as np
        from jax import lax
        B, L, D = (2, 256, 256)
        H, DK, DV, K = (16, 128, 128, 4)
        Q_DIM = H * DK
        V_DIM = H * DV

        def silu(x):
            return x * jax.nn.sigmoid(x)

        def causal_dwconv(x, w, b):
            Kk = w.shape[1]
            xp = jnp.pad(x, ((0, 0), (Kk - 1, 0), (0, 0)))
            kern = w.T[:, None, :]
            y = lax.conv_general_dilated(xp, kern, window_strides=(1,), padding='VALID', dimension_numbers=('NWC', 'WIO', 'NWC'), feature_group_count=w.shape[0])
            return y + b

        def layernorm(x, w, b, eps=1e-05):
            m = jnp.mean(x, axis=-1, keepdims=True)
            var = jnp.mean((x - m) ** 2, axis=-1, keepdims=True)
            return (x - m) * lax.rsqrt(var + eps) * w + b
        Bs, Ls, Ds = hidden_states.shape
        q = hidden_states @ Wq
        k = hidden_states @ Wk
        v = hidden_states @ Wv
        beta = jax.nn.sigmoid(hidden_states @ Wb + bb)
        gate = silu(hidden_states @ Wg)
        q = silu(causal_dwconv(q, qconv_w, qconv_b))
        k = silu(causal_dwconv(k, kconv_w, kconv_b))
        q = layernorm(q.reshape(Bs, Ls, H, DK), qn_w, qn_b)
        k = layernorm(k.reshape(Bs, Ls, H, DK), kn_w, kn_b)
        v = v.reshape(Bs, Ls, H, DV)
        qs = q.transpose(1, 0, 2, 3)
        ks_ = k.transpose(1, 0, 2, 3)
        vs = v.transpose(1, 0, 2, 3)
        bs = beta.transpose(1, 0, 2)
        S0 = jnp.zeros((Bs, H, DV, DK), hidden_states.dtype)

        def step(S, inp):
            q_t, k_t, v_t, b_t = inp
            b = b_t[..., None, None]
            S = (1.0 - b) * S + b * (v_t[..., :, None] * k_t[..., None, :])
            o_t = jnp.einsum('bhvk,bhk->bhv', S, q_t)
            return (S, o_t)
        _, os = lax.scan(step, S0, (qs, ks_, vs, bs))
        o = os.transpose(1, 0, 2, 3).reshape(Bs, Ls, H * DV)
        o = o * gate
        return o @ Wo

    def _L0_ffn_ref(hidden_states, router_w, w_gate, w_up, w_down):
        import jax, jax.numpy as jnp
        import numpy as np
        B, S, H, E, K, I = (2, 128, 256, 32, 8, 96)
        Bq, Sq, Hd = hidden_states.shape
        x = hidden_states.reshape(-1, Hd)
        logits = x @ router_w.T
        probs = jax.nn.softmax(logits.astype(jnp.float32), axis=-1)
        rw, sel = jax.lax.top_k(probs, K)
        rw = rw / jnp.sum(rw, axis=-1, keepdims=True)
        rw = rw.astype(x.dtype)

        def body(acc, operand):
            e, wg, wu, wd = operand
            w_e = jnp.sum(jnp.where(sel == e, rw, jnp.zeros_like(rw)), axis=-1)
            h = jax.nn.silu(x @ wg) * (x @ wu)
            return (acc + h @ wd * w_e[:, None], None)
        acc0 = jnp.zeros_like(x)
        acc, _ = jax.lax.scan(body, acc0, (jnp.arange(E), w_gate, w_up, w_down))
        return acc.reshape(Bq, Sq, Hd)
    x = L0_attn_a_hidden_states
    x = x + _L0_attn_a_ref(_layernorm(x, axis=-1), L0_attn_a_Wqa, L0_attn_a_Wqb, L0_attn_a_Wkva, L0_attn_a_Wkvb, L0_attn_a_Wo)
    x = x + _L0_ffn_ref(_layernorm(x, axis=-1), L0_ffn_router_w, L0_ffn_w_gate, L0_ffn_w_up, L0_ffn_w_down)
    x = x + _L0_attn_b_ref(_layernorm(x, axis=-1), L0_attn_b_Wq, L0_attn_b_Wk, L0_attn_b_Wv, L0_attn_b_Wb, L0_attn_b_bb, L0_attn_b_Wg, L0_attn_b_Wo, L0_attn_b_qconv_w, L0_attn_b_qconv_b, L0_attn_b_kconv_w, L0_attn_b_kconv_b, L0_attn_b_qn_w, L0_attn_b_qn_b, L0_attn_b_kn_w, L0_attn_b_kn_b)
    x = x + _L0_ffn_ref(_layernorm(x, axis=-1), L0_ffn_router_w, L0_ffn_w_gate, L0_ffn_w_up, L0_ffn_w_down)
    return x

_drawn_inputs = setup_inputs


def setup_inputs(seed=0):
    import zlib

    import numpy as np

    out = dict(_drawn_inputs(seed))
    spreads = {'L0_attn_b_bb': (-2.0, 0.6),
     'L0_attn_b_qconv_b': (0.0, 0.8),
     'L0_attn_b_kconv_b': (0.0, 0.8),
     'L0_attn_b_qn_w': (1.0, 0.6),
     'L0_attn_b_qn_b': (0.0, 2.0),
     'L0_attn_b_kn_w': (1.0, 0.6),
     'L0_attn_b_kn_b': (0.0, 2.0)}
    factors = {'L0_attn_a_Wqa': 8.0,
     'L0_attn_a_Wqb': 8.0,
     'L0_attn_a_Wkva': 6.107,
     'L0_attn_a_Wkvb': 5.744,
     'L0_attn_a_Wo': 5.968,
     'L0_attn_b_Wq': 3.118,
     'L0_attn_b_Wk': 3.181,
     'L0_attn_b_Wv': 2.743,
     'L0_attn_b_Wb': 8.0,
     'L0_attn_b_Wg': 2.772,
     'L0_attn_b_Wo': 2.737,
     'L0_attn_b_qconv_w': 3.112,
     'L0_attn_b_kconv_w': 3.11}
    for name, (base, spread) in spreads.items():
        noise = np.random.default_rng([zlib.crc32(name.encode()), seed]).standard_normal(out[name].shape)
        drawn = base * np.exp(spread * noise) if base else spread * noise
        out[name] = jnp.asarray(drawn.astype(out[name].dtype))
    for name, factor in factors.items():
        out[name] = (out[name] * factor).astype(out[name].dtype)
    return out
```

```python
from contextlib import ExitStack

import numpy as np

import concourse.bass as bass
from concourse import mybir

F32 = mybir.dt.float32
F32R = mybir.dt.float32r
BF16 = mybir.dt.bfloat16
ALU = mybir.AluOpType
ACT = mybir.ActivationFunctionType
AX_X = mybir.AxisListType.X
ds = bass.ds

P = 128
S, D = 1024, 256
NT = S // P
KD = D // P
HALF = 512
EPS = 1e-5

HA, QLORA, KVLORA, ROPE, NOPE, VDIM = 16, 192, 64, 64, 64, 128
QCH = QLORA // 2
QSCALE = float(NOPE + ROPE) ** -0.5
HG = 4
NEG = -1.0e37

E, TOPK, INNER = 32, 8, 96
GE = 4
GC = GE * INNER // P
NG = E // GE

HB, DK, DV, TAPS = 16, 128, 128, 4


def mm3(pe, out, lhs, rhs, start, stop):
    pe.matmul(out, lhs[0], rhs[0], start=start, stop=False)
    pe.matmul(out, lhs[0], rhs[1], start=False, stop=False)
    return pe.matmul(out, lhs[1], rhs[0], start=False, stop=stop)


class Memory:

    def __init__(self, nc, ctx):
        self.nc, self.ctx, self.sems = nc, ctx, []

    def sb(self, name, shape, dt=F32, ctx=None):
        return (ctx or self.ctx).enter_context(self.nc.sbuf_tensor(name, shape, dt))

    def ps(self, name, shape, dt=F32, ctx=None):
        return (ctx or self.ctx).enter_context(self.nc.psum_tensor(name, shape, dt))

    def sem(self, name):
        self.sems.append(self.nc.alloc_semaphore(name))
        return self.sems[-1]

    def recycle(self):
        self.nc.clear_and_free_semaphores(self.sems)
        self.nc.all_engine_barrier()
        self.sems = []


def load_stage(m, a):
    nc = m.nc
    m.x = m.sb("x", [P, NT, D])
    m.h_hi = m.sb("h_hi", [P, KD, S], F32R)
    m.h_lo = m.sb("h_lo", [P, KD, S], F32R)
    m.ident = m.sb("ident", [P, P])
    m.identb = m.sb("identb", [P, P], BF16)
    m.neghalf = m.sb("neghalf", [P, 2 * NT])
    loaded = m.sem("load_x")
    made = m.sem("load_made")
    with nc.Block() as block:

        @block.sync
        def _(sp):
            sp.dma_start(m.ident[:, :], a["ident"]).then_inc(loaded, 16)
            sp.dma_start(m.x[:, :, :], a["x"].rearrange("b (t p) d -> p (b t) d", p=P)).then_inc(loaded, 16)
            sp.wait_ge(loaded, 32)

        @block.vector
        def _(dve):
            dve.memset(m.neghalf[:, :], -0.5)
            dve.wait_ge(loaded, 32)
            dve.tensor_copy(m.identb[:, :], m.ident[:, :]).then_inc(made, 1)
            dve.wait_ge(made, 1)


def norm_stage(m, tag):
    nc = m.nc
    with ExitStack() as ctx:
        stats = m.sb(f"{tag}_stats", [P, NT, 6], F32, ctx)
        mv = m.sb(f"{tag}_mv", [P, NT, 2], F32, ctx)
        ve = m.sb(f"{tag}_ve", [P, NT], F32, ctx)
        rstd = m.sb(f"{tag}_rstd", [P, NT], F32, ctx)
        hn = m.sb(f"{tag}_hn", [P, NT, D], F32, ctx)
        hT = m.ps(f"{tag}_hT", [P, KD, S], F32, ctx)
        stats_done = m.sem(f"{tag}_stats_done")
        aggr_done = m.sem(f"{tag}_aggr_done")
        var_done = m.sem(f"{tag}_var_done")
        rstd_done = m.sem(f"{tag}_rstd_done")
        hn_done = m.sem(f"{tag}_hn_done")
        hT_done = m.sem(f"{tag}_hT_done")
        hi_done = m.sem(f"{tag}_hi_done")
        pieces = [(half, k) for half in range(2) for k in range(KD)]
        with nc.Block() as block:

            @block.vector
            def _(dve):
                for t in range(NT):
                    dve.bn_stats(stats[:, t, :], m.x[:, t, :]).then_inc(stats_done, 1)
                for t in range(NT):
                    dve.wait_ge(stats_done, t + 1)
                    dve.bn_aggr(mv[:, t, :], stats[:, t, :]).then_inc(aggr_done, 1)
                dve.wait_ge(aggr_done, NT)
                dve.tensor_scalar(ve[:, :], mv[:, :, 1], EPS, None, ALU.add).then_inc(var_done, 1)
                dve.wait_ge(rstd_done, 1)
                for t in range(NT):
                    dve.tensor_scalar(hn[:, t, :], m.x[:, t, :], mv[:, t, 0:1], rstd[:, t:t + 1],
                                      ALU.subtract, ALU.mult).then_inc(hn_done, 1)
                for n, (half, k) in enumerate(pieces):
                    at = slice(half * HALF, (half + 1) * HALF)
                    dve.wait_ge(hi_done, n + 1)
                    dve.tensor_tensor(m.h_lo[:, k, at], hT[:, k, at], m.h_hi[:, k, at].bitcast(F32), ALU.subtract)

            @block.gpsimd
            def _(pool):
                pool.wait_ge(var_done, 1)
                pool.tensor_tensor(rstd[:, :], ve[:, :], m.neghalf[:, 0:NT], ALU.pow).then_inc(rstd_done, 1)

            @block.tensor
            def _(pe):
                for t in range(NT):
                    pe.wait_ge(hn_done, t + 1)
                    for k in range(KD):
                        pe.transpose(hT[:, k, t * P:(t + 1) * P], hn[:, t, k * P:(k + 1) * P],
                                     m.ident[:, :]).then_inc(hT_done, 1)

            @block.scalar
            def _(act):
                for half, k in pieces:
                    at = slice(half * HALF, (half + 1) * HALF)
                    act.wait_ge(hT_done, (half + 1) * (NT // 2) * KD - (KD - 1 - k))
                    act.activation(m.h_hi[:, k, at], hT[:, k, at], ACT.Copy).then_inc(hi_done, 1)


def moe_stage(m, a, tag):
    nc = m.nc
    with ExitStack() as ctx:
        def sb(name, shape, dt=F32):
            return m.sb(f"{tag}_{name}", shape, dt, ctx)

        def sem(name):
            return m.sem(f"{tag}_{name}")

        rw = sb("rw", [E, D])
        rwT_hi = sb("rwT_hi", [P, KD, E], F32R)
        rwT_lo = sb("rwT_lo", [P, KD, E], F32R)
        top = sb("top", [P, NT, TOPK])
        stat = sb("stat", [P, 4, NT])
        lg = sb("lg", [P, NT, E])
        pr = sb("pr", [P, NT, E])
        rest = sb("rest", [P, NT, E])
        wT = sb("wT", [E, S])
        wT_dram = m.wT_dram[tag]
        raw = [sb(f"raw{b}", [P, 3, GC * D]) for b in range(2)]
        w_hi = [sb(f"w_hi{b}", [P, 3, GC * D], F32R) for b in range(2)]
        w_lo = [sb(f"w_lo{b}", [P, 3, GC * D], F32R) for b in range(2)]
        wb = [sb(f"wb{b}", [P, GC, S]) for b in range(2)]
        s = sb("s", [P, 2, HALF])
        sw = sb("sw", [P, 2, HALF])
        act_f = sb("act_f", [P, 2, HALF])
        act_hi = sb("act_hi", [P, 2, HALF], F32R)
        act_lo = sb("act_lo", [P, 2, HALF], F32R)
        yT = sb("yT", [P, KD, S])
        zero_r = sb("zero_r", [P, HALF], F32R)

        acc = m.ps(f"{tag}_acc", [P, KD, S], F32, ctx)
        gu = m.ps(f"{tag}_gu", [P, 2, 2, HALF], F32, ctx)
        lg_ps = gu[:, 0, 0, 0:NT * E].rearrange("p (t e) -> p t e", e=E)
        rwT_ps = gu[:, 0, 1, 0:KD * E].rearrange("p (k e) -> p k e", e=E)
        wT_ps = gu[0:E, 1, :, :].rearrange("p a b -> p (a b)")
        y_ps = gu[:, :, :, :].rearrange("p a b c -> p (a b c)").rearrange("p (t d) -> p t d", d=D)

        rw_in, rwT_done, rwT_hi_done, rwT_lo_done = sem("rw_in"), sem("rwT_done"), sem("rwT_hi_done"), sem("rwT_lo_done")
        lg_done, soft, exp_done, wT_done, wT_sb_done, wT_stored = (
            sem("lg_done"), sem("soft"), sem("exp_done"), sem("wT_done"), sem("wT_sb_done"), sem("wT_stored"))
        raw_in = [sem(f"raw_in{b}") for b in range(2)]
        wb_in = [sem(f"wb_in{b}") for b in range(2)]
        hi_split, lo_split = sem("hi_split"), sem("lo_split")
        picked, replaced = sem("picked"), sem("replaced")
        s_done, sw_done, gu_done = sem("s_done"), sem("sw_done"), sem("gu_done")
        act_done, act_hi_done, act_lo_done, down_done = sem("act_done"), sem("act_hi_done"), sem("act_lo_done"), sem("down_done")
        zeroed = sem("zeroed")
        y_done, yT_done, yt_done = sem("y_done"), sem("yT_done"), sem("yt_done")

        UNITS = 2 * GC
        gate_r = a["w_gate"].rearrange("e (k p) i -> k p e i", p=P)
        up_r = a["w_up"].rearrange("e (k p) i -> k p e i", p=P)
        down_r = a["w_down"].rearrange("e i d -> (e i) d").rearrange("(c p) d -> p c d", p=P)

        def weight(parts, b, kind, k, c):
            base = k * GE * INNER + c * P
            return [part[b][:, kind, base:base + P] for part in parts]

        with nc.Block() as block:

            @block.sync
            def _(sp):
                sp.dma_start(rw[:, :], a["router_w"]).then_inc(rw_in, 16)

                def load_weights(g, b):
                    for k in range(KD):
                        for kind, src in ((0, gate_r), (1, up_r)):
                            dst = raw[b][:, kind, k * GE * INNER:(k + 1) * GE * INNER]
                            sp.dma_start(dst.rearrange("p (e i) -> p e i", i=INNER),
                                         src[k, :, ds(g * GE, GE), :]).then_inc(raw_in[b], 16)
                    sp.dma_start(raw[b][:, 2, :].rearrange("p (c d) -> p c d", d=D),
                                 down_r[:, ds(g * GC, GC), :]).then_inc(raw_in[b], 16)

                def load_routing(g, b):
                    for e in range(GE):
                        for c in range(GC):
                            lo, hi = max(e * INNER, c * P), min((e + 1) * INNER, (c + 1) * P)
                            if lo < hi:
                                sp.dma_start(wb[b][lo - c * P:hi - c * P, c, :],
                                             wT_dram[ds(g * GE + e, 1), :].partition_broadcast(hi - lo)
                                             .rearrange("p a s -> p (a s)")).then_inc(wb_in[b], 16)

                load_weights(0, 0)
                load_weights(1, 1)
                sp.wait_ge(wT_sb_done, 2)
                sp.dma_start(wT_dram, wT[:, :]).then_inc(wT_stored, 16)
                sp.wait_ge(wT_stored, 16)
                load_routing(0, 0)
                load_routing(1, 1)

                def step(i):
                    for b in range(2):
                        g = 2 * i + b
                        sp.wait_ge(lo_split, g + 3)
                        sp.wait_ge(hi_split, g + 3)
                        load_weights(g + 2, b)
                        sp.wait_ge(sw_done, UNITS * (g + 1) + 2)
                        load_routing(g + 2, b)

                with sp.Fori(0, NG // 2 - 1) as i:
                    step(i)

            @block.tensor
            def _(pe):
                pe.wait_ge(rw_in, 16)
                for k in range(KD):
                    pe.transpose(rwT_ps[:, k, :], rw[:, k * P:(k + 1) * P], m.ident[0:E, 0:E]).then_inc(rwT_done, 1)
                pe.wait_ge(rwT_lo_done, 1)
                for t in range(NT):
                    for k in range(KD):
                        tok = slice(t * P, (t + 1) * P)
                        last = mm3(pe, lg_ps[:, t, :], (m.h_hi[:, k, tok], m.h_lo[:, k, tok]),
                                   (rwT_hi[:, k, :], rwT_lo[:, k, :]), k == 0, k == KD - 1)
                last.then_inc(lg_done, 1)
                pe.wait_ge(soft, 7)
                for t in range(NT):
                    pe.transpose(wT_ps[:, t * P:(t + 1) * P], rest[:, t, :], m.ident[:, :]).then_inc(wT_done, 1)
                pe.wait_ge(zeroed, 1)
                for k in range(KD):
                    for half in range(2):
                        pe.matmul(acc[:, k, half * HALF:(half + 1) * HALF], zero_r[:, 0:P], zero_r[:, :],
                                  start=True, stop=False)
                pe.wait_ge(wT_sb_done, 2)

                def gate_up(i, b, u):
                    n = (2 * i + b) * UNITS + u
                    c, half = u // 2, u % 2
                    if u == 0:
                        pe.wait_ge(hi_split, 2 * i + b + 3)
                        pe.wait_ge(lo_split, 2 * i + b + 3)
                    pe.wait_ge(act_done, n + 1)
                    tok = slice(half * HALF, (half + 1) * HALF)
                    for kind in range(2):
                        for k in range(KD):
                            last = mm3(pe, gu[:, half, kind, :], weight((w_hi, w_lo), b, kind, k, c),
                                       (m.h_hi[:, k, tok], m.h_lo[:, k, tok]), k == 0, k == KD - 1)
                        last.then_inc(gu_done, 1)

                def down(i, b, u):
                    n = (2 * i + b) * UNITS + u
                    c, half = u // 2, u % 2
                    pe.wait_ge(act_lo_done, n + 3)
                    for k in range(KD):
                        base = c * D + k * P
                        last = mm3(pe, acc[:, k, half * HALF:(half + 1) * HALF],
                                   [part[b][:, 2, base:base + P] for part in (w_hi, w_lo)],
                                   (act_hi[:, half, :], act_lo[:, half, :]), False, False)
                    last.then_inc(down_done, 1)

                def step(i, first=False):
                    for b in range(2):
                        for u in range(UNITS):
                            gate_up(i, b, u)
                            if u >= LAG:
                                down(i, b, u - LAG)
                            elif b == 1:
                                down(i, 0, UNITS + u - LAG)
                            elif not first:
                                down(i - 1, 1, UNITS + u - LAG)

                LAG = 2
                step(0, first=True)
                with pe.Fori(1, NG // 2) as i:
                    step(i)
                for u in range(UNITS - LAG, UNITS):
                    down(NG // 2 - 1, 1, u)
                for k in range(KD):
                    for half in range(2):
                        pe.matmul(acc[:, k, half * HALF:(half + 1) * HALF], zero_r[:, 0:P], zero_r[:, :],
                                  start=False, stop=True).then_inc(y_done, 1)
                for t in range(NT):
                    pe.wait_ge(yT_done, (t // (NT // 2) + 1) * KD)
                    for k in range(KD):
                        pe.transpose(y_ps[:, t, k * P:(k + 1) * P], yT[:, k, t * P:(t + 1) * P],
                                     m.ident[:, :]).then_inc(yt_done, 1)

            @block.scalar
            def _(act):
                act.wait_ge(rwT_done, KD)
                act.activation(rwT_hi[:, :, :], rwT_ps, ACT.Copy).then_inc(rwT_hi_done, 1)
                act.wait_ge(soft, 2)
                act.activation(pr[:, :, :], lg[:, :, :], ACT.Exp).then_inc(exp_done, 1)

                def split(i, b):
                    act.wait_ge(raw_in[b], 16 * 5 * (i + 1))
                    act.activation(w_hi[b][:, :, :], raw[b][:, :, :], ACT.Copy).then_inc(hi_split, 1)

                act.sem_inc(hi_split, 2)
                act.sem_inc(s_done, 2)
                act.sem_inc(act_hi_done, 2)
                split(0, 0)
                act.wait_ge(wT_done, NT)
                for half in range(2):
                    act.activation(wT[:, half * HALF:(half + 1) * HALF], wT_ps[:, half * HALF:(half + 1) * HALF],
                                   ACT.Copy).then_inc(wT_sb_done, 1)

                def silu(i, b, u):
                    n = (2 * i + b) * UNITS + u
                    act.wait_ge(gu_done, 2 * n + 1)
                    act.wait_ge(sw_done, n + 1)
                    act.activation(s[:, u % 2, :], gu[:, u % 2, 0, :], ACT.Silu).then_inc(s_done, 1)

                def hi(i, b, u):
                    n = (2 * i + b) * UNITS + u
                    act.wait_ge(act_done, n + 3)
                    act.wait_ge(down_done, n + 1)
                    act.activation(act_hi[:, u % 2, :], act_f[:, u % 2, :], ACT.Copy).then_inc(act_hi_done, 1)

                def step(i, last=False):
                    for b in range(2):
                        for u in range(UNITS):
                            silu(i, b, u)
                            hi(i, b, u)
                            if u == 2 and not (last and b == 1):
                                act.wait_ge(down_done, UNITS * (2 * i + b) + 2)
                                split(*((i, 1) if b == 0 else (i + 1, 0)))

                act.preload_act_table(ACT.Silu)
                with act.Fori(0, NG // 2 - 1) as i:
                    step(i)
                step(NG // 2 - 1, last=True)
                for half in range(2):
                    for k in range(KD):
                        act.wait_ge(y_done, 2 * KD)
                        at = slice(half * HALF, (half + 1) * HALF)
                        act.activation(yT[:, k, at], acc[:, k, at], ACT.Copy).then_inc(yT_done, 1)

            @block.vector
            def _(dve):
                dve.memset(zero_r[:, :].bitcast(F32), 0.0).then_inc(zeroed, 1)
                dve.wait_ge(rwT_hi_done, 1)
                dve.tensor_tensor(rwT_lo[:, :, :], rwT_ps, rwT_hi[:, :, :].bitcast(F32),
                                  ALU.subtract).then_inc(rwT_lo_done, 1)
                dve.wait_ge(lg_done, 1)
                dve.tensor_reduce(stat[:, 0, :], lg_ps, AX_X, ALU.max).then_inc(soft, 1)
                dve.wait_ge(soft, 1)
                dve.tensor_tensor(lg[:, :, :], lg_ps, stat[:, 0, :].unsqueeze(2).to_broadcast([P, NT, E]),
                                  ALU.subtract).then_inc(soft, 1)
                dve.wait_ge(exp_done, 1)
                dve.tensor_reduce(stat[:, 1, :], pr[:, :, :], AX_X, ALU.add).then_inc(soft, 1)
                dve.wait_ge(soft, 3)
                dve.reciprocal(stat[:, 2, :], stat[:, 1, :]).then_inc(soft, 1)
                dve.wait_ge(soft, 4)
                dve.tensor_tensor(pr[:, :, :], pr[:, :, :], stat[:, 2, :].unsqueeze(2).to_broadcast([P, NT, E]),
                                  ALU.mult).then_inc(soft, 1)
                dve.wait_ge(soft, 5)
                for t in range(NT):
                    dve.max(top[:, t, :], pr[:, t, :]).then_inc(picked, 1)
                for t in range(NT):
                    dve.wait_ge(picked, t + 1)
                    dve.match_replace(rest[:, t, :], top[:, t, :], pr[:, t, :], 0.0).then_inc(replaced, 1)
                dve.tensor_reduce(stat[:, 3, :], top[:, :, :], AX_X, ALU.add).then_inc(picked, 1)
                dve.wait_ge(picked, NT + 1)
                dve.reciprocal(stat[:, 0, :], stat[:, 3, :]).then_inc(picked, 1)
                dve.wait_ge(replaced, NT)
                dve.tensor_tensor(pr[:, :, :], pr[:, :, :], rest[:, :, :], ALU.subtract).then_inc(soft, 1)
                dve.wait_ge(picked, NT + 2)
                dve.wait_ge(soft, 6)
                dve.tensor_tensor(rest[:, :, :], pr[:, :, :], stat[:, 0, :].unsqueeze(2).to_broadcast([P, NT, E]),
                                  ALU.mult).then_inc(soft, 1)

                def split(i, b):
                    dve.wait_ge(hi_split, 2 * i + b + 3)
                    dve.tensor_tensor(w_lo[b][:, :, :], raw[b][:, :, :], w_hi[b][:, :, :].bitcast(F32),
                                      ALU.subtract).then_inc(lo_split, 1)

                dve.sem_inc(lo_split, 2)
                dve.sem_inc(act_done, 2)
                dve.sem_inc(act_lo_done, 2)
                split(0, 0)

                def product(i, b, u):
                    n = (2 * i + b) * UNITS + u
                    dve.wait_ge(sw_done, n + 3)
                    dve.wait_ge(gu_done, 2 * n + 2)
                    dve.wait_ge(act_lo_done, n + 1)
                    dve.tensor_tensor(act_f[:, u % 2, :], gu[:, u % 2, 1, :], sw[:, u % 2, :],
                                      ALU.mult).then_inc(act_done, 1)

                def lo(i, b, u):
                    n = (2 * i + b) * UNITS + u
                    dve.wait_ge(act_hi_done, n + 3)
                    dve.tensor_tensor(act_lo[:, u % 2, :], act_f[:, u % 2, :], act_hi[:, u % 2, :].bitcast(F32),
                                      ALU.subtract).then_inc(act_lo_done, 1)

                def step(i, last=False):
                    for b in range(2):
                        for u in range(UNITS):
                            product(i, b, u)
                            lo(i, b, u)
                            if u == 2 and not (last and b == 1):
                                split(*((i, 1) if b == 0 else (i + 1, 0)))

                with dve.Fori(0, NG // 2 - 1) as i:
                    step(i)
                step(NG // 2 - 1, last=True)
                for t in range(NT):
                    dve.wait_ge(yt_done, 2 * KD * (t // 2 + 1))
                    dve.tensor_tensor(m.x[:, t, :], m.x[:, t, :], y_ps[:, t, :], ALU.add)

            @block.gpsimd
            def _(pool):
                pool.sem_inc(sw_done, 2)
                pool.sem_inc(down_done, 2)

                def step(i):
                    for b in range(2):
                        for u in range(UNITS):
                            n = (2 * i + b) * UNITS + u
                            if u == 0:
                                pool.wait_ge(wb_in[b], 16 * 6 * (i + 1))
                            pool.wait_ge(s_done, n + 3)
                            pool.wait_ge(act_done, n + 1)
                            half = slice((u % 2) * HALF, (u % 2 + 1) * HALF)
                            pool.tensor_tensor(sw[:, u % 2, :], s[:, u % 2, :], wb[b][:, u // 2, half],
                                               ALU.mult).then_inc(sw_done, 1)

                with pool.Fori(0, NG // 2) as i:
                    step(i)


def attn_prepare(m, a, w, o):
    nc = m.nc
    with ExitStack() as ctx:
        def sb(name, shape, dt=F32):
            return m.sb(f"ap_{name}", shape, dt, ctx)

        def sem(name):
            return m.sem(f"ap_{name}")

        wqa, wkva = sb("wqa", [P, KD, QLORA]), sb("wkva", [P, KD, KVLORA + ROPE])
        wqa_hi, wqa_lo = sb("wqa_hi", [P, KD, QLORA], F32R), sb("wqa_lo", [P, KD, QLORA], F32R)
        wkva_hi, wkva_lo = sb("wkva_hi", [P, KD, P], F32R), sb("wkva_lo", [P, KD, P], F32R)
        wqb = sb("wqb", [QCH, 2, HA, P])
        wkvb = sb("wkvb", [KVLORA, HA, NOPE + VDIM])
        flat = o[:, :, :].rearrange("p j s -> p (j s)")
        wo = flat[:, 0:HA * D].rearrange("p (h n) -> p h n", h=HA)
        wqbT = flat[0:NOPE, HA * D:].rearrange("p (h n) -> p h n", h=HA)
        wvT = sb("wvT", [VDIM, HA, KVLORA])
        ktok = sb("ktok", [P, NT, P])
        turned = sb("turned", [P, NT, ROPE])
        mask = sb("mask", [P, 2, P])
        bank = m.ps("ap_bank", [P, 2, 4 * HALF], F32, ctx)

        w_in = {n: sem(f"{n}_in") for n in ("proj", "rope", "mask", "wqb", "wkvb", "wo")}
        hi_ready, lo_ready = sem("hi_ready"), sem("lo_ready")
        pe_job, act_job, dve_job = sem("pe_job"), sem("act_job"), sem("dve_job")
        chain = sem("chain")
        QLAT, KV, T0, KT, T1, FOLD, VT, VO0, VO1 = range(9)
        H2 = HA // 2

        def dve_jobs(job):
            return sum(n <= job for n in (QLAT, KV, KT, FOLD, VO0, VO1))

        def half_of(job):
            return bank[:, job % 2, :]

        def turned_view(job):
            return half_of(job)[0:NOPE].rearrange("p (h c) -> p h c", h=H2)

        with nc.Block() as block:

            @block.sync
            def _(sp):
                sp.dma_start(wqa[:, :, :], a["a_Wqa"].rearrange("(k p) n -> p k n", p=P)).then_inc(w_in["proj"], 16)
                sp.dma_start(wkva[:, :, :], a["a_Wkva"].rearrange("(k p) n -> p k n", p=P)).then_inc(w_in["proj"], 16)
                sp.dma_start(w["cos"][:, :, :], a["rope_cos"].rearrange("(t p) c -> p t c", p=P)).then_inc(w_in["rope"], 16)
                sp.dma_start(w["sin"][:, :, :], a["rope_sin"].rearrange("(t p) c -> p t c", p=P)).then_inc(w_in["rope"], 16)
                sp.dma_start(wqb[:, :, :, :], a["a_Wqb"].rearrange("(c p) (h n) -> p c h n", p=QCH, n=P)).then_inc(w_in["wqb"], 16)
                sp.dma_start(wkvb[:, :, :], a["a_Wkvb"].rearrange("p (h n) -> p h n", h=HA)).then_inc(w_in["wkvb"], 16)
                sp.dma_start(wo[:, :, :], a["a_Wo"].rearrange("(h p) n -> p h n", p=VDIM)).then_inc(w_in["wo"], 16)
                sp.dma_start(mask[:, 0, :], a["mask_qk"]).then_inc(w_in["mask"], 16)
                sp.dma_start(mask[:, 1, :], a["mask_kq"]).then_inc(w_in["mask"], 16)

            @block.tensor
            def _(pe):
                def free(job):
                    if job >= 2:
                        pe.wait_ge(act_job, job - 1)
                        pe.wait_ge(dve_job, dve_jobs(job - 2))

                pe.wait_ge(lo_ready, 2)
                for c in range(2):
                    for half in range(2):
                        for k in range(KD):
                            tok = slice(half * HALF, (half + 1) * HALF)
                            last = mm3(pe, half_of(QLAT)[0:QCH, (2 * c + half) * HALF:(2 * c + half + 1) * HALF],
                                       [p[:, k, c * QCH:(c + 1) * QCH] for p in (wqa_hi, wqa_lo)],
                                       (m.h_hi[:, k, tok], m.h_lo[:, k, tok]), k == 0, k == KD - 1)
                last.then_inc(pe_job, 1)
                for t in range(NT):
                    for k in range(KD):
                        tok = slice(t * P, (t + 1) * P)
                        last = mm3(pe, half_of(KV)[:, t * P:(t + 1) * P], (m.h_hi[:, k, tok], m.h_lo[:, k, tok]),
                                   (wkva_hi[:, k, :], wkva_lo[:, k, :]), k == 0, k == KD - 1)
                last.then_inc(pe_job, 1)

                def turn_heads(job, h0):
                    free(job)
                    for h in range(h0, h0 + H2):
                        out = turned_view(job)[:, h - h0, :]
                        for c in range(2):
                            pe.transpose(out[:, c * QCH:(c + 1) * QCH], wqb[:, c, h, 0:NOPE], m.ident[0:QCH, 0:QCH])
                        last = pe.transpose(out[:, QLORA:], wkvb[:, h, 0:NOPE], m.ident[0:KVLORA, 0:KVLORA])
                    last.then_inc(pe_job, 1)

                pe.wait_ge(w_in["wqb"], 16)
                pe.wait_ge(w_in["wkvb"], 16)
                turn_heads(T0, 0)
                free(KT)
                for t in range(NT):
                    last = pe.transpose(half_of(KT)[:, t * P:(t + 1) * P], ktok[:, t, :], m.ident[:, :])
                last.then_inc(pe_job, 1)
                turn_heads(T1, H2)
                pe.wait_ge(act_job, T1 + 1)
                free(FOLD)
                for c in range(2):
                    for h in range(HA):
                        last = pe.matmul(half_of(FOLD)[0:QCH, (c * HA + h) * KVLORA:(c * HA + h + 1) * KVLORA],
                                         wqbT[:, h, c * QCH:(c + 1) * QCH], wqbT[:, h, QLORA:], start=True, stop=True)
                last.then_inc(pe_job, 1)
                free(VT)
                for h in range(HA):
                    last = pe.transpose(half_of(VT)[:, h * KVLORA:(h + 1) * KVLORA], wkvb[:, h, NOPE:],
                                        m.ident[0:KVLORA, 0:KVLORA])
                last.then_inc(pe_job, 1)
                pe.wait_ge(w_in["wo"], 16)
                pe.wait_ge(act_job, VT + 1)
                for job in (VO0, VO1):
                    free(job)
                    for n in range(H2):
                        h = (job - VO0) * H2 + n
                        last = pe.matmul(half_of(job)[0:KVLORA, n * D:(n + 1) * D], wvT[:, h, :], wo[:, h, :],
                                         start=True, stop=True)
                    last.then_inc(pe_job, 1)

            @block.scalar
            def _(act):
                act.wait_ge(w_in["proj"], 32)
                act.activation(wqa_hi[:, :, :], wqa[:, :, :], ACT.Copy).then_inc(hi_ready, 1)
                act.activation(wkva_hi[:, :, :], wkva[:, :, :], ACT.Copy).then_inc(hi_ready, 1)
                act.wait_ge(w_in["wqb"], 16)
                act.activation(w["wq_hi"][:, :, :, NOPE:].rearrange("p c h n -> p (c h) n"),
                               wqb[:, :, :, NOPE:].rearrange("p c h n -> p (c h) n"), ACT.Copy).then_inc(hi_ready, 1)

                def begin(job):
                    act.wait_ge(pe_job, job + 1)

                begin(QLAT)
                act.activation(w["qlat_hi"][:, :, :], half_of(QLAT)[0:QCH].rearrange("p (c s) -> p c s", c=2),
                               ACT.Copy).then_inc(act_job, 1)
                begin(KV)
                kv = half_of(KV)[:, 0:NT * P].rearrange("p (t c) -> p t c", t=NT)
                act.activation(w["v_hi"][:, :, 0:KVLORA], kv[:, :, 0:KVLORA], ACT.Copy)
                act.activation(ktok[:, :, 0:KVLORA], kv[:, :, 0:KVLORA], ACT.Copy).then_inc(act_job, 1)
                begin(T0)
                act.activation(wqbT[:, 0:H2, :], turned_view(T0), ACT.Copy).then_inc(act_job, 1)
                begin(KT)
                act.activation(w["kT_hi"][:, :], half_of(KT)[:, 0:S], ACT.Copy).then_inc(act_job, 1)
                begin(T1)
                act.activation(wqbT[:, H2:, :], turned_view(T1), ACT.Copy).then_inc(act_job, 1)
                begin(FOLD)
                act.activation(w["wq_hi"][:, :, :, 0:NOPE].rearrange("p c h n -> p (c h) n"),
                               half_of(FOLD)[0:QCH].rearrange("p (g n) -> p g n", n=KVLORA),
                               ACT.Copy).then_inc(act_job, 1)
                begin(VT)
                act.activation(wvT[:, :, :], half_of(VT)[:, 0:HA * KVLORA].rearrange("p (h n) -> p h n", h=HA),
                               ACT.Copy).then_inc(act_job, 1)
                for job in (VO0, VO1):
                    begin(job)
                    pair = slice((job - VO0) * H2 // 2, (job - VO0 + 1) * H2 // 2)
                    vo = half_of(job)[0:KVLORA].rearrange("p (j o d) -> p j o d", o=2, d=D)
                    for odd in range(2):
                        last = act.activation(w["vo_hi"][odd * KVLORA:(odd + 1) * KVLORA, pair, :], vo[:, :, odd, :], ACT.Copy)
                    last.then_inc(act_job, 1)

            @block.vector
            def _(dve):
                steps = [0]

                def link(instruction):
                    steps[0] += 1
                    instruction.then_inc(chain, 1)
                    dve.wait_ge(chain, steps[0])

                dve.memset(turned[:, :, :], 1.0)
                link(dve.memset(w["minus_one"][:, :], -1.0))
                dve.tensor_copy(w["v_hi"][:, :, KVLORA:], turned[:, :, :])
                dve.tensor_scalar(w["v_lo"][:, :, KVLORA:], turned[:, :, :], 0.0, None, ALU.mult)
                dve.tensor_copy(w["minus_one_r"][:, :], w["minus_one"][:, :])
                dve.wait_ge(hi_ready, 1)
                dve.tensor_tensor(wqa_lo[:, :, :], wqa[:, :, :], wqa_hi[:, :, :].bitcast(F32), ALU.subtract).then_inc(lo_ready, 1)
                dve.wait_ge(hi_ready, 2)
                dve.tensor_tensor(wkva_lo[:, :, :], wkva[:, :, :], wkva_hi[:, :, :].bitcast(F32), ALU.subtract).then_inc(lo_ready, 1)
                dve.wait_ge(w_in["mask"], 32)
                dve.tensor_copy(w["mask_qk"][:, :], mask[:, 0, :])
                dve.tensor_copy(w["mask_kq"][:, :, :], mask[:, 1, :].unsqueeze(1).to_broadcast([P, HG, P]))

                def after(job):
                    dve.wait_ge(pe_job, job + 1)
                    dve.wait_ge(act_job, job + 1)

                after(QLAT)
                dve.tensor_tensor(w["qlat_lo"][:, :, :], half_of(QLAT)[0:QCH].rearrange("p (c s) -> p c s", c=2),
                                  w["qlat_hi"][:, :, :].bitcast(F32), ALU.subtract).then_inc(dve_job, 1)
                after(KV)
                kv = half_of(KV)[:, 0:NT * P].rearrange("p (t c) -> p t c", t=NT)
                dve.tensor_tensor(w["v_lo"][:, :, 0:KVLORA], kv[:, :, 0:KVLORA],
                                  w["v_hi"][:, :, 0:KVLORA].bitcast(F32), ALU.subtract)
                dve.wait_ge(w_in["rope"], 32)
                pe_part = kv[:, :, KVLORA:]
                for odd in range(2):
                    dve.tensor_tensor(turned[:, :, odd::2], pe_part[:, :, 1 - odd::2], w["sin"][:, :, odd::2], ALU.mult)
                link(dve.tensor_tensor(ktok[:, :, KVLORA:], pe_part, w["cos"][:, :, :], ALU.mult))
                dve.tensor_tensor(ktok[:, :, KVLORA:], ktok[:, :, KVLORA:], turned[:, :, :], ALU.add).then_inc(dve_job, 1)
                after(KT)
                dve.tensor_tensor(w["kT_lo"][:, :], half_of(KT)[:, 0:S], w["kT_hi"][:, :].bitcast(F32),
                                  ALU.subtract).then_inc(dve_job, 1)
                dve.wait_ge(hi_ready, 3)
                dve.tensor_tensor(w["wq_lo"][:, :, :, NOPE:].rearrange("p c h n -> p (c h) n"),
                                  wqb[:, :, :, NOPE:].rearrange("p c h n -> p (c h) n"),
                                  w["wq_hi"][:, :, :, NOPE:].bitcast(F32).rearrange("p c h n -> p (c h) n"), ALU.subtract)
                after(FOLD)
                dve.tensor_tensor(w["wq_lo"][:, :, :, 0:NOPE].rearrange("p c h n -> p (c h) n"),
                                  half_of(FOLD)[0:QCH].rearrange("p (g n) -> p g n", n=KVLORA),
                                  w["wq_hi"][:, :, :, 0:NOPE].bitcast(F32).rearrange("p c h n -> p (c h) n"),
                                  ALU.subtract).then_inc(dve_job, 1)
                for job in (VO0, VO1):
                    after(job)
                    pair = slice((job - VO0) * H2 // 2, (job - VO0 + 1) * H2 // 2)
                    vo = half_of(job)[0:KVLORA].rearrange("p (j o d) -> p j o d", o=2, d=D)
                    for odd in range(2):
                        rows = slice(odd * KVLORA, (odd + 1) * KVLORA)
                        last = dve.tensor_tensor(w["vo_lo"][rows, pair, :], vo[:, :, odd, :],
                                                 w["vo_hi"][rows, pair, :].bitcast(F32), ALU.subtract)
                    last.then_inc(dve_job, 1)


def attn_stage(m, a):
    nc = m.nc
    with ExitStack() as ctx:
        w = {"vo_hi": m.sb("aw_vo_hi", [P, HA // 2, D], F32R, ctx), "vo_lo": m.sb("aw_vo_lo", [P, HA // 2, D], F32R, ctx)}
        o = m.sb("at_o", [P, HA // 2, S], F32, ctx)
        inner = ctx.enter_context(ExitStack())
        for name, shape, dt in (
                ("cos", [P, NT, ROPE], F32), ("sin", [P, NT, ROPE], F32),
                ("qlat_hi", [QCH, 2, S], F32R), ("qlat_lo", [QCH, 2, S], F32R),
                ("wq_hi", [QCH, 2, HA, P], F32R), ("wq_lo", [QCH, 2, HA, P], F32R),
                ("kT_hi", [P, S], F32R), ("kT_lo", [P, S], F32R),
                ("v_hi", [P, NT, P], F32R), ("v_lo", [P, NT, P], F32R),
                ("mask_qk", [P, P], BF16), ("mask_kq", [P, HG, P], BF16),
                ("minus_one", [P, P], F32), ("minus_one_r", [P, P], F32R)):
            w[name] = m.sb(f"aw_{name}", shape, dt, inner)
        attn_prepare(m, a, w, o)

        attn_units(m, w, o)
        inner.close()
        output_stage(m, "ao", o, w["vo_hi"], w["vo_lo"], HA // 2)


def attn_units(m, w, o):
    nc = m.nc
    with ExitStack() as ctx:
        def sb(name, shape, dt=F32):
            return m.sb(f"at_{name}", shape, dt, ctx)

        def sem(name):
            return m.sem(f"at_{name}")

        qt, swapped = sb("qt", [P, HG, P]), sb("swapped", [P, HG, ROPE])
        LAG = 3
        Q, R = 4, LAG + 1
        q_hi, q_lo = sb("q_hi", [P, Q, HALF], F32R), sb("q_lo", [P, Q, HALF], F32R)
        piece_max, row_max = sb("piece_max", [P, 2, HG, 2]), sb("row_max", [P, HG])
        shift = sb("shift", [P, Q, HG, P], F32R)
        p_f, p_hi, p_lo = sb("p_f", [P, 3, HALF]), sb("p_hi", [P, R, HALF], F32R), sb("p_lo", [P, R, HALF], F32R)
        sums, rec_few, rec = sb("sums", [KVLORA, HALF]), sb("rec_few", [KVLORA, HALF // 32]), sb("rec", [KVLORA, HG, P])
        qtok_ps = m.ps("at_qtok_ps", [P, HALF], F32, ctx)      
        qT_ps = m.ps("at_qT_ps", [P, HALF], F32, ctx)
        mx_ps = m.ps("at_mx_ps", [P, 2, HALF], F32, ctx)
        st_ps = m.ps("at_st_ps", [P, 2, HALF], F32, ctx)
        acc_ps = m.ps("at_acc_ps", [P, 2, HALF], F32, ctx)

        qtok_done, swap_done, rope_done, qT_done = sem("qtok_done"), sem("swap_done"), sem("rope_done"), sem("qT_done")
        q_hi_done, q_lo_done = sem("q_hi_done"), sem("q_lo_done")
        q_copied = sem("q_copied")
        mx_done, piece_done, row_max_done, shift_done = sem("mx_done"), sem("piece_done"), sem("row_max_done"), sem("shift_done")
        st_done, exp_done, p_hi_done, p_lo_done, pv_done = (
            sem("st_done"), sem("exp_done"), sem("p_hi_done"), sem("p_lo_done"), sem("pv_done"))
        sums_done, few_done, rec_done, norm_done = sem("sums_done"), sem("few_done"), sem("rec_done"), sem("norm_done")

        units = [(i, g) for i in range(NT) for g in range(HA // HG)]
        first = [sum(units[v][0] + 1 for v in range(u)) for u in range(len(units) + 1)]
        steps = [(u, j) for u, (i, g) in enumerate(units) for j in range(i + 1)]

        def pieces(u):
            keys = (units[u][0] + 1) * P
            return [(h, n, lo, min(lo + HALF, keys)) for h in range(HG) for n, lo in enumerate(range(0, keys, HALF))]

        first_piece = [sum(len(pieces(v)) for v in range(u)) for u in range(len(units))]

        def during(u):
            def of(v, parts):
                return [(v, *part) for part in parts] if 0 <= v < len(units) else []
            maxima = [("max", r, *p) for r, p in enumerate(pieces(u + 2))] if 0 <= u + 2 < len(units) else []
            half = len(maxima) // 2
            return (of(u + 3, [("turn",)]) + of(u + 2, maxima[:half]) + of(u + 4, [("queries",)])
                    + of(u + 2, maxima[half:]) + of(u + 2, [("shift",)]))

        before = [part for u in range(-4, 0) for part in during(u)]

        def between(k):
            u, j = steps[k]
            todo, n = during(u), units[u][0] + 1
            return todo[len(todo) * j // n:len(todo) * (j + 1) // n]

        with nc.Block() as block:

            @block.tensor
            def _(pe):
                def prepare(u, kind, *args):
                    i, g = units[u]
                    tok = slice(i * P, (i + 1) * P)
                    if kind == "queries":
                        if u >= 1:
                            pe.wait_ge(swap_done, u)
                        for c in range(2):
                            heads = slice(g * HG, (g + 1) * HG)
                            last = mm3(pe, qtok_ps[:, :], [w[q][:, c, tok] for q in ("qlat_hi", "qlat_lo")],
                                       [w[q][:, c, heads, :].rearrange("p h n -> p (h n)") for q in ("wq_hi", "wq_lo")],
                                       c == 0, c == 1)
                        last.then_inc(qtok_done, 1)
                    elif kind == "turn":
                        pe.wait_ge(rope_done, u + 1)
                        if u >= 1:
                            pe.wait_ge(q_lo_done, u)
                        for h in range(HG):
                            last = pe.transpose(qT_ps[:, h * P:(h + 1) * P], qt[:, h, :], m.ident[:, :])
                        last.then_inc(qT_done, 1)
                    elif kind == "max":
                        r, h, n, lo, hi = args
                        r += first_piece[u]
                        pe.wait_ge(q_hi_done, u + 1)
                        if r >= 2:
                            pe.wait_ge(piece_done, r - 1)
                        diagonal = hi == (i + 1) * P
                        last = pe.matmul(mx_ps[:, r % 2, 0:hi - lo], q_hi[:, u % Q, h * P:(h + 1) * P],
                                         w["kT_hi"][:, lo:hi], start=True, stop=not diagonal)
                        if diagonal:
                            last = pe.matmul(mx_ps[:, r % 2, hi - lo - P:hi - lo], m.identb[:, :], w["mask_qk"][:, :],
                                             start=False, stop=True)
                        last.then_inc(mx_done, 1)

                def scores(k):
                    u, j = steps[k]
                    if j == 0:
                        pe.wait_ge(q_lo_done, u + 1)
                        pe.wait_ge(shift_done, u + 1)
                    if k >= 2:
                        pe.wait_ge(exp_done, k - 1)
                    diagonal = j == units[u][0]
                    out = st_ps[:, k % 2, :]
                    mm3(pe, out, [w[q][:, j * P:(j + 1) * P] for q in ("kT_hi", "kT_lo")],
                        (q_hi[:, u % Q, :], q_lo[:, u % Q, :]), True, False)
                    last = pe.matmul(out, w["minus_one_r"][:, :], shift[:, u % Q, :, :].rearrange("p h q -> p (h q)"),
                                     start=False, stop=not diagonal)
                    if diagonal:
                        last = pe.matmul(out, m.identb[:, :], w["mask_kq"][:, :, :].rearrange("p h q -> p (h q)"),
                                         start=False, stop=True)
                    last.then_inc(st_done, 1)

                def values(k):
                    u, j = steps[k]
                    if j == 0 and u >= 2:
                        pe.wait_ge(norm_done, u - 1)
                    pe.wait_ge(p_lo_done, k + 1)
                    mm3(pe, acc_ps[:, u % 2, :], [w[q][:, j, :] for q in ("v_hi", "v_lo")],
                        (p_hi[:, k % R, :], p_lo[:, k % R, :]), j == 0, j == units[u][0]).then_inc(pv_done, 1)

                for part in before:
                    prepare(*part)
                for k in range(len(steps) + LAG):
                    if k < len(steps):
                        scores(k)
                        for part in between(k):
                            prepare(*part)
                    if k >= LAG:
                        values(k - LAG)

            @block.vector
            def _(dve):
                def prepare(u, kind, *args):
                    i, g = units[u]
                    if kind == "queries":
                        dve.wait_ge(q_copied, u + 1)
                        if u >= 1:
                            dve.wait_ge(qT_done, u)
                        q = qtok_ps[:, :].rearrange("p (h n) -> p h n", h=HG)[:, :, NOPE:]
                        for odd in range(2):
                            dve.tensor_tensor(swapped[:, :, odd::2], q[:, :, 1 - odd::2],
                                              w["sin"][:, i, odd::2].unsqueeze(1).to_broadcast([P, HG, ROPE // 2]), ALU.mult)
                        dve.tensor_tensor(qt[:, :, NOPE:], q, w["cos"][:, i, :].unsqueeze(1).to_broadcast([P, HG, ROPE]),
                                          ALU.mult).then_inc(swap_done, 1)
                        dve.wait_ge(swap_done, u + 1)
                        dve.tensor_tensor(qt[:, :, NOPE:], qt[:, :, NOPE:], swapped[:, :, :], ALU.add).then_inc(rope_done, 1)
                    elif kind == "turn":
                        dve.wait_ge(q_hi_done, u + 1)
                        dve.tensor_tensor(q_lo[:, u % Q, :], qT_ps[:, :], q_hi[:, u % Q, :].bitcast(F32),
                                          ALU.subtract).then_inc(q_lo_done, 1)
                    elif kind == "max":
                        r, h, n, lo, hi = args
                        r += first_piece[u]
                        dve.wait_ge(mx_done, r + 1)
                        if h == n == 0 and u >= 2:
                            dve.wait_ge(row_max_done, u - 1)
                        dve.tensor_reduce(piece_max[:, u % 2, h, n:n + 1], mx_ps[:, r % 2, 0:hi - lo], AX_X,
                                          ALU.max).then_inc(piece_done, 1)
                    else:
                        count = len(pieces(u))
                        dve.wait_ge(piece_done, first_piece[u] + count)
                        if u >= 1:
                            dve.wait_ge(shift_done, u)
                        dve.tensor_reduce(row_max[:, :], piece_max[:, u % 2, :, 0:count // HG], AX_X,
                                          ALU.max).then_inc(row_max_done, 1)

                def normalise(u):
                    dve.wait_ge(pv_done, first[u + 1])
                    acc = acc_ps[:, u % 2, :].rearrange("p (h q) -> p h q", h=HG)
                    dve.transpose(sums[:, :], acc_ps[KVLORA:, u % 2, :]).then_inc(sums_done, 1)
                    dve.wait_ge(sums_done, u + 1)
                    dve.reciprocal(rec_few[:, :], sums[:, ::32]).then_inc(few_done, 1)
                    dve.wait_ge(few_done, u + 1)
                    dve.transpose(rec[:, :, :].rearrange("p h q -> p (h q)"),
                                  rec_few[:, :].unsqueeze(2).to_broadcast([KVLORA, HALF // 32, 32])).then_inc(rec_done, 1)
                    dve.wait_ge(rec_done, u + 1)
                    i, g = units[u]
                    for odd in range(2):
                        last = dve.tensor_tensor(o[odd * KVLORA:(odd + 1) * KVLORA, g * HG // 2:(g + 1) * HG // 2,
                                                   i * P:(i + 1) * P],
                                                 acc[0:KVLORA, odd::2, :], rec[:, odd::2, :], ALU.mult)
                    last.then_inc(norm_done, 1)

                for part in before:
                    prepare(*part)
                for k in range(len(steps) + LAG):
                    if k < len(steps):
                        for part in between(k):
                            prepare(*part)
                    if k >= LAG:
                        u, j = steps[k - LAG]
                        if j == units[u][0]:
                            normalise(u)

            @block.gpsimd
            def _(pool):
                def prepare(u, kind, *args):
                    if kind == "shift":
                        pool.wait_ge(row_max_done, u + 1)
                        if u >= Q:
                            pool.wait_ge(st_done, first[u - Q + 1])
                        pool.tensor_tensor(shift[:, u % Q, :, :], m.ident[:, :].unsqueeze(1).to_broadcast([P, HG, P]),
                                           row_max[:, :].unsqueeze(2).to_broadcast([P, HG, P]),
                                           ALU.mult).then_inc(shift_done, 1)

                def low(k):
                    pool.wait_ge(p_hi_done, k + 1)
                    if k >= R:
                        pool.wait_ge(pv_done, k - R + 1)
                    pool.tensor_tensor(p_lo[:, k % R, :], p_f[:, k % 3, :], p_hi[:, k % R, :].bitcast(F32),
                                       ALU.subtract).then_inc(p_lo_done, 1)

                for part in before:
                    prepare(*part)
                for k in range(len(steps)):
                    for part in between(k):
                        prepare(*part)
                    low(k)

            @block.scalar
            def _(act):
                def prepare(u, kind, *args):
                    if kind == "queries":
                        act.wait_ge(qtok_done, u + 1)
                        if u >= 1:
                            act.wait_ge(qT_done, u)
                        act.activation(qt[:, :, 0:NOPE], qtok_ps[:, :].rearrange("p (h n) -> p h n", h=HG)[:, :, 0:NOPE],
                                       ACT.Copy).then_inc(q_copied, 1)
                    elif kind == "turn":
                        act.wait_ge(qT_done, u + 1)
                        if u >= Q:
                            act.wait_ge(st_done, first[u - Q + 1])
                        act.activation(q_hi[:, u % Q, :], qT_ps[:, :], ACT.Copy).then_inc(q_hi_done, 1)

                def exponent(k):
                    act.wait_ge(st_done, k + 1)
                    if k >= 3:
                        act.wait_ge(p_lo_done, k - 2)
                    act.activation(p_f[:, k % 3, :], st_ps[:, k % 2, :], ACT.Exp, scale=QSCALE).then_inc(exp_done, 1)

                def high(k):
                    act.wait_ge(exp_done, k + 1)
                    if k >= R:
                        act.wait_ge(pv_done, k - R + 1)
                    act.activation(p_hi[:, k % R, :], p_f[:, k % 3, :], ACT.Copy).then_inc(p_hi_done, 1)

                for part in before:
                    prepare(*part)
                for k in range(len(steps)):
                    exponent(k)
                    high(k)
                    for part in between(k):
                        prepare(*part)


def output_stage(m, tag, o, w_hi, w_lo, chunks, w_dram=None):
    nc = m.nc
    with ExitStack() as ctx:
        raw = m.sb(f"{tag}_raw", [P, chunks, D], F32, ctx) if w_dram is not None else None
        o_hi = m.sb(f"{tag}_o_hi", [P, 2, chunks, P], F32R, ctx)
        o_lo = m.sb(f"{tag}_o_lo", [P, 2, chunks, P], F32R, ctx)
        out_ps = m.ps(f"{tag}_out_ps", [P, NT, HALF], F32, ctx)
        o_hi_done, o_lo_done, out_done = m.sem(f"{tag}_o_hi_done"), m.sem(f"{tag}_o_lo_done"), m.sem(f"{tag}_out_done")
        w_in, w_hi_done, w_lo_done = m.sem(f"{tag}_w_in"), m.sem(f"{tag}_w_hi_done"), m.sem(f"{tag}_w_lo_done")
        pieces = [slice(n * chunks // 4, (n + 1) * chunks // 4) for n in range(4)] if w_dram is not None else []
        with nc.Block() as block:

            @block.sync
            def _(sp):
                for piece in pieces:
                    sp.dma_start(raw[:, piece, :], w_dram[:, piece, :]).then_inc(w_in, 16)
                if pieces:
                    sp.wait_ge(w_in, 16 * len(pieces))

            @block.scalar
            def _(act):
                def high(t):
                    if t >= 2:
                        act.wait_ge(out_done, t - 1)
                    act.activation(o_hi[:, t % 2, :, :], o[:, :, t * P:(t + 1) * P], ACT.Copy).then_inc(o_hi_done, 1)

                high(0)
                if pieces:
                    act.wait_ge(w_in, 16 * len(pieces))
                for piece in pieces:
                    act.activation(w_hi[:, piece, :], raw[:, piece, :], ACT.Copy).then_inc(w_hi_done, 1)
                for t in range(1, NT):
                    high(t)

            @block.tensor
            def _(pe):
                for t in range(NT):
                    pe.wait_ge(o_lo_done, t + 1)
                    for j in range(chunks):
                        if t == 0 and pieces and j % (chunks // 4) == 0:
                            pe.wait_ge(w_lo_done, j // (chunks // 4) + 1)
                        last = mm3(pe, out_ps[:, t, 0:D], (o_hi[:, t % 2, j, :], o_lo[:, t % 2, j, :]),
                                   (w_hi[:, j, :], w_lo[:, j, :]), j == 0, j == chunks - 1)
                    last.then_inc(out_done, 1)

            @block.vector
            def _(dve):
                def low(t):
                    dve.wait_ge(o_hi_done, t + 1)
                    dve.tensor_tensor(o_lo[:, t % 2, :, :], o[:, :, t * P:(t + 1) * P],
                                      o_hi[:, t % 2, :, :].bitcast(F32), ALU.subtract).then_inc(o_lo_done, 1)

                low(0)
                for n, piece in enumerate(pieces):
                    dve.wait_ge(w_hi_done, n + 1)
                    dve.tensor_tensor(w_lo[:, piece, :], raw[:, piece, :], w_hi[:, piece, :].bitcast(F32),
                                      ALU.subtract).then_inc(w_lo_done, 1)
                for t in range(NT):
                    if t + 1 < NT:
                        low(t + 1)
                    dve.wait_ge(out_done, t + 1)
                    dve.tensor_tensor(m.x[:, t, :], m.x[:, t, :], out_ps[:, t, 0:D], ALU.add)


def value_stage(m, a, v_all, rows_dram):
    nc = m.nc
    with ExitStack() as ctx:
        def sb(name, shape, dt=F32):
            return m.sb(f"lv_{name}", shape, dt, ctx)

        def sem(name):
            return m.sem(f"lv_{name}")

        wb, wb_hi, wb_lo = sb("wb", [P, KD, HB]), sb("wb_hi", [P, KD, HB], F32R), sb("wb_lo", [P, KD, HB], F32R)
        bb = sb("bb", [P, HB])
        wv = sb("wv", [P, KD, HB * DV])
        wv_hi, wv_lo = sb("wv_hi", [P, KD, HB * DV], F32R), sb("wv_lo", [P, KD, HB * DV], F32R)
        z, ez = sb("z", [P, NT, HB]), sb("ez", [P, 2, NT, HB])
        beta, keep = sb("beta", [P, NT, HB]), sb("keep", [P, NT, HB])
        keepT, prodT, zeros = sb("keepT", [HB, S]), sb("prodT", [HB, S]), sb("zeros", [HB, P])
        z_ps = m.ps("lv_z_ps", [P, NT, HB], F32, ctx)
        keepT_ps = m.ps("lv_keepT_ps", [P, S], F32, ctx)
        v_ps = m.ps("lv_v_ps", [P, 4, HALF], F32, ctx)
        wb_loaded, wv_loaded, rows_stored = sem("wb_loaded"), sem("wv_loaded"), sem("rows_stored")
        hi_done, lo_done = sem("hi_done"), sem("lo_done")
        z_done, z_sb, ez_done, soft, keepT_done, keepT_sb, prod_done = (
            sem("z_done"), sem("z_sb"), sem("ez_done"), sem("soft"), sem("keepT_done"), sem("keepT_sb"), sem("prod_done"))
        v_done, v_out = sem("v_done"), sem("v_out")
        GV = HALF // DV
        NGV = HB // GV
        units = [(g, t) for g in range(NGV) for t in range(NT)]

        with nc.Block() as block:

            @block.sync
            def _(sp):
                sp.dma_start(wb[:, :, :], a["b_Wb"].rearrange("(k p) n -> p k n", p=P)).then_inc(wb_loaded, 16)
                sp.dma_start(bb[:, :], a["b_bb"].rearrange("(a n) -> a n", a=1).to_broadcast([P, HB])).then_inc(wb_loaded, 16)
                for g in range(NGV):
                    cols = slice(g * HALF, (g + 1) * HALF)
                    sp.dma_start(wv[:, :, cols], a["b_Wv"].rearrange("(k p) n -> p k n", p=P)[:, :, cols]).then_inc(wv_loaded, 16)
                    if g == 0:
                        sp.wait_ge(wv_loaded, 16)
                sp.wait_ge(keepT_sb, 1)
                sp.dma_start(rows_dram[0], keepT[:, :]).then_inc(rows_stored, 16)
                sp.wait_ge(prod_done, NT)
                sp.dma_start(rows_dram[1], prodT[:, :]).then_inc(rows_stored, 16)
                sp.wait_ge(rows_stored, 32)

            @block.tensor
            def _(pe):
                pe.wait_ge(lo_done, 1)
                for t in range(NT):
                    for k in range(KD):
                        tok = slice(t * P, (t + 1) * P)
                        last = mm3(pe, z_ps[:, t, :], (m.h_hi[:, k, tok], m.h_lo[:, k, tok]),
                                   (wb_hi[:, k, :], wb_lo[:, k, :]), k == 0, k == KD - 1)
                last.then_inc(z_done, 1)

                def value(n):
                    g, t = units[n]
                    tok = slice(t * P, (t + 1) * P)
                    if t == 0:
                        pe.wait_ge(lo_done, g + 2)
                    if n >= 4:
                        pe.wait_ge(v_out, n - 3)
                    for k in range(KD):
                        last = mm3(pe, v_ps[:, n % 4, :], (m.h_hi[:, k, tok], m.h_lo[:, k, tok]),
                                   [p[:, k, g * HALF:(g + 1) * HALF] for p in (wv_hi, wv_lo)], k == 0, k == KD - 1)
                    last.then_inc(v_done, 1)

                for n in range(len(units)):
                    if n == 4:
                        pe.wait_ge(soft, 4)
                        for t in range(NT):
                            last = pe.transpose(keepT_ps[0:HB, t * P:(t + 1) * P], keep[:, t, :], m.ident[:, :])
                        last.then_inc(keepT_done, 1)
                    value(n)

            @block.scalar
            def _(act):
                act.wait_ge(wb_loaded, 32)
                act.activation(wb_hi[:, :, :], wb[:, :, :], ACT.Copy).then_inc(hi_done, 1)

                def split(g):
                    cols = slice(g * HALF, (g + 1) * HALF)
                    act.wait_ge(wv_loaded, 16 if g == 0 else 16 * NGV)
                    act.activation(wv_hi[:, :, cols], wv[:, :, cols], ACT.Copy).then_inc(hi_done, 1)

                split(0)
                act.wait_ge(z_sb, 1)
                act.activation(ez[:, 0, :, :], z[:, :, :], ACT.Exp, scale=-1.0)
                act.activation(ez[:, 1, :, :], z[:, :, :], ACT.Exp).then_inc(ez_done, 1)
                for g in range(1, NGV):
                    split(g)
                act.wait_ge(keepT_done, 1)
                act.activation(keepT[:, :], keepT_ps[0:HB, :], ACT.Copy).then_inc(keepT_sb, 1)

            @block.vector
            def _(dve):
                dve.memset(zeros[:, :], 0.0)
                dve.wait_ge(hi_done, 1)
                dve.tensor_tensor(wb_lo[:, :, :], wb[:, :, :], wb_hi[:, :, :].bitcast(F32), ALU.subtract).then_inc(lo_done, 1)

                def split(g):
                    cols = slice(g * HALF, (g + 1) * HALF)
                    dve.wait_ge(hi_done, g + 2)
                    dve.tensor_tensor(wv_lo[:, :, cols], wv[:, :, cols], wv_hi[:, :, cols].bitcast(F32),
                                      ALU.subtract).then_inc(lo_done, 1)

                split(0)
                dve.wait_ge(z_done, 1)
                dve.tensor_tensor(z[:, :, :], z_ps[:, :, :], bb[:, :].unsqueeze(1).to_broadcast([P, NT, HB]),
                                  ALU.add).then_inc(z_sb, 1)
                dve.wait_ge(ez_done, 1)
                for n, out in enumerate((beta, keep)):
                    dve.tensor_scalar(ez[:, n, :, :], ez[:, n, :, :], 1.0, None, ALU.add).then_inc(soft, 1)
                for n, out in enumerate((beta, keep)):
                    dve.wait_ge(soft, n + 1)
                    dve.reciprocal(out[:, :, :], ez[:, n, :, :]).then_inc(soft, 1)
                dve.wait_ge(soft, 3)
                for n, (g, t) in enumerate(units):
                    if t == 4 and g + 1 < NGV:
                        split(g + 1)
                    if n == 6:
                        dve.wait_ge(keepT_sb, 1)
                        for c in range(NT):
                            at = slice(c * P, (c + 1) * P)
                            dve.tensor_tensor_scan(prodT[:, at], keepT[:, at], zeros[:, :], 1.0, ALU.mult,
                                                   ALU.add).then_inc(prod_done, 1)
                    dve.wait_ge(v_done, n + 1)
                    dve.tensor_tensor(v_all[:, g * GV:(g + 1) * GV, t * P:(t + 1) * P],
                                      v_ps[:, n % 4, :].rearrange("p (h v) -> p h v", v=DV),
                                      beta[:, t, g * GV:(g + 1) * GV].unsqueeze(2).to_broadcast([P, GV, DV]),
                                      ALU.mult).then_inc(v_out, 1)


def head_stage(m, a, v_all, rows_dram):
    nc = m.nc
    with ExitStack() as ctx:
        def sb(name, shape, dt=F32):
            return m.sb(f"lh_{name}", shape, dt, ctx)

        def sem(name):
            return m.sem(f"lh_{name}")

        raw = [sb(f"raw{b}", [P, 3, KD, DK]) for b in range(2)]
        conv = [sb(f"conv{b}", [P, 2, TAPS + 1]) for b in range(2)]
        w_hi = [sb(f"w_hi{b}", [P, 3, KD, DK], F32R) for b in range(2)]
        w_lo = [sb(f"w_lo{b}", [P, 3, KD, DK], F32R) for b in range(2)]
        norm = sb("norm", [P, 4])
        kn_rows = sb("kn_rows", [P, 2, DK])
        PAD = TAPS - 1
        pre = sb("pre", [P, 2, PAD + S])
        y = sb("y", [P, 2, S])
        yn = sb("yn", [P, 2, 4, DK])
        qT = [sb(f"qT{b}", [P, S]) for b in range(2)]
        kT = [sb(f"kT{b}", [P, S]) for b in range(2)]
        ktok = [sb(f"ktok{b}", [P, NT, DK]) for b in range(2)]
        gate = [sb(f"gate{b}", [P, S]) for b in range(2)]
        v = [sb(f"v{b}", [P, NT, DV]) for b in range(2)]
        prod = [sb(f"prod{b}", [P, S]) for b in range(2)]
        keep = sb("keep", [P, S])
        stats, mv = sb("stats", [P, 4, 6]), sb("mv", [P, 4, 2])
        ve, rstd, nbias = sb("ve", [P, 2, 4]), sb("rstd", [P, 2, 4]), sb("nbias", [P, 2, 4])
        decay, probs, qg = sb("decay", [P, S]), sb("probs", [P, S]), sb("qg", [P, S])
        vd = sb("vd", [P, NT, DV])
        state = sb("state", [P, NT, DV])

        proj_ps = m.ps("lh_proj_ps", [P, 2, HALF], F32, ctx)
        tok_ps = m.ps("lh_tok_ps", [P, 2, HALF], F32, ctx)
        back_ps = m.ps("lh_back_ps", [P, HALF], F32, ctx)
        sc_ps = m.ps("lh_sc_ps", [P, HALF], F32, ctx)
        ds_ps = m.ps("lh_ds_ps", [P, HALF], F32, ctx)
        o_ps = m.ps("lh_o_ps", [P, HALF], F32, ctx)

        consts_in, padded = sem("consts_in"), sem("padded")
        raw_in = [sem(f"raw_in{b}") for b in range(2)]
        v_in = [sem(f"v_in{b}") for b in range(2)]
        keep_in = sem("keep_in")
        w_hi_done, w_lo_done, proj_done = sem("w_hi_done"), sem("w_lo_done"), sem("proj_done")
        out_done, tap_done, silu_done, tok_done = sem("out_done"), sem("tap_done"), sem("silu_done"), sem("tok_done")
        stats_done, aggr_done, ve_done, rstd_done, nbias_done = (
            sem("stats_done"), sem("aggr_done"), sem("ve_done"), sem("rstd_done"), sem("nbias_done"))
        aggr_begun = sem("aggr_begun")
        yn_done, back_done, hat_done, kw_done, ktok_done = (
            sem("yn_done"), sem("back_done"), sem("hat_done"), sem("kw_done"), sem("ktok_done"))
        decay_done, sc_done, probs_done, vd_done, qg_done = (
            sem("decay_done"), sem("sc_done"), sem("probs_done"), sem("vd_done"), sem("qg_done"))
        ds_done, state_done, o_done, og_done = sem("ds_done"), sem("state_done"), sem("o_done"), sem("og_done")
        C_OUT, C_TAP, C_TOK, C_YN, C_BACK, C_HAT, C_KTOK = 2, 12, 4, 2, 2, 1, 2
        C_PROBS, C_VD, C_DS, C_STATE, C_O, C_OG = 1, 2, 2, 7, 2, 1
        PIECES = 6
        BLK = NT // 2

        def half_of(half):
            return slice(half * HALF, (half + 1) * HALF)

        def chunk(c):
            return slice(c * P, (c + 1) * P)

        with nc.Block() as block:

            @block.sync
            def _(sp):
                def load_weights(h, b):
                    for n, name in enumerate(("b_Wq", "b_Wk", "b_Wg")):
                        sp.dma_start(raw[b][:, n, :, :],
                                     a[name].rearrange("(k p) n -> p k n", p=P)[:, :, ds(h * DK, DK)]).then_inc(raw_in[b], 16)
                    sp.dma_start(conv[b][:, :, :].rearrange("p z c -> p (z c)"),
                                 a["conv"][ds(h, 1), :, :].rearrange("a p c -> p (a c)")).then_inc(raw_in[b], 16)

                def load_values(h, b):
                    sp.dma_start(v[b][:, :, :].rearrange("p c v -> p (c v)"),
                                 v_all[:, ds(h, 1), :].rearrange("p a s -> p (a s)")).then_inc(v_in[b], 16)
                    sp.dma_start(prod[b][:, :], rows_dram[1, ds(h, 1), :].to_broadcast([P, S])).then_inc(v_in[b], 16)

                def load_keep(h):
                    sp.dma_start(keep[:, :], rows_dram[0, ds(h, 1), :].to_broadcast([P, S])).then_inc(keep_in, 16)

                load_weights(0, 0)
                load_weights(1, 1)
                sp.dma_start(norm[:, :], a["norm"]).then_inc(consts_in, 16)
                for n, name in enumerate(("b_kn_w", "b_kn_b")):
                    sp.dma_start(kn_rows[:, n, :], a[name].rearrange("(a n) -> a n", a=1).to_broadcast([P, DK])).then_inc(consts_in, 16)
                load_values(0, 0)
                load_keep(0)

                def step(h, b, more):
                    if more:
                        sp.wait_ge(w_lo_done, h + 1)
                        sp.wait_ge(tap_done, 12 * (h + 1) + C_TAP)
                        load_weights(h + 2, b)
                    sp.wait_ge(o_done, 2 * h + C_O)
                    load_values(h + 1, 1 - b)
                    sp.wait_ge(decay_done, NT * (h + 1))
                    load_keep(h + 1)

                with sp.Fori(0, HB // 2 - 1) as i:
                    step(2 * i, 0, True)
                    step(2 * i + 1, 1, True)
                step(HB - 2, 0, False)

            @block.tensor
            def _(pe):
                pe.sem_inc(tok_done, C_TOK)
                pe.sem_inc(back_done, C_BACK)
                pe.sem_inc(ds_done, C_DS)
                pe.sem_inc(o_done, C_O)

                def project(h, b, n):
                    kind, half = n // 2, n % 2
                    pe.wait_ge(w_lo_done, h + 1)
                    pe.wait_ge(out_done, PIECES * h + n + 1)
                    for k in range(KD):
                        last = mm3(pe, proj_ps[:, n % 2, :], (w_hi[b][:, kind, k, :], w_lo[b][:, kind, k, :]),
                                   (m.h_hi[:, k, half_of(half)], m.h_lo[:, k, half_of(half)]), k == 0, k == KD - 1)
                    last.then_inc(proj_done, 1)

                def to_tokens(h, p):
                    pe.wait_ge(silu_done, 4 * h + p + 1)
                    pe.wait_ge(yn_done, 4 * h + p + 1)
                    for c in range(BLK):
                        at = chunk((p % 2) * BLK + c)
                        last = pe.transpose(tok_ps[:, p % 2, chunk(c)], y[:, p // 2, at], m.ident[:, :])
                    last.then_inc(tok_done, 1)

                def to_features(h, p):
                    pe.wait_ge(yn_done, 4 * h + p + 1 + C_YN)
                    pe.wait_ge(hat_done, 4 * h + p + 1)
                    for c in range(BLK):
                        last = pe.transpose(back_ps[:, chunk(c)], yn[:, p % 2, c, :], m.ident[:, :])
                    last.then_inc(back_done, 1)

                def scores(h, b, half):
                    pe.wait_ge(hat_done, 4 * h + 4 + C_HAT)
                    pe.wait_ge(probs_done, 2 * h + half + 1)
                    for c in range(BLK):
                        at = chunk(half * BLK + c)
                        last = pe.matmul(sc_ps[:, chunk(c)], kT[b][:, at], qT[b][:, at], start=True, stop=True)
                    last.then_inc(sc_done, 1)

                def state_change(h, b, half):
                    pe.wait_ge(ktok_done, 2 * h + 2 + C_KTOK)
                    pe.wait_ge(vd_done, 2 * h + half + 1 + C_VD)
                    pe.wait_ge(state_done, 7 * h + 4 * half + C_STATE)
                    for c in range(BLK):
                        n = half * BLK + c
                        if n < NT - 1:
                            last = pe.matmul(ds_ps[:, chunk(c)], ktok[b][:, n, :], vd[:, n, :], start=True, stop=True)
                    last.then_inc(ds_done, 1)

                def output(h, b, half):
                    pe.wait_ge(probs_done, 2 * h + half + 1 + C_PROBS)
                    pe.wait_ge(qg_done, 2 * h + half + 1)
                    pe.wait_ge(state_done, 7 * h + (3 if half == 0 else 7) + C_STATE)
                    pe.wait_ge(og_done, 2 * h + half + 1)
                    for c in range(BLK):
                        n = half * BLK + c
                        last = pe.matmul(o_ps[:, chunk(c)], v[b][:, n, :], probs[:, chunk(n)], start=True, stop=n == 0)
                        if n:
                            last = pe.matmul(o_ps[:, chunk(c)], state[:, n, :], qg[:, chunk(n)], start=False, stop=True)
                    last.then_inc(o_done, 1)

                def prepare(h, b):
                    for n in range(PIECES):
                        project(h, b, n)
                    for p in range(4):
                        to_tokens(h, p)
                        to_features(h, p)

                def step(h, b):
                    nh, nb = h + 1, 1 - b
                    project(nh, nb, 0)
                    project(nh, nb, 1)
                    scores(h, b, 0)
                    project(nh, nb, 2)
                    state_change(h, b, 0)
                    scores(h, b, 1)
                    project(nh, nb, 3)
                    to_tokens(nh, 0)
                    state_change(h, b, 1)
                    project(nh, nb, 4)
                    to_tokens(nh, 1)
                    output(h, b, 0)
                    project(nh, nb, 5)
                    to_features(nh, 0)
                    to_tokens(nh, 2)
                    to_features(nh, 1)
                    output(h, b, 1)
                    to_tokens(nh, 3)
                    to_features(nh, 2)
                    to_features(nh, 3)

                pe.wait_ge(consts_in, 48)
                prepare(0, 0)
                with pe.Fori(0, HB // 2 - 1) as i:
                    step(2 * i, 0)
                    step(2 * i + 1, 1)
                step(HB - 2, 0)
                h, b = HB - 1, 1
                for half in range(2):
                    scores(h, b, half)
                    state_change(h, b, half)
                for half in range(2):
                    output(h, b, half)

            @block.scalar
            def _(act):
                act.sem_inc(out_done, C_OUT)
                act.sem_inc(yn_done, C_YN)
                act.sem_inc(hat_done, C_HAT)

                def split(h, b, turn):
                    act.wait_ge(raw_in[b], 64 * (turn + 1))
                    act.activation(w_hi[b][:, :, :, :], raw[b][:, :, :, :], ACT.Copy).then_inc(w_hi_done, 1)

                def take(h, b, n):
                    kind, half = n // 2, n % 2
                    act.wait_ge(proj_done, PIECES * h + n + 1)
                    if kind < 2:
                        act.wait_ge(tap_done, 12 * h + C_TAP)
                        act.wait_ge(tok_done, 4 * h + C_TOK)
                        act.activation(pre[:, kind, PAD + half * HALF:PAD + (half + 1) * HALF], proj_ps[:, n % 2, :], ACT.Copy)
                        act.activation(y[:, kind, half_of(half)], proj_ps[:, n % 2, :], ACT.Identity,
                                       bias=conv[b][:, kind, TAPS:TAPS + 1],
                                       scale=conv[b][:, kind, TAPS - 1:TAPS]).then_inc(out_done, 1)
                    else:
                        act.wait_ge(og_done, 2 * h - 1)
                        act.activation(gate[b][:, half_of(half)], proj_ps[:, n % 2, :], ACT.Silu).then_inc(out_done, 1)

                def silu(h, p):
                    z, half = p // 2, p % 2
                    act.wait_ge(tap_done, 12 * h + 6 * z + 5 + half + C_TAP)
                    act.activation(y[:, z, half_of(half)], y[:, z, half_of(half)], ACT.Silu).then_inc(silu_done, 1)

                def normalise(h, p):
                    act.wait_ge(nbias_done, 4 * h + p + 1)
                    act.wait_ge(back_done, 4 * h + p + 1)
                    if p < 2:
                        act.wait_ge(ktok_done, 2 * h + p + 1)
                    for c in range(BLK):
                        last = act.activation(yn[:, p % 2, c, :], tok_ps[:, p % 2, chunk(c)], ACT.Identity,
                                              bias=nbias[:, p % 2, c:c + 1], scale=rstd[:, p % 2, c:c + 1])
                    last.then_inc(yn_done, 1)

                def hat(h, b, p):
                    z, half = p // 2, p % 2
                    act.wait_ge(back_done, 4 * h + p + 1 + C_BACK)
                    act.wait_ge(o_done, 2 * h)
                    act.activation((qT, kT)[z][b][:, half_of(half)], back_ps[:, :], ACT.Identity,
                                   bias=norm[:, 2 * z + 1:2 * z + 2], scale=norm[:, 2 * z:2 * z + 1]).then_inc(hat_done, 1)

                def step(h, b, turn, more):
                    nh, nb = h + 1, 1 - b
                    for n in range(4):
                        take(nh, nb, n)
                    silu(nh, 0)
                    silu(nh, 1)
                    take(nh, nb, 4)
                    silu(nh, 2)
                    silu(nh, 3)
                    take(nh, nb, 5)
                    normalise(nh, 0)
                    normalise(nh, 1)
                    hat(nh, nb, 0)
                    hat(nh, nb, 1)
                    normalise(nh, 2)
                    normalise(nh, 3)
                    hat(nh, nb, 2)
                    hat(nh, nb, 3)
                    if more:
                        act.wait_ge(proj_done, PIECES * (h + 1))
                        split(h + 2, b, turn + 1)

                act.preload_act_table(ACT.Silu)
                act.wait_ge(consts_in, 48)
                split(0, 0, 0)
                split(1, 1, 0)
                for n in range(PIECES):
                    if n < 4:
                        act.wait_ge(padded, 1)
                    kind, half = n // 2, n % 2
                    if kind < 2:
                        take(0, 0, n)
                    else:
                        act.wait_ge(proj_done, n + 1)
                        act.activation(gate[0][:, half_of(half)], proj_ps[:, n % 2, :], ACT.Silu).then_inc(out_done, 1)
                for p in range(4):
                    silu(0, p)
                for p in range(4):
                    normalise(0, p)
                    z, half = p // 2, p % 2
                    act.wait_ge(back_done, p + 1 + C_BACK)
                    act.activation((qT, kT)[z][0][:, half_of(half)], back_ps[:, :], ACT.Identity,
                                   bias=norm[:, 2 * z + 1:2 * z + 2], scale=norm[:, 2 * z:2 * z + 1]).then_inc(hat_done, 1)
                with act.Fori(0, HB // 2 - 1) as i:
                    step(2 * i, 0, i, True)
                    step(2 * i + 1, 1, i, True)
                step(HB - 2, 0, HB // 2 - 1, False)

            @block.vector
            def _(dve):
                dve.sem_inc(tap_done, C_TAP)
                dve.sem_inc(probs_done, C_PROBS)
                dve.sem_inc(state_done, C_STATE)
                dve.sem_inc(og_done, C_OG)
                dve.memset(pre[:, :, 0:PAD], 0.0).then_inc(padded, 1)

                def split(h, b):
                    dve.wait_ge(w_hi_done, h + 1)
                    dve.tensor_tensor(w_lo[b][:, :, :, :], raw[b][:, :, :, :], w_hi[b][:, :, :, :].bitcast(F32),
                                      ALU.subtract).then_inc(w_lo_done, 1)

                def convolve(h, b, z):
                    for tap in range(TAPS - 1):
                        for half in range(2):
                            if tap == 0:
                                dve.wait_ge(out_done, PIECES * h + 2 * z + half + 1 + C_OUT)
                            else:
                                dve.wait_ge(tap_done, 12 * h + 6 * z + 2 * tap + half - 1 + C_TAP)
                            lag = half * HALF + tap
                            dve.scalar_tensor_tensor(y[:, z, half_of(half)], pre[:, z, lag:lag + HALF],
                                                     conv[b][:, z, tap:tap + 1], y[:, z, half_of(half)],
                                                     ALU.mult, ALU.add).then_inc(tap_done, 1)

                def moments(h, p):
                    dve.wait_ge(tok_done, 4 * h + p + 1 + C_TOK)
                    for c in range(BLK):
                        dve.bn_stats(stats[:, c, :], tok_ps[:, p % 2, chunk(c)]).then_inc(stats_done, 1)
                    dve.wait_ge(stats_done, 16 * h + 4 * p + 4)
                    dve.sem_inc(aggr_begun, 1)
                    for c in range(BLK):
                        dve.bn_aggr(mv[:, c, :], stats[:, c, :]).then_inc(aggr_done, 1)
                    dve.wait_ge(aggr_done, 16 * h + 4 * p + 4)
                    dve.tensor_scalar(ve[:, p % 2, :], mv[:, :, 1], EPS, None, ALU.add).then_inc(ve_done, 1)

                def bias(h, p):
                    dve.wait_ge(rstd_done, 4 * h + p + 1)
                    dve.wait_ge(yn_done, 4 * h + p + 1)
                    dve.scalar_tensor_tensor(nbias[:, p % 2, :], mv[:, :, 0], -1.0, rstd[:, p % 2, :],
                                             ALU.mult, ALU.mult).then_inc(nbias_done, 1)

                def decays(h):
                    dve.wait_ge(keep_in, 16 * (h + 1))
                    dve.wait_ge(vd_done, 2 * h + C_VD)
                    for c in range(NT):
                        dve.tensor_tensor_scan(decay[:, chunk(c)], keep[:, chunk(c)], m.ident[:, :], 0.0,
                                               ALU.mult, ALU.add).then_inc(decay_done, 1)

                def weigh(h, half):
                    dve.wait_ge(sc_done, 2 * h + half + 1)
                    dve.wait_ge(decay_done, NT * h + BLK * (half + 1))
                    dve.wait_ge(o_done, 2 * h + half - 1 + C_O)
                    dve.tensor_tensor(probs[:, half_of(half)], sc_ps[:, :], decay[:, half_of(half)],
                                      ALU.mult).then_inc(probs_done, 1)

                def states(h, b, turn, half):
                    dve.wait_ge(ds_done, 2 * h + half + 1 + C_DS)
                    if half == 0:
                        dve.wait_ge(v_in[b], 32 * (turn + 1))
                        dve.wait_ge(o_done, 2 * h + C_O)
                    for c in range(BLK):
                        n = half * BLK + c
                        if n == 0:
                            dve.tensor_copy(state[:, 1, :], ds_ps[:, chunk(0)]).then_inc(state_done, 1)
                        elif n < NT - 1:
                            dve.wait_ge(state_done, 7 * h + n + C_STATE)
                            dve.scalar_tensor_tensor(state[:, n + 1, :], state[:, n, :],
                                                     prod[b][:, n * P + P - 1:n * P + P], ds_ps[:, chunk(c)],
                                                     ALU.mult, ALU.add).then_inc(state_done, 1)

                def gated(h, b, half):
                    dve.wait_ge(o_done, 2 * h + half + 1 + C_O)
                    dve.wait_ge(out_done, PIECES * (h + 1) + C_OUT)
                    dve.tensor_tensor(v_all[:, ds(h, 1), half_of(half)].rearrange("p a s -> p (a s)"), o_ps[:, :],
                                      gate[b][:, half_of(half)], ALU.mult).then_inc(og_done, 1)

                def step(h, b, turn, more):
                    nh, nb = h + 1, 1 - b
                    decays(h)
                    weigh(h, 0)
                    convolve(nh, nb, 0)
                    states(h, b, turn, 0)
                    weigh(h, 1)
                    convolve(nh, nb, 1)
                    moments(nh, 0)
                    states(h, b, turn, 1)
                    bias(nh, 0)
                    moments(nh, 1)
                    gated(h, b, 0)
                    bias(nh, 1)
                    moments(nh, 2)
                    gated(h, b, 1)
                    bias(nh, 2)
                    moments(nh, 3)
                    bias(nh, 3)
                    if more:
                        split(h + 2, b)

                split(0, 0)
                split(1, 1)
                convolve(0, 0, 0)
                convolve(0, 0, 1)
                for p in range(4):
                    moments(0, p)
                    bias(0, p)
                with dve.Fori(0, HB // 2 - 1) as i:
                    step(2 * i, 0, i, True)
                    step(2 * i + 1, 1, i, True)
                step(HB - 2, 0, HB // 2 - 1, False)
                h, b = HB - 1, 1
                decays(h)
                for half in range(2):
                    weigh(h, half)
                    states(h, b, HB // 2 - 1, half)
                for half in range(2):
                    gated(h, b, half)

            @block.gpsimd
            def _(pool):
                pool.sem_inc(ktok_done, C_KTOK)
                pool.sem_inc(vd_done, C_VD)

                def decayed_values(h, b, turn, half):
                    if half == 0:
                        pool.wait_ge(v_in[b], 32 * (turn + 1))
                    pool.wait_ge(decay_done, NT * h + BLK * (half + 1))
                    pool.wait_ge(ds_done, 2 * h + half - 1 + C_DS)
                    at = slice(half * BLK, (half + 1) * BLK)
                    to_end = decay[:, :].rearrange("p (c t) -> p c t", t=P)[:, at, P - 1:P].to_broadcast([P, BLK, DV])
                    pool.tensor_tensor(vd[:, at, :], v[b][:, at, :], to_end, ALU.mult).then_inc(vd_done, 1)

                def decayed_queries(h, b, half):
                    pool.wait_ge(hat_done, 4 * h + 4 + C_HAT)
                    pool.wait_ge(o_done, 2 * h + half - 1 + C_O)
                    pool.tensor_tensor(qg[:, half_of(half)], qT[b][:, half_of(half)], prod[b][:, half_of(half)],
                                       ALU.mult).then_inc(qg_done, 1)

                def rstds(h, p):
                    pool.wait_ge(ve_done, 4 * h + p + 1)
                    pool.wait_ge(yn_done, 4 * h + p + 1)
                    pool.tensor_tensor(rstd[:, p % 2, :], ve[:, p % 2, :], m.neghalf[:, 0:4], ALU.pow).then_inc(rstd_done, 1)

                def key_tokens(h, b, half):
                    pool.wait_ge(yn_done, 4 * h + 2 + half + 1 + C_YN)
                    at = ktok[b][:, half * BLK:(half + 1) * BLK, :]
                    pool.tensor_tensor(at, yn[:, half, :, :], kn_rows[:, 0, :].unsqueeze(1).to_broadcast([P, BLK, DK]),
                                       ALU.mult).then_inc(kw_done, 1)
                    pool.wait_ge(kw_done, 2 * h + half + 1)
                    pool.tensor_tensor(at, at, kn_rows[:, 1, :].unsqueeze(1).to_broadcast([P, BLK, DK]),
                                       ALU.add).then_inc(ktok_done, 1)

                def step(h, b, turn):
                    nh, nb = h + 1, 1 - b
                    decayed_values(h, b, turn, 0)
                    decayed_values(h, b, turn, 1)
                    decayed_queries(h, b, 0)
                    rstds(nh, 0)
                    decayed_queries(h, b, 1)
                    rstds(nh, 1)
                    rstds(nh, 2)
                    pool.wait_ge(o_done, 2 * nh)
                    key_tokens(nh, nb, 0)
                    rstds(nh, 3)
                    key_tokens(nh, nb, 1)

                pool.wait_ge(consts_in, 48)
                for p in range(4):
                    rstds(0, p)
                    if p >= 2:
                        key_tokens(0, 0, p - 2)
                with pool.Fori(0, HB // 2 - 1) as i:
                    step(2 * i, 0, i)
                    step(2 * i + 1, 1, i)
                step(HB - 2, 0, HB // 2 - 1)
                h, b = HB - 1, 1
                for half in range(2):
                    decayed_values(h, b, HB // 2 - 1, half)
                    decayed_queries(h, b, half)


def linear_stage(m, a):
    with ExitStack() as ctx:
        v_all = m.sb("li_v_all", [P, HB, S], F32, ctx)
        rows_dram = m.rows_dram
        value_stage(m, a, v_all, rows_dram)
        head_stage(m, a, v_all, rows_dram)
        w_hi = m.sb("li_wo_hi", [P, HB, D], F32R, ctx)
        w_lo = m.sb("li_wo_lo", [P, HB, D], F32R, ctx)
        output_stage(m, "lo", v_all, w_hi, w_lo, HB, a["b_Wo"].rearrange("(h p) n -> p h n", p=DV))


def build(nc, a, out, stages=None):
    with ExitStack() as ctx:
        m = Memory(nc, ctx)
        m.wT_dram = {tag: nc.dram_tensor(f"{tag}_wT_dram", (E, S), F32, kind="Internal").ap() for tag in ("moe1", "moe2")}
        m.rows_dram = nc.dram_tensor("linear_rows_dram", (2, HB, S), F32, kind="Internal").ap()
        stages = stages or ["attn", "moe1", "linear", "moe2"]
        load_stage(m, a)
        for stage in stages:
            norm_stage(m, stage)
            if stage == "attn":
                attn_stage(m, a)
            elif stage == "linear":
                linear_stage(m, a)
            else:
                moe_stage(m, a, stage)
            m.recycle()
        stored = m.sem("stored")
        with nc.Block() as block:

            @block.sync
            def _(sp):
                sp.dma_start(out.rearrange("b (t p) d -> p (b t) d", p=P), m.x[:, :, :]).then_inc(stored, 16)
                sp.wait_ge(stored, 16)


def constants():
    pos = np.arange(S, dtype=np.float32)
    inv = (np.float32(1.0) / np.float32(10000.0) ** (np.arange(ROPE // 2, dtype=np.float32) * np.float32(2.0 / ROPE)))
    angle = (pos[:, None] * inv.astype(np.float32)[None, :]).astype(np.float32)
    cos, sin = np.cos(angle), np.sin(angle)
    q, k = np.arange(P)[:, None], np.arange(P)[None, :]
    return {
        "ident": np.eye(P, dtype=np.float32),
        "rope_cos": np.repeat(cos, 2, axis=1).astype(np.float32),
        "rope_sin": np.stack([-sin, sin], axis=2).reshape(S, ROPE).astype(np.float32),
        "mask_qk": np.where(k > q, NEG, 0.0).astype(np.float32),
        "mask_kq": np.where(k > q, NEG, 0.0).astype(np.float32).T,
    }


def kernel(**inputs):
    import concourse.bacc as bacc
    from concourse.bass_utils import run_bass_kernel_spmd

    nc = bacc.Bacc("TRN2", target_bir_lowering=False, num_devices=1)
    arrays, a = {}, {}
    names = {"L0_attn_a_hidden_states": "x", "L0_ffn_router_w": "router_w", "L0_ffn_w_gate": "w_gate",
             "L0_ffn_w_up": "w_up", "L0_ffn_w_down": "w_down"}
    data = {names.get(k, k.removeprefix("L0_attn_")): v for k, v in inputs.items()}
    data["conv"] = np.concatenate([np.concatenate([np.asarray(data[f"b_{z}conv_w"]).reshape(HB, DK, TAPS),
                                                   np.asarray(data[f"b_{z}conv_b"]).reshape(HB, DK, 1)], 2)
                                   for z in "qk"], 2)
    data["norm"] = np.stack([np.asarray(data[f"b_{z}n_{p}"]) for z in "qk" for p in "wb"], 1)
    for name in ("qconv_w", "qconv_b", "kconv_w", "kconv_b", "qn_w", "qn_b"):
        del data[f"b_{name}"]
    for name, v in {**data, **constants()}.items():
        v = np.ascontiguousarray(v)
        arrays[f"in_{name}_dram"] = v
        a[name] = nc.dram_tensor(f"in_{name}_dram", v.shape, mybir.dt.from_np(v.dtype), kind="ExternalInput").ap()
    out = nc.dram_tensor("out_dram", (1, S, D), F32, kind="ExternalOutput").ap()
    build(nc, a, out)
    return run_bass_kernel_spmd(nc, [arrays], core_ids=[0]).results[0]["out_dram"]
```

```python
from contextlib import ExitStack

import numpy as np

import concourse.bass as bass
from concourse import mybir

F32 = mybir.dt.float32
F32R = mybir.dt.float32r
BF16 = mybir.dt.bfloat16
ALU = mybir.AluOpType
ACT = mybir.ActivationFunctionType
AX_X = mybir.AxisListType.X
ds = bass.ds

P = 128
S, D = 1024, 256
NT = S // P
KD = D // P
HALF = 512
EPS = 1e-5

HA, QLORA, KVLORA, ROPE, NOPE, VDIM = 16, 192, 64, 64, 64, 128
QCH = QLORA // 2
QSCALE = float(NOPE + ROPE) ** -0.5
HG = 4
NEG = -1.0e37

E, TOPK, INNER = 32, 8, 96
GE = 4
GC = GE * INNER // P
NG = E // GE

HB, DK, DV, TAPS = 16, 128, 128, 4


def mm3(pe, out, lhs, rhs, start, stop):
    pe.matmul(out, lhs[0], rhs[0], start=start, stop=False)
    pe.matmul(out, lhs[0], rhs[1], start=False, stop=False)
    return pe.matmul(out, lhs[1], rhs[0], start=False, stop=stop)


class Memory:

    def __init__(self, nc, ctx):
        self.nc, self.ctx, self.sems = nc, ctx, []

    def sb(self, name, shape, dt=F32, ctx=None):
        return (ctx or self.ctx).enter_context(self.nc.sbuf_tensor(name, shape, dt))

    def ps(self, name, shape, dt=F32, ctx=None):
        return (ctx or self.ctx).enter_context(self.nc.psum_tensor(name, shape, dt))

    def sem(self, name):
        self.sems.append(self.nc.alloc_semaphore(name))
        return self.sems[-1]

    def recycle(self):
        self.nc.clear_and_free_semaphores(self.sems)
        self.nc.all_engine_barrier()
        self.sems = []


def load_stage(m, a):
    nc = m.nc
    m.x = m.sb("x", [P, NT, D])
    m.h_hi = m.sb("h_hi", [P, KD, S], F32R)
    m.h_lo = m.sb("h_lo", [P, KD, S], F32R)
    m.ident = m.sb("ident", [P, P])
    m.identb = m.sb("identb", [P, P], BF16)
    m.neghalf = m.sb("neghalf", [P, 2 * NT])
    loaded = m.sem("load_x")
    made = m.sem("load_made")
    with nc.Block() as block:

        @block.sync
        def _(sp):
            sp.dma_start(m.ident[:, :], a["ident"]).then_inc(loaded, 16)
            sp.dma_start(m.x[:, :, :], a["x"].rearrange("b (t p) d -> p (b t) d", p=P)).then_inc(loaded, 16)
            sp.wait_ge(loaded, 32)

        @block.vector
        def _(dve):
            dve.memset(m.neghalf[:, :], -0.5)
            dve.wait_ge(loaded, 32)
            dve.tensor_copy(m.identb[:, :], m.ident[:, :]).then_inc(made, 1)
            dve.wait_ge(made, 1)


def norm_stage(m, tag, prefetch):
    nc = m.nc
    with ExitStack() as ctx:
        stats = m.sb(f"{tag}_stats", [P, NT, 6], F32, ctx)
        mv = m.sb(f"{tag}_mv", [P, NT, 2], F32, ctx)
        ve = m.sb(f"{tag}_ve", [P, NT], F32, ctx)
        rstd = m.sb(f"{tag}_rstd", [P, NT], F32, ctx)
        hn = m.sb(f"{tag}_hn", [P, NT, D], F32, ctx)
        hT = m.ps(f"{tag}_hT", [P, KD, S], F32, ctx)
        stats_done = m.sem(f"{tag}_stats_done")
        aggr_done = m.sem(f"{tag}_aggr_done")
        var_done = m.sem(f"{tag}_var_done")
        rstd_done = m.sem(f"{tag}_rstd_done")
        hn_done = m.sem(f"{tag}_hn_done")
        hT_done = m.sem(f"{tag}_hT_done")
        hi_done = m.sem(f"{tag}_hi_done")
        NH = NT // 2
        pieces = [(half, k) for half in range(2) for k in range(KD)]
        with nc.Block() as block:

            @block.sync
            def _(sp):
                prefetch(sp)

            @block.vector
            def _(dve):
                def moments(half):
                    for t in range(half * NH, (half + 1) * NH):
                        dve.bn_stats(stats[:, t, :], m.x[:, t, :]).then_inc(stats_done, 1)
                    for t in range(half * NH, (half + 1) * NH):
                        dve.wait_ge(stats_done, t + 1)
                        dve.bn_aggr(mv[:, t, :], stats[:, t, :]).then_inc(aggr_done, 1)
                    dve.wait_ge(aggr_done, (half + 1) * NH)
                    tiles = slice(half * NH, (half + 1) * NH)
                    dve.tensor_scalar(ve[:, tiles], mv[:, tiles, 1], EPS, None, ALU.add).then_inc(var_done, 1)

                def normalise(half):
                    dve.wait_ge(rstd_done, half + 1)
                    for t in range(half * NH, (half + 1) * NH):
                        dve.tensor_scalar(hn[:, t, :], m.x[:, t, :], mv[:, t, 0:1], rstd[:, t:t + 1],
                                          ALU.subtract, ALU.mult).then_inc(hn_done, 1)

                moments(0)
                moments(1)
                normalise(0)
                normalise(1)
                for n, (half, k) in enumerate(pieces):
                    at = slice(half * HALF, (half + 1) * HALF)
                    dve.wait_ge(hi_done, n + 1)
                    dve.tensor_tensor(m.h_lo[:, k, at], hT[:, k, at], m.h_hi[:, k, at].bitcast(F32), ALU.subtract)

            @block.gpsimd
            def _(pool):
                for half in range(2):
                    tiles = slice(half * NH, (half + 1) * NH)
                    pool.wait_ge(var_done, half + 1)
                    pool.tensor_tensor(rstd[:, tiles], ve[:, tiles], m.neghalf[:, tiles], ALU.pow).then_inc(rstd_done, 1)

            @block.tensor
            def _(pe):
                for t in range(NT):
                    pe.wait_ge(hn_done, t + 1)
                    for k in range(KD):
                        pe.transpose(hT[:, k, t * P:(t + 1) * P], hn[:, t, k * P:(k + 1) * P],
                                     m.ident[:, :]).then_inc(hT_done, 1)

            @block.scalar
            def _(act):
                for half, k in pieces:
                    at = slice(half * HALF, (half + 1) * HALF)
                    act.wait_ge(hT_done, (half + 1) * (NT // 2) * KD - (KD - 1 - k))
                    act.activation(m.h_hi[:, k, at], hT[:, k, at], ACT.Copy).then_inc(hi_done, 1)


def moe_stage(m, a, tag):
    nc = m.nc
    with ExitStack() as ctx:
        def sb(name, shape, dt=F32):
            return m.sb(f"{tag}_{name}", shape, dt, ctx)

        def sem(name):
            return m.sem(f"{tag}_{name}")

        rw = sb("rw", [P, D])
        rwT_hi = sb("rwT_hi", [P, KD, P], F32R)
        rwT_lo = sb("rwT_lo", [P, KD, P], F32R)
        lgT = sb("lgT", [E, S])
        owner = sb("owner", [GE, P])
        top = sb("top", [P, NT, TOPK])
        stat = sb("stat", [P, 4, NT])
        lg = sb("lg", [P, NT, E])
        pr = sb("pr", [P, NT, E])
        rest = sb("rest", [P, NT, E])
        wT = sb("wT", [E, S])
        wT_dram = m.wT_dram[tag]
        raw = [sb(f"raw{b}", [P, 3, GC * D]) for b in range(2)]
        w_hi = [sb(f"w_hi{b}", [P, 3, GC * D], F32R) for b in range(2)]
        w_lo = [sb(f"w_lo{b}", [P, 3, GC * D], F32R) for b in range(2)]
        wb = [sb(f"wb{b}", [P, GC, S]) for b in range(2)]
        s = sb("s", [P, 2, HALF])
        sw = sb("sw", [P, 2, HALF])
        act_f = sb("act_f", [P, 2, HALF])
        act_hi = sb("act_hi", [P, 2, HALF], F32R)
        act_lo = sb("act_lo", [P, 2, HALF], F32R)
        yT = sb("yT", [P, KD, S])
        zero_r = sb("zero_r", [P, HALF], F32R)

        rw_in, owner_in = sem("rw_in"), sem("owner_in")
        raw_in = [sem(f"raw_in{b}") for b in range(2)]
        gate_r = a["w_gate"].rearrange("e (k p) i -> k p e i", p=P)
        up_r = a["w_up"].rearrange("e (k p) i -> k p e i", p=P)
        down_r = a["w_down"].rearrange("e i d -> (e i) d").rearrange("(c p) d -> p c d", p=P)

        def load_weights(sp, g, b):
            for k in range(KD):
                for kind, src in ((0, gate_r), (1, up_r)):
                    dst = raw[b][:, kind, k * GE * INNER:(k + 1) * GE * INNER]
                    sp.dma_start(dst.rearrange("p (e i) -> p e i", i=INNER),
                                 src[k, :, ds(g * GE, GE), :]).then_inc(raw_in[b], 16)
            sp.dma_start(raw[b][:, 2, :].rearrange("p (c d) -> p c d", d=D),
                         down_r[:, ds(g * GC, GC), :]).then_inc(raw_in[b], 16)

        def first_loads(sp):
            sp.dma_start(rw[0:E, :], a["router_w"]).then_inc(rw_in, 16)
            sp.dma_start(owner[:, :], a["owner"]).then_inc(owner_in, 16)
            load_weights(sp, 0, 0)
            load_weights(sp, 1, 1)

        norm_stage(m, f"{tag}_norm", first_loads)

        acc = m.ps(f"{tag}_acc", [P, KD, S], F32, ctx)
        gu = m.ps(f"{tag}_gu", [P, 2, 2, HALF], F32, ctx)
        lgT_ps = acc[:, 0, :]
        wT_ps = acc[0:E, 0, :]
        lg_ps = acc[:, 1, 0:NT * E].rearrange("p (t e) -> p t e", e=E)
        rwT_ps = acc[:, 1, HALF:HALF + KD * P].rearrange("p (k e) -> p k e", e=P)
        y_ps = gu[:, :, :, :].rearrange("p a b c -> p (a b c)").rearrange("p (t d) -> p t d", d=D)

        rwT_done, rwT_hi_done, rwT_lo_done = sem("rwT_done"), sem("rwT_hi_done"), sem("rwT_lo_done")
        padded, lgT_done, lgT_sb_done = sem("padded"), sem("lgT_done"), sem("lgT_sb_done")
        lg_done, soft, exp_done, wT_done, wT_sb_done, wT_stored = (
            sem("lg_done"), sem("soft"), sem("exp_done"), sem("wT_done"), sem("wT_sb_done"), sem("wT_stored"))
        wb_in = [[sem(f"wb_in{b}_{c}") for c in range(GC)] for b in range(2)]
        spread = sem("spread")
        hi_split, lo_split = sem("hi_split"), sem("lo_split")
        picked, replaced = sem("picked"), sem("replaced")
        s_done, sw_done, gu_done = sem("s_done"), sem("sw_done"), sem("gu_done")
        act_done, act_hi_done, act_lo_done, down_done = sem("act_done"), sem("act_hi_done"), sem("act_lo_done"), sem("down_done")
        zeroed = sem("zeroed")
        y_done, yT_done, yt_done = sem("y_done"), sem("yT_done"), sem("yt_done")

        UNITS = 2 * GC

        def weight(parts, b, kind, k, c):
            base = k * GE * INNER + c * P
            return [part[b][:, kind, base:base + P] for part in parts]

        with nc.Block() as block:

            @block.sync
            def _(sp):
                def load_routing(g, b, first_chunk=0):
                    for c in range(first_chunk, GC):
                        for e in range(GE):
                            lo, hi = max(e * INNER, c * P), min((e + 1) * INNER, (c + 1) * P)
                            if lo < hi:
                                sp.dma_start(wb[b][lo - c * P:hi - c * P, c, :],
                                             wT_dram[ds(g * GE + e, 1), :].partition_broadcast(hi - lo)
                                             .rearrange("p a s -> p (a s)")).then_inc(wb_in[b][c], 16)

                sp.wait_ge(wT_sb_done, 2)
                sp.dma_start(wT_dram, wT[:, :]).then_inc(wT_stored, 16)
                sp.wait_ge(wT_stored, 16)
                load_routing(0, 0, 1)
                load_routing(1, 1)

                def step(i):
                    for b in range(2):
                        g = 2 * i + b
                        sp.wait_ge(lo_split, g + 3)
                        sp.wait_ge(hi_split, g + 3)
                        load_weights(sp, g + 2, b)
                        sp.wait_ge(sw_done, UNITS * (g + 1) + 2)
                        load_routing(g + 2, b)

                with sp.Fori(0, NG // 2 - 1) as i:
                    step(i)

            @block.tensor
            def _(pe):
                pe.wait_ge(rw_in, 16)
                pe.wait_ge(padded, 2)
                for k in range(KD):
                    pe.transpose(rwT_ps[:, k, :], rw[:, k * P:(k + 1) * P], m.ident[:, :]).then_inc(rwT_done, 1)
                pe.wait_ge(rwT_lo_done, 1)
                for half in range(2):
                    for k in range(KD):
                        tok = slice(half * HALF, (half + 1) * HALF)
                        last = mm3(pe, lgT_ps[:, tok], (rwT_hi[:, k, :], rwT_lo[:, k, :]),
                                   (m.h_hi[:, k, tok], m.h_lo[:, k, tok]), k == 0, k == KD - 1)
                    last.then_inc(lgT_done, 1)
                for t in range(NT):
                    if t % (NT // 2) == 0:
                        pe.wait_ge(lgT_sb_done, t // (NT // 2) + 1)
                    last = pe.transpose(lg_ps[:, t, :], lgT[:, t * P:(t + 1) * P], m.ident[0:E, 0:E])
                last.then_inc(lg_done, 1)

                def finish_routing():
                    pe.wait_ge(soft, 7)
                    for t in range(NT):
                        pe.transpose(wT_ps[:, t * P:(t + 1) * P], rest[:, t, :], m.ident[:, :]).then_inc(wT_done, 1)
                    pe.wait_ge(owner_in, 16)
                    pe.wait_ge(wT_sb_done, 2)
                    for half in range(2):
                        at = slice(half * HALF, (half + 1) * HALF)
                        pe.matmul(acc[:, 0, at], owner[:, :], wT[0:GE, at], start=True, stop=True).then_inc(spread, 1)
                    pe.wait_ge(zeroed, 1)
                    pe.wait_ge(wb_in[0][0], 32)
                    for k in range(KD):
                        for half in range(2):
                            pe.matmul(acc[:, k, half * HALF:(half + 1) * HALF], zero_r[:, 0:P], zero_r[:, :],
                                      start=True, stop=False)

                def gate_up(i, b, u):
                    n = (2 * i + b) * UNITS + u
                    c, half = u // 2, u % 2
                    if u == 0:
                        pe.wait_ge(hi_split, 2 * i + b + 3)
                        pe.wait_ge(lo_split, 2 * i + b + 3)
                    pe.wait_ge(act_done, n + 1)
                    tok = slice(half * HALF, (half + 1) * HALF)
                    for kind in range(2):
                        for k in range(KD):
                            last = mm3(pe, gu[:, half, kind, :], weight((w_hi, w_lo), b, kind, k, c),
                                       (m.h_hi[:, k, tok], m.h_lo[:, k, tok]), k == 0, k == KD - 1)
                        last.then_inc(gu_done, 1)

                def down(i, b, u):
                    n = (2 * i + b) * UNITS + u
                    c, half = u // 2, u % 2
                    pe.wait_ge(act_lo_done, n + 3)
                    for k in range(KD):
                        base = c * D + k * P
                        last = mm3(pe, acc[:, k, half * HALF:(half + 1) * HALF],
                                   [part[b][:, 2, base:base + P] for part in (w_hi, w_lo)],
                                   (act_hi[:, half, :], act_lo[:, half, :]), False, False)
                    last.then_inc(down_done, 1)

                def step(i, first=False):
                    for b in range(2):
                        for u in range(UNITS):
                            if first and b == 0 and u == LAG:
                                finish_routing()
                            gate_up(i, b, u)
                            if u >= LAG:
                                down(i, b, u - LAG)
                            elif b == 1:
                                down(i, 0, UNITS + u - LAG)
                            elif not first:
                                down(i - 1, 1, UNITS + u - LAG)

                LAG = 2
                step(0, first=True)
                with pe.Fori(1, NG // 2) as i:
                    step(i)
                for u in range(UNITS - LAG, UNITS):
                    down(NG // 2 - 1, 1, u)
                for k in range(KD):
                    for half in range(2):
                        pe.matmul(acc[:, k, half * HALF:(half + 1) * HALF], zero_r[:, 0:P], zero_r[:, :],
                                  start=False, stop=True).then_inc(y_done, 1)
                for t in range(NT):
                    pe.wait_ge(yT_done, (t // (NT // 2) + 1) * KD)
                    for k in range(KD):
                        pe.transpose(y_ps[:, t, k * P:(k + 1) * P], yT[:, k, t * P:(t + 1) * P],
                                     m.ident[:, :]).then_inc(yt_done, 1)

            @block.scalar
            def _(act):
                act.wait_ge(rwT_done, KD)
                act.activation(rwT_hi[:, :, :], rwT_ps, ACT.Copy).then_inc(rwT_hi_done, 1)

                def split(i, b):
                    act.wait_ge(raw_in[b], 16 * 5 * (i + 1))
                    act.activation(w_hi[b][:, :, :], raw[b][:, :, :], ACT.Copy).then_inc(hi_split, 1)

                act.sem_inc(hi_split, 2)
                act.sem_inc(s_done, 2)
                act.sem_inc(act_hi_done, 2)
                split(0, 0)
                for half in range(2):
                    tok = slice(half * HALF, (half + 1) * HALF)
                    act.wait_ge(lgT_done, half + 1)
                    act.activation(lgT[:, tok], lgT_ps[0:E, tok], ACT.Copy).then_inc(lgT_sb_done, 1)
                act.wait_ge(soft, 2)
                act.activation(pr[:, :, :], lg[:, :, :], ACT.Exp).then_inc(exp_done, 1)
                act.preload_act_table(ACT.Silu)
                for half in range(2):
                    act.wait_ge(wT_done, NT // 2 * (half + 1))
                    act.activation(wT[:, half * HALF:(half + 1) * HALF], wT_ps[:, half * HALF:(half + 1) * HALF],
                                   ACT.Copy).then_inc(wT_sb_done, 1)

                def silu(i, b, u):
                    n = (2 * i + b) * UNITS + u
                    act.wait_ge(gu_done, 2 * n + 1)
                    act.wait_ge(sw_done, n + 1)
                    act.activation(s[:, u % 2, :], gu[:, u % 2, 0, :], ACT.Silu).then_inc(s_done, 1)

                def hi(i, b, u):
                    n = (2 * i + b) * UNITS + u
                    act.wait_ge(act_done, n + 3)
                    act.wait_ge(down_done, n + 1)
                    act.activation(act_hi[:, u % 2, :], act_f[:, u % 2, :], ACT.Copy).then_inc(act_hi_done, 1)

                def step(i, last=False):
                    for b in range(2):
                        for u in range(UNITS):
                            silu(i, b, u)
                            hi(i, b, u)
                            if u == 2 and not (last and b == 1):
                                act.wait_ge(down_done, UNITS * (2 * i + b) + 2)
                                split(*((i, 1) if b == 0 else (i + 1, 0)))

                with act.Fori(0, NG // 2 - 1) as i:
                    step(i)
                step(NG // 2 - 1, last=True)
                for half in range(2):
                    for k in range(KD):
                        act.wait_ge(y_done, 2 * KD)
                        at = slice(half * HALF, (half + 1) * HALF)
                        act.activation(yT[:, k, at], acc[:, k, at], ACT.Copy).then_inc(yT_done, 1)

            @block.vector
            def _(dve):
                dve.memset(zero_r[:, :].bitcast(F32), 0.0).then_inc(zeroed, 1)
                dve.wait_ge(rwT_hi_done, 1)
                dve.tensor_tensor(rwT_lo[:, :, :], rwT_ps, rwT_hi[:, :, :].bitcast(F32),
                                  ALU.subtract).then_inc(rwT_lo_done, 1)

                def split(i, b):
                    dve.wait_ge(hi_split, 2 * i + b + 3)
                    dve.tensor_tensor(w_lo[b][:, :, :], raw[b][:, :, :], w_hi[b][:, :, :].bitcast(F32),
                                      ALU.subtract).then_inc(lo_split, 1)

                dve.sem_inc(lo_split, 2)
                dve.sem_inc(act_done, 2)
                dve.sem_inc(act_lo_done, 2)
                split(0, 0)
                dve.wait_ge(lg_done, 1)
                dve.tensor_reduce(stat[:, 0, :], lg_ps, AX_X, ALU.max).then_inc(soft, 1)
                dve.wait_ge(soft, 1)
                dve.tensor_tensor(lg[:, :, :], lg_ps, stat[:, 0, :].unsqueeze(2).to_broadcast([P, NT, E]),
                                  ALU.subtract).then_inc(soft, 1)
                dve.wait_ge(exp_done, 1)
                dve.tensor_reduce(stat[:, 1, :], pr[:, :, :], AX_X, ALU.add).then_inc(soft, 1)
                dve.wait_ge(soft, 3)
                dve.reciprocal(stat[:, 2, :], stat[:, 1, :]).then_inc(soft, 1)
                dve.wait_ge(soft, 4)
                dve.tensor_tensor(pr[:, :, :], pr[:, :, :], stat[:, 2, :].unsqueeze(2).to_broadcast([P, NT, E]),
                                  ALU.mult).then_inc(soft, 1)
                dve.wait_ge(soft, 5)
                for t in range(NT):
                    dve.max(top[:, t, :], pr[:, t, :]).then_inc(picked, 1)
                for t in range(NT):
                    dve.wait_ge(picked, t + 1)
                    dve.match_replace(rest[:, t, :], top[:, t, :], pr[:, t, :], 0.0).then_inc(replaced, 1)
                dve.tensor_reduce(stat[:, 3, :], top[:, :, :], AX_X, ALU.add).then_inc(picked, 1)
                dve.wait_ge(picked, NT + 1)
                dve.reciprocal(stat[:, 0, :], stat[:, 3, :]).then_inc(picked, 1)
                dve.wait_ge(replaced, NT)
                dve.tensor_tensor(pr[:, :, :], pr[:, :, :], rest[:, :, :], ALU.subtract).then_inc(soft, 1)
                dve.wait_ge(picked, NT + 2)
                dve.wait_ge(soft, 6)
                dve.tensor_tensor(rest[:, :, :], pr[:, :, :], stat[:, 0, :].unsqueeze(2).to_broadcast([P, NT, E]),
                                  ALU.mult).then_inc(soft, 1)

                for half in range(2):
                    at = slice(half * HALF, (half + 1) * HALF)
                    dve.wait_ge(spread, half + 1)
                    dve.tensor_copy(wb[0][:, 0, at], acc[:, 0, at]).then_inc(wb_in[0][0], 16)

                def product(i, b, u):
                    n = (2 * i + b) * UNITS + u
                    dve.wait_ge(sw_done, n + 3)
                    dve.wait_ge(gu_done, 2 * n + 2)
                    dve.wait_ge(act_lo_done, n + 1)
                    dve.tensor_tensor(act_f[:, u % 2, :], gu[:, u % 2, 1, :], sw[:, u % 2, :],
                                      ALU.mult).then_inc(act_done, 1)

                def lo(i, b, u):
                    n = (2 * i + b) * UNITS + u
                    dve.wait_ge(act_hi_done, n + 3)
                    dve.tensor_tensor(act_lo[:, u % 2, :], act_f[:, u % 2, :], act_hi[:, u % 2, :].bitcast(F32),
                                      ALU.subtract).then_inc(act_lo_done, 1)

                def step(i, last=False):
                    for b in range(2):
                        for u in range(UNITS):
                            product(i, b, u)
                            lo(i, b, u)
                            if u == 2 and not (last and b == 1):
                                split(*((i, 1) if b == 0 else (i + 1, 0)))

                with dve.Fori(0, NG // 2 - 1) as i:
                    step(i)
                step(NG // 2 - 1, last=True)
                for t in range(NT):
                    dve.wait_ge(yt_done, 2 * KD * (t // 2 + 1))
                    dve.tensor_tensor(m.x[:, t, :], m.x[:, t, :], y_ps[:, t, :], ALU.add)

            @block.gpsimd
            def _(pool):
                pool.memset(rw[E:2 * E, :], 0.0).then_inc(padded, 1)
                pool.memset(rw[2 * E:, :], 0.0).then_inc(padded, 1)
                pool.sem_inc(sw_done, 2)
                pool.sem_inc(down_done, 2)

                def step(i):
                    for b in range(2):
                        for u in range(UNITS):
                            n = (2 * i + b) * UNITS + u
                            if u % 2 == 0:
                                pool.wait_ge(wb_in[b][u // 2], 32 * (i + 1))
                            pool.wait_ge(s_done, n + 3)
                            pool.wait_ge(act_done, n + 1)
                            half = slice((u % 2) * HALF, (u % 2 + 1) * HALF)
                            pool.tensor_tensor(sw[:, u % 2, :], s[:, u % 2, :], wb[b][:, u // 2, half],
                                               ALU.mult).then_inc(sw_done, 1)

                with pool.Fori(0, NG // 2) as i:
                    step(i)


def attn_prepare(m, a, w, o):
    nc = m.nc
    with ExitStack() as ctx:
        def sb(name, shape, dt=F32):
            return m.sb(f"ap_{name}", shape, dt, ctx)

        def sem(name):
            return m.sem(f"ap_{name}")

        wqa, wkva = sb("wqa", [P, KD, QLORA]), sb("wkva", [P, KD, KVLORA + ROPE])
        wqa_hi, wqa_lo = sb("wqa_hi", [P, KD, QLORA], F32R), sb("wqa_lo", [P, KD, QLORA], F32R)
        wkva_hi, wkva_lo = sb("wkva_hi", [P, KD, P], F32R), sb("wkva_lo", [P, KD, P], F32R)
        wqb = sb("wqb", [QCH, 2, HA, P])
        wkvb = sb("wkvb", [KVLORA, HA, NOPE + VDIM])
        flat = o[:, :, :].rearrange("p j s -> p (j s)")
        wo = flat[:, 0:HA * D].rearrange("p (h n) -> p h n", h=HA)
        wqbT = flat[0:NOPE, HA * D:].rearrange("p (h n) -> p h n", h=HA)
        wvT = sb("wvT", [VDIM, HA, KVLORA])
        kvT = sb("kvT", [P, S])
        ktok = sb("ktok", [P, NT, P])
        turned = sb("turned", [P, NT, ROPE])
        mask = sb("mask", [P, 2, P])
        w_in = {n: sem(f"{n}_in") for n in ("proj", "rope", "mask", "wqb", "wkvb", "wo")}

        def first_loads(sp):
            sp.dma_start(wqa[:, :, :], a["a_Wqa"].rearrange("(k p) n -> p k n", p=P)).then_inc(w_in["proj"], 16)
            sp.dma_start(wkva[:, :, :], a["a_Wkva"].rearrange("(k p) n -> p k n", p=P)).then_inc(w_in["proj"], 16)
            sp.dma_start(wqb[:, :, :, :], a["a_Wqb"].rearrange("(c p) (h n) -> p c h n", p=QCH, n=P)).then_inc(w_in["wqb"], 16)
            sp.dma_start(wkvb[:, :, :], a["a_Wkvb"].rearrange("p (h n) -> p h n", h=HA)).then_inc(w_in["wkvb"], 16)
            sp.dma_start(w["cos"][:, :, :], a["rope_cos"].rearrange("(t p) c -> p t c", p=P)).then_inc(w_in["rope"], 16)
            sp.dma_start(w["sin"][:, :, :], a["rope_sin"].rearrange("(t p) c -> p t c", p=P)).then_inc(w_in["rope"], 16)
            sp.dma_start(wo[:, :, :], a["a_Wo"].rearrange("(h p) n -> p h n", p=VDIM)).then_inc(w_in["wo"], 16)
            sp.dma_start(mask[:, 0, :], a["mask_qk"]).then_inc(w_in["mask"], 16)
            sp.dma_start(mask[:, 1, :], a["mask_kq"]).then_inc(w_in["mask"], 16)

        norm_stage(m, "attn_norm", first_loads)

        bank = m.ps("ap_bank", [P, 2, 4 * HALF], F32, ctx)

        hi_ready, lo_ready = sem("hi_ready"), sem("lo_ready")
        pe_job, act_job, dve_job = sem("pe_job"), sem("act_job"), sem("dve_job")
        chain = sem("chain")
        KVT, QLAT, T0, KV, T1, KT, FOLD, VT, VO0, VO1 = range(10)
        H2 = HA // 2

        def dve_jobs(job):
            return sum(n <= job for n in (QLAT, KV, KT, FOLD, VO0, VO1))

        def half_of(job):
            return bank[:, job % 2, :]

        def turned_view(job):
            return half_of(job)[0:NOPE].rearrange("p (h c) -> p h c", h=H2)

        with nc.Block() as block:

            @block.tensor
            def _(pe):
                def free(job):
                    if job >= 2:
                        pe.wait_ge(act_job, job - 1)
                        pe.wait_ge(dve_job, dve_jobs(job - 2))

                pe.wait_ge(lo_ready, 1)
                for half in range(2):
                    tok = slice(half * HALF, (half + 1) * HALF)
                    for k in range(KD):
                        last = mm3(pe, half_of(KVT)[:, tok], (wkva_hi[:, k, :], wkva_lo[:, k, :]),
                                   (m.h_hi[:, k, tok], m.h_lo[:, k, tok]), k == 0, k == KD - 1)
                last.then_inc(pe_job, 1)
                pe.wait_ge(lo_ready, 2)
                for c in range(2):
                    for half in range(2):
                        for k in range(KD):
                            tok = slice(half * HALF, (half + 1) * HALF)
                            last = mm3(pe, half_of(QLAT)[0:QCH, (2 * c + half) * HALF:(2 * c + half + 1) * HALF],
                                       [p[:, k, c * QCH:(c + 1) * QCH] for p in (wqa_hi, wqa_lo)],
                                       (m.h_hi[:, k, tok], m.h_lo[:, k, tok]), k == 0, k == KD - 1)
                last.then_inc(pe_job, 1)
                def turn_heads(job, h0):
                    free(job)
                    for h in range(h0, h0 + H2):
                        out = turned_view(job)[:, h - h0, :]
                        for c in range(2):
                            pe.transpose(out[:, c * QCH:(c + 1) * QCH], wqb[:, c, h, 0:NOPE], m.ident[0:QCH, 0:QCH])
                        last = pe.transpose(out[:, QLORA:], wkvb[:, h, 0:NOPE], m.ident[0:KVLORA, 0:KVLORA])
                    last.then_inc(pe_job, 1)

                pe.wait_ge(w_in["wqb"], 16)
                pe.wait_ge(w_in["wkvb"], 16)
                turn_heads(T0, 0)
                free(KV)
                pe.wait_ge(act_job, KVT + 1)
                for t in range(NT):
                    last = pe.transpose(half_of(KV)[:, t * P:(t + 1) * P], kvT[:, t * P:(t + 1) * P], m.ident[:, :])
                last.then_inc(pe_job, 1)
                turn_heads(T1, H2)
                free(KT)
                for t in range(NT):
                    last = pe.transpose(half_of(KT)[:, t * P:(t + 1) * P], ktok[:, t, :], m.ident[:, :])
                last.then_inc(pe_job, 1)
                pe.wait_ge(act_job, T1 + 1)
                free(FOLD)
                for c in range(2):
                    for h in range(HA):
                        last = pe.matmul(half_of(FOLD)[0:QCH, (c * HA + h) * KVLORA:(c * HA + h + 1) * KVLORA],
                                         wqbT[:, h, c * QCH:(c + 1) * QCH], wqbT[:, h, QLORA:], start=True, stop=True)
                last.then_inc(pe_job, 1)
                free(VT)
                for h in range(HA):
                    last = pe.transpose(half_of(VT)[:, h * KVLORA:(h + 1) * KVLORA], wkvb[:, h, NOPE:],
                                        m.ident[0:KVLORA, 0:KVLORA])
                last.then_inc(pe_job, 1)
                pe.wait_ge(w_in["wo"], 16)
                pe.wait_ge(act_job, VT + 1)
                for job in (VO0, VO1):
                    free(job)
                    for n in range(H2):
                        h = (job - VO0) * H2 + n
                        last = pe.matmul(half_of(job)[0:KVLORA, n * D:(n + 1) * D], wvT[:, h, :], wo[:, h, :],
                                         start=True, stop=True)
                    last.then_inc(pe_job, 1)

            @block.scalar
            def _(act):
                act.wait_ge(w_in["proj"], 32)
                act.activation(wkva_hi[:, :, :], wkva[:, :, :], ACT.Copy).then_inc(hi_ready, 1)
                act.activation(wqa_hi[:, :, :], wqa[:, :, :], ACT.Copy).then_inc(hi_ready, 1)
                act.wait_ge(w_in["wqb"], 16)
                act.activation(w["wq_hi"][:, :, :, NOPE:].rearrange("p c h n -> p (c h) n"),
                               wqb[:, :, :, NOPE:].rearrange("p c h n -> p (c h) n"), ACT.Copy).then_inc(hi_ready, 1)

                def begin(job):
                    act.wait_ge(pe_job, job + 1)

                begin(KVT)
                act.activation(kvT[:, :], half_of(KVT)[:, 0:S], ACT.Copy).then_inc(act_job, 1)
                begin(QLAT)
                act.activation(w["qlat_hi"][:, :, :], half_of(QLAT)[0:QCH].rearrange("p (c s) -> p c s", c=2),
                               ACT.Copy).then_inc(act_job, 1)
                begin(T0)
                act.activation(wqbT[:, 0:H2, :], turned_view(T0), ACT.Copy).then_inc(act_job, 1)
                begin(KV)
                kv = half_of(KV)[:, 0:NT * P].rearrange("p (t c) -> p t c", t=NT)
                act.activation(w["v_hi"][:, :, 0:KVLORA], kv[:, :, 0:KVLORA], ACT.Copy)
                act.activation(ktok[:, :, 0:KVLORA], kv[:, :, 0:KVLORA], ACT.Copy).then_inc(act_job, 1)
                begin(T1)
                act.activation(wqbT[:, H2:, :], turned_view(T1), ACT.Copy).then_inc(act_job, 1)
                begin(KT)
                act.activation(w["kT_hi"][:, :], half_of(KT)[:, 0:S], ACT.Copy).then_inc(act_job, 1)
                begin(FOLD)
                act.activation(w["wq_hi"][:, :, :, 0:NOPE].rearrange("p c h n -> p (c h) n"),
                               half_of(FOLD)[0:QCH].rearrange("p (g n) -> p g n", n=KVLORA),
                               ACT.Copy).then_inc(act_job, 1)
                begin(VT)
                act.activation(wvT[:, :, :], half_of(VT)[:, 0:HA * KVLORA].rearrange("p (h n) -> p h n", h=HA),
                               ACT.Copy).then_inc(act_job, 1)
                for job in (VO0, VO1):
                    begin(job)
                    pair = slice((job - VO0) * H2 // 2, (job - VO0 + 1) * H2 // 2)
                    vo = half_of(job)[0:KVLORA].rearrange("p (j o d) -> p j o d", o=2, d=D)
                    for odd in range(2):
                        last = act.activation(w["vo_hi"][odd * KVLORA:(odd + 1) * KVLORA, pair, :], vo[:, :, odd, :], ACT.Copy)
                    last.then_inc(act_job, 1)

            @block.vector
            def _(dve):
                steps = [0]

                def link(instruction):
                    steps[0] += 1
                    instruction.then_inc(chain, 1)
                    dve.wait_ge(chain, steps[0])

                dve.memset(turned[:, :, :], 1.0)
                link(dve.memset(w["minus_one"][:, :], -1.0))
                dve.tensor_copy(w["v_hi"][:, :, KVLORA:], turned[:, :, :])
                dve.tensor_scalar(w["v_lo"][:, :, KVLORA:], turned[:, :, :], 0.0, None, ALU.mult)
                dve.tensor_copy(w["minus_one_r"][:, :], w["minus_one"][:, :])
                dve.wait_ge(hi_ready, 1)
                dve.tensor_tensor(wkva_lo[:, :, :], wkva[:, :, :], wkva_hi[:, :, :].bitcast(F32), ALU.subtract).then_inc(lo_ready, 1)
                dve.wait_ge(hi_ready, 2)
                dve.tensor_tensor(wqa_lo[:, :, :], wqa[:, :, :], wqa_hi[:, :, :].bitcast(F32), ALU.subtract).then_inc(lo_ready, 1)
                dve.wait_ge(w_in["mask"], 32)
                dve.tensor_copy(w["mask_qk"][:, :], mask[:, 0, :])
                dve.tensor_copy(w["mask_kq"][:, :, :], mask[:, 1, :].unsqueeze(1).to_broadcast([P, HG, P]))

                def after(job):
                    dve.wait_ge(pe_job, job + 1)
                    dve.wait_ge(act_job, job + 1)

                after(QLAT)
                dve.tensor_tensor(w["qlat_lo"][:, :, :], half_of(QLAT)[0:QCH].rearrange("p (c s) -> p c s", c=2),
                                  w["qlat_hi"][:, :, :].bitcast(F32), ALU.subtract).then_inc(dve_job, 1)
                after(KV)
                kv = half_of(KV)[:, 0:NT * P].rearrange("p (t c) -> p t c", t=NT)
                dve.tensor_tensor(w["v_lo"][:, :, 0:KVLORA], kv[:, :, 0:KVLORA],
                                  w["v_hi"][:, :, 0:KVLORA].bitcast(F32), ALU.subtract)
                dve.wait_ge(w_in["rope"], 32)
                pe_part = kv[:, :, KVLORA:]
                for odd in range(2):
                    dve.tensor_tensor(turned[:, :, odd::2], pe_part[:, :, 1 - odd::2], w["sin"][:, :, odd::2], ALU.mult)
                link(dve.tensor_tensor(ktok[:, :, KVLORA:], pe_part, w["cos"][:, :, :], ALU.mult))
                dve.tensor_tensor(ktok[:, :, KVLORA:], ktok[:, :, KVLORA:], turned[:, :, :], ALU.add).then_inc(dve_job, 1)
                after(KT)
                dve.tensor_tensor(w["kT_lo"][:, :], half_of(KT)[:, 0:S], w["kT_hi"][:, :].bitcast(F32),
                                  ALU.subtract).then_inc(dve_job, 1)
                dve.wait_ge(hi_ready, 3)
                dve.tensor_tensor(w["wq_lo"][:, :, :, NOPE:].rearrange("p c h n -> p (c h) n"),
                                  wqb[:, :, :, NOPE:].rearrange("p c h n -> p (c h) n"),
                                  w["wq_hi"][:, :, :, NOPE:].bitcast(F32).rearrange("p c h n -> p (c h) n"), ALU.subtract)
                after(FOLD)
                dve.tensor_tensor(w["wq_lo"][:, :, :, 0:NOPE].rearrange("p c h n -> p (c h) n"),
                                  half_of(FOLD)[0:QCH].rearrange("p (g n) -> p g n", n=KVLORA),
                                  w["wq_hi"][:, :, :, 0:NOPE].bitcast(F32).rearrange("p c h n -> p (c h) n"),
                                  ALU.subtract).then_inc(dve_job, 1)
                for job in (VO0, VO1):
                    after(job)
                    pair = slice((job - VO0) * H2 // 2, (job - VO0 + 1) * H2 // 2)
                    vo = half_of(job)[0:KVLORA].rearrange("p (j o d) -> p j o d", o=2, d=D)
                    for odd in range(2):
                        rows = slice(odd * KVLORA, (odd + 1) * KVLORA)
                        last = dve.tensor_tensor(w["vo_lo"][rows, pair, :], vo[:, :, odd, :],
                                                 w["vo_hi"][rows, pair, :].bitcast(F32), ALU.subtract)
                    last.then_inc(dve_job, 1)


def attn_stage(m, a):
    nc = m.nc
    with ExitStack() as ctx:
        w = {"vo_hi": m.sb("aw_vo_hi", [P, HA // 2, D], F32R, ctx), "vo_lo": m.sb("aw_vo_lo", [P, HA // 2, D], F32R, ctx)}
        o = m.sb("at_o", [P, HA // 2, S], F32, ctx)
        inner = ctx.enter_context(ExitStack())
        for name, shape, dt in (
                ("cos", [P, NT, ROPE], F32), ("sin", [P, NT, ROPE], F32),
                ("qlat_hi", [QCH, 2, S], F32R), ("qlat_lo", [QCH, 2, S], F32R),
                ("wq_hi", [QCH, 2, HA, P], F32R), ("wq_lo", [QCH, 2, HA, P], F32R),
                ("kT_hi", [P, S], F32R), ("kT_lo", [P, S], F32R),
                ("v_hi", [P, NT, P], F32R), ("v_lo", [P, NT, P], F32R),
                ("mask_qk", [P, P], BF16), ("mask_kq", [P, HG, P], BF16),
                ("minus_one", [P, P], F32), ("minus_one_r", [P, P], F32R)):
            w[name] = m.sb(f"aw_{name}", shape, dt, inner)
        attn_prepare(m, a, w, o)

        attn_units(m, w, o)
        inner.close()
        output_stage(m, "ao", o, w["vo_hi"], w["vo_lo"], HA // 2)


def attn_units(m, w, o):
    nc = m.nc
    with ExitStack() as ctx:
        def sb(name, shape, dt=F32):
            return m.sb(f"at_{name}", shape, dt, ctx)

        def sem(name):
            return m.sem(f"at_{name}")

        qt, swapped = sb("qt", [P, HG, P]), sb("swapped", [P, HG, ROPE])
        LAG = 4
        Q, R = 4, LAG + 1
        q_hi, q_lo = sb("q_hi", [P, Q, HALF], F32R), sb("q_lo", [P, Q, HALF], F32R)
        piece_max, row_max = sb("piece_max", [P, 2, HG, 2]), sb("row_max", [P, HG])
        shift = sb("shift", [P, Q, HG, P], F32R)
        p_f, p_hi, p_lo = sb("p_f", [P, 3, HALF]), sb("p_hi", [P, R, HALF], F32R), sb("p_lo", [P, R, HALF], F32R)
        sums, rec_few, rec = sb("sums", [KVLORA, HALF]), sb("rec_few", [KVLORA, HALF // 32]), sb("rec", [KVLORA, HG, P])
        qtok_ps = m.ps("at_qtok_ps", [P, HALF], F32, ctx)      
        qT_ps = m.ps("at_qT_ps", [P, HALF], F32, ctx)
        mx_ps = m.ps("at_mx_ps", [P, 2, HALF], F32, ctx)
        st_ps = m.ps("at_st_ps", [P, 2, HALF], F32, ctx)
        acc_ps = m.ps("at_acc_ps", [P, 2, HALF], F32, ctx)

        qtok_done, swap_done, rope_done, qT_done = sem("qtok_done"), sem("swap_done"), sem("rope_done"), sem("qT_done")
        q_hi_done, q_lo_done = sem("q_hi_done"), sem("q_lo_done")
        q_copied = sem("q_copied")
        mx_done, piece_done, row_max_done, shift_done = sem("mx_done"), sem("piece_done"), sem("row_max_done"), sem("shift_done")
        st_done, exp_done, p_hi_done, p_lo_done, pv_done = (
            sem("st_done"), sem("exp_done"), sem("p_hi_done"), sem("p_lo_done"), sem("pv_done"))
        sums_done, few_done, rec_done, norm_done = sem("sums_done"), sem("few_done"), sem("rec_done"), sem("norm_done")

        units = [(i, g) for i in range(NT) for g in range(HA // HG)]
        first = [sum(units[v][0] + 1 for v in range(u)) for u in range(len(units) + 1)]
        steps = [(u, j) for u, (i, g) in enumerate(units) for j in range(i + 1)]

        def pieces(u):
            keys = (units[u][0] + 1) * P
            return [(h, n, lo, min(lo + HALF, keys)) for h in range(HG) for n, lo in enumerate(range(0, keys, HALF))]

        first_piece = [sum(len(pieces(v)) for v in range(u)) for u in range(len(units))]

        def during(u):
            def of(v, parts):
                return [(v, *part) for part in parts] if 0 <= v < len(units) else []
            maxima = [("max", r, *p) for r, p in enumerate(pieces(u + 2))] if 0 <= u + 2 < len(units) else []
            half = len(maxima) // 2
            return (of(u + 3, [("turn",)]) + of(u + 2, maxima[:half]) + of(u + 4, [("queries",)])
                    + of(u + 2, maxima[half:]) + of(u + 2, [("shift",)]))

        before = [part for u in range(-4, 0) for part in during(u)]

        def between(k):
            u, j = steps[k]
            todo, n = during(u), units[u][0] + 1
            return todo[len(todo) * j // n:len(todo) * (j + 1) // n]

        with nc.Block() as block:

            @block.tensor
            def _(pe):
                def prepare(u, kind, *args):
                    i, g = units[u]
                    tok = slice(i * P, (i + 1) * P)
                    if kind == "queries":
                        if u >= 1:
                            pe.wait_ge(swap_done, u)
                        for c in range(2):
                            heads = slice(g * HG, (g + 1) * HG)
                            last = mm3(pe, qtok_ps[:, :], [w[q][:, c, tok] for q in ("qlat_hi", "qlat_lo")],
                                       [w[q][:, c, heads, :].rearrange("p h n -> p (h n)") for q in ("wq_hi", "wq_lo")],
                                       c == 0, c == 1)
                        last.then_inc(qtok_done, 1)
                    elif kind == "turn":
                        pe.wait_ge(rope_done, u + 1)
                        if u >= 1:
                            pe.wait_ge(q_lo_done, u)
                        for h in range(HG):
                            last = pe.transpose(qT_ps[:, h * P:(h + 1) * P], qt[:, h, :], m.ident[:, :])
                        last.then_inc(qT_done, 1)
                    elif kind == "max":
                        r, h, n, lo, hi = args
                        r += first_piece[u]
                        pe.wait_ge(q_hi_done, u + 1)
                        if r >= 2:
                            pe.wait_ge(piece_done, r - 1)
                        diagonal = hi == (i + 1) * P
                        last = pe.matmul(mx_ps[:, r % 2, 0:hi - lo], q_hi[:, u % Q, h * P:(h + 1) * P],
                                         w["kT_hi"][:, lo:hi], start=True, stop=not diagonal)
                        if diagonal:
                            last = pe.matmul(mx_ps[:, r % 2, hi - lo - P:hi - lo], m.identb[:, :], w["mask_qk"][:, :],
                                             start=False, stop=True)
                        last.then_inc(mx_done, 1)

                def scores(k):
                    u, j = steps[k]
                    if j == 0:
                        pe.wait_ge(q_lo_done, u + 1)
                        pe.wait_ge(shift_done, u + 1)
                    if k >= 2:
                        pe.wait_ge(exp_done, k - 1)
                    diagonal = j == units[u][0]
                    out = st_ps[:, k % 2, :]
                    mm3(pe, out, [w[q][:, j * P:(j + 1) * P] for q in ("kT_hi", "kT_lo")],
                        (q_hi[:, u % Q, :], q_lo[:, u % Q, :]), True, False)
                    last = pe.matmul(out, w["minus_one_r"][:, :], shift[:, u % Q, :, :].rearrange("p h q -> p (h q)"),
                                     start=False, stop=not diagonal)
                    if diagonal:
                        last = pe.matmul(out, m.identb[:, :], w["mask_kq"][:, :, :].rearrange("p h q -> p (h q)"),
                                         start=False, stop=True)
                    last.then_inc(st_done, 1)

                def values(k):
                    u, j = steps[k]
                    if j == 0 and u >= 2:
                        pe.wait_ge(norm_done, u - 1)
                    pe.wait_ge(p_lo_done, k + 1)
                    mm3(pe, acc_ps[:, u % 2, :], [w[q][:, j, :] for q in ("v_hi", "v_lo")],
                        (p_hi[:, k % R, :], p_lo[:, k % R, :]), j == 0, j == units[u][0]).then_inc(pv_done, 1)

                for part in before:
                    prepare(*part)
                for k in range(len(steps) + LAG):
                    todo = between(k) if k < len(steps) else []
                    if k < len(steps):
                        scores(k)
                    for part in todo[:len(todo) // 2]:
                        prepare(*part)
                    if k >= LAG:
                        values(k - LAG)
                    for part in todo[len(todo) // 2:]:
                        prepare(*part)

            @block.vector
            def _(dve):
                def prepare(u, kind, *args):
                    i, g = units[u]
                    if kind == "queries":
                        dve.wait_ge(q_copied, u + 1)
                        if u >= 1:
                            dve.wait_ge(qT_done, u)
                        q = qtok_ps[:, :].rearrange("p (h n) -> p h n", h=HG)[:, :, NOPE:]
                        for odd in range(2):
                            dve.tensor_tensor(swapped[:, :, odd::2], q[:, :, 1 - odd::2],
                                              w["sin"][:, i, odd::2].unsqueeze(1).to_broadcast([P, HG, ROPE // 2]), ALU.mult)
                        dve.tensor_tensor(qt[:, :, NOPE:], q, w["cos"][:, i, :].unsqueeze(1).to_broadcast([P, HG, ROPE]),
                                          ALU.mult).then_inc(swap_done, 1)
                        dve.wait_ge(swap_done, u + 1)
                        dve.tensor_tensor(qt[:, :, NOPE:], qt[:, :, NOPE:], swapped[:, :, :], ALU.add).then_inc(rope_done, 1)
                    elif kind == "turn":
                        dve.wait_ge(q_hi_done, u + 1)
                        dve.tensor_tensor(q_lo[:, u % Q, :], qT_ps[:, :], q_hi[:, u % Q, :].bitcast(F32),
                                          ALU.subtract).then_inc(q_lo_done, 1)
                    elif kind == "max":
                        r, h, n, lo, hi = args
                        r += first_piece[u]
                        dve.wait_ge(mx_done, r + 1)
                        if h == n == 0 and u >= 2:
                            dve.wait_ge(row_max_done, u - 1)
                        dve.tensor_reduce(piece_max[:, u % 2, h, n:n + 1], mx_ps[:, r % 2, 0:hi - lo], AX_X,
                                          ALU.max).then_inc(piece_done, 1)
                    else:
                        count = len(pieces(u))
                        dve.wait_ge(piece_done, first_piece[u] + count)
                        if u >= 1:
                            dve.wait_ge(shift_done, u)
                        dve.tensor_reduce(row_max[:, :], piece_max[:, u % 2, :, 0:count // HG], AX_X,
                                          ALU.max).then_inc(row_max_done, 1)

                def gather(u):
                    dve.wait_ge(pv_done, first[u + 1])
                    dve.transpose(sums[:, :], acc_ps[KVLORA:, u % 2, :]).then_inc(sums_done, 1)

                def invert(u):
                    dve.wait_ge(sums_done, u + 1)
                    dve.reciprocal(rec_few[:, :], sums[:, ::32]).then_inc(few_done, 1)

                def spread(u):
                    dve.wait_ge(few_done, u + 1)
                    dve.transpose(rec[:, :, :].rearrange("p h q -> p (h q)"),
                                  rec_few[:, :].unsqueeze(2).to_broadcast([KVLORA, HALF // 32, 32])).then_inc(rec_done, 1)

                def scale(u):
                    dve.wait_ge(rec_done, u + 1)
                    i, g = units[u]
                    acc = acc_ps[:, u % 2, :].rearrange("p (h q) -> p h q", h=HG)
                    for odd in range(2):
                        last = dve.tensor_tensor(o[odd * KVLORA:(odd + 1) * KVLORA, g * HG // 2:(g + 1) * HG // 2,
                                                   i * P:(i + 1) * P],
                                                 acc[0:KVLORA, odd::2, :], rec[:, odd::2, :], ALU.mult)
                    last.then_inc(norm_done, 1)

                def finished(k):
                    return [steps[k][0]] if 0 <= k < len(steps) and steps[k][1] == units[steps[k][0]][0] else []

                for part in before:
                    prepare(*part)
                for k in range(len(steps) + LAG + 1):
                    todo = between(k) if k < len(steps) else []
                    for part in todo[:len(todo) // 2]:
                        prepare(*part)
                    for u in finished(k - LAG - 1):
                        spread(u)
                    for u in finished(k - LAG):
                        gather(u)
                    for part in todo[len(todo) // 2:]:
                        prepare(*part)
                    for u in finished(k - LAG - 1):
                        scale(u)
                    for u in finished(k - LAG):
                        invert(u)

            @block.gpsimd
            def _(pool):
                def prepare(u, kind, *args):
                    if kind == "shift":
                        pool.wait_ge(row_max_done, u + 1)
                        if u >= Q:
                            pool.wait_ge(st_done, first[u - Q + 1])
                        pool.tensor_tensor(shift[:, u % Q, :, :], m.ident[:, :].unsqueeze(1).to_broadcast([P, HG, P]),
                                           row_max[:, :].unsqueeze(2).to_broadcast([P, HG, P]),
                                           ALU.mult).then_inc(shift_done, 1)

                def low(k):
                    pool.wait_ge(p_hi_done, k + 1)
                    if k >= R:
                        pool.wait_ge(pv_done, k - R + 1)
                    pool.tensor_tensor(p_lo[:, k % R, :], p_f[:, k % 3, :], p_hi[:, k % R, :].bitcast(F32),
                                       ALU.subtract).then_inc(p_lo_done, 1)

                for part in before:
                    prepare(*part)
                for k in range(len(steps)):
                    for part in between(k):
                        prepare(*part)
                    low(k)

            @block.scalar
            def _(act):
                def prepare(u, kind, *args):
                    if kind == "queries":
                        act.wait_ge(qtok_done, u + 1)
                        if u >= 1:
                            act.wait_ge(qT_done, u)
                        act.activation(qt[:, :, 0:NOPE], qtok_ps[:, :].rearrange("p (h n) -> p h n", h=HG)[:, :, 0:NOPE],
                                       ACT.Copy).then_inc(q_copied, 1)
                    elif kind == "turn":
                        act.wait_ge(qT_done, u + 1)
                        if u >= Q:
                            act.wait_ge(st_done, first[u - Q + 1])
                        act.activation(q_hi[:, u % Q, :], qT_ps[:, :], ACT.Copy).then_inc(q_hi_done, 1)

                def exponent(k):
                    act.wait_ge(st_done, k + 1)
                    if k >= 3:
                        act.wait_ge(p_lo_done, k - 2)
                    act.activation(p_f[:, k % 3, :], st_ps[:, k % 2, :], ACT.Exp, scale=QSCALE).then_inc(exp_done, 1)

                def high(k):
                    act.wait_ge(exp_done, k + 1)
                    if k >= R:
                        act.wait_ge(pv_done, k - R + 1)
                    act.activation(p_hi[:, k % R, :], p_f[:, k % 3, :], ACT.Copy).then_inc(p_hi_done, 1)

                for part in before:
                    prepare(*part)
                for k in range(len(steps)):
                    exponent(k)
                    high(k)
                    for part in between(k):
                        prepare(*part)


def output_stage(m, tag, o, w_hi, w_lo, chunks, w_dram=None):
    nc = m.nc
    with ExitStack() as ctx:
        raw = m.sb(f"{tag}_raw", [P, chunks, D], F32, ctx) if w_dram is not None else None
        o_hi = m.sb(f"{tag}_o_hi", [P, 2, chunks, P], F32R, ctx)
        o_lo = m.sb(f"{tag}_o_lo", [P, 2, chunks, P], F32R, ctx)
        out_ps = m.ps(f"{tag}_out_ps", [P, NT, HALF], F32, ctx)
        o_hi_done, o_lo_done, out_done = m.sem(f"{tag}_o_hi_done"), m.sem(f"{tag}_o_lo_done"), m.sem(f"{tag}_out_done")
        w_hi_done, w_lo_done = m.sem(f"{tag}_w_hi_done"), m.sem(f"{tag}_w_lo_done")
        pieces = [slice(n * chunks // 4, (n + 1) * chunks // 4) for n in range(4)] if w_dram is not None else []
        w_in = [m.sem(f"{tag}_w_in{n}") for n in range(len(pieces))]
        with nc.Block() as block:

            @block.sync
            def _(sp):
                for n, piece in enumerate(pieces):
                    sp.dma_start(raw[:, piece, :], w_dram[:, piece, :]).then_inc(w_in[n], 16)

            @block.scalar
            def _(act):
                def high(t):
                    if t >= 2:
                        act.wait_ge(out_done, t - 1)
                    act.activation(o_hi[:, t % 2, :, :], o[:, :, t * P:(t + 1) * P], ACT.Copy).then_inc(o_hi_done, 1)

                high(0)
                for n, piece in enumerate(pieces):
                    act.wait_ge(w_in[n], 16)
                    act.activation(w_hi[:, piece, :], raw[:, piece, :], ACT.Copy).then_inc(w_hi_done, 1)
                for t in range(1, NT):
                    high(t)

            @block.tensor
            def _(pe):
                for t in range(NT):
                    pe.wait_ge(o_lo_done, t + 1)
                    for j in range(chunks):
                        if t == 0 and pieces and j % (chunks // 4) == 0:
                            pe.wait_ge(w_lo_done, j // (chunks // 4) + 1)
                        last = mm3(pe, out_ps[:, t, 0:D], (o_hi[:, t % 2, j, :], o_lo[:, t % 2, j, :]),
                                   (w_hi[:, j, :], w_lo[:, j, :]), j == 0, j == chunks - 1)
                    last.then_inc(out_done, 1)

            @block.vector
            def _(dve):
                def low(t):
                    dve.wait_ge(o_hi_done, t + 1)
                    dve.tensor_tensor(o_lo[:, t % 2, :, :], o[:, :, t * P:(t + 1) * P],
                                      o_hi[:, t % 2, :, :].bitcast(F32), ALU.subtract).then_inc(o_lo_done, 1)

                low(0)
                for n, piece in enumerate(pieces):
                    dve.wait_ge(w_hi_done, n + 1)
                    dve.tensor_tensor(w_lo[:, piece, :], raw[:, piece, :], w_hi[:, piece, :].bitcast(F32),
                                      ALU.subtract).then_inc(w_lo_done, 1)
                for t in range(NT):
                    if t + 1 < NT:
                        low(t + 1)
                    dve.wait_ge(out_done, t + 1)
                    dve.tensor_tensor(m.x[:, t, :], m.x[:, t, :], out_ps[:, t, 0:D], ALU.add)


def value_stage(m, a, v_all, rows_dram, prefetch):
    nc = m.nc
    with ExitStack() as ctx:
        def sb(name, shape, dt=F32):
            return m.sb(f"lv_{name}", shape, dt, ctx)

        def sem(name):
            return m.sem(f"lv_{name}")

        wb = sb("wb", [P, KD, HB])
        wb_hi, wb_lo = sb("wb_hi", [P, KD, P], F32R), sb("wb_lo", [P, KD, P], F32R)
        zT = sb("zT", [HB, S])
        bb = sb("bb", [P, HB])
        wv = sb("wv", [P, KD, HB * DV])
        wv_hi, wv_lo = sb("wv_hi", [P, KD, HB * DV], F32R), sb("wv_lo", [P, KD, HB * DV], F32R)
        z, ez = sb("z", [P, NT, HB]), sb("ez", [P, 2, NT, HB])
        beta, keep = sb("beta", [P, NT, HB]), sb("keep", [P, NT, HB])
        keepT, prodT, zeros = sb("keepT", [HB, S]), sb("prodT", [HB, S]), sb("zeros", [HB, P])
        GV = HALF // DV
        NGV = HB // GV
        wb_loaded, rows_stored = sem("wb_loaded"), sem("rows_stored")
        wv_loaded = [sem(f"wv_loaded{g}") for g in range(NGV)]

        def first_loads(sp):
            sp.dma_start(wb[:, :, :], a["b_Wb"].rearrange("(k p) n -> p k n", p=P)).then_inc(wb_loaded, 16)
            sp.dma_start(bb[:, :], a["b_bb"].rearrange("(a n) -> a n", a=1).to_broadcast([P, HB])).then_inc(wb_loaded, 16)
            for g in range(NGV):
                cols = slice(g * HALF, (g + 1) * HALF)
                sp.dma_start(wv[:, :, cols], a["b_Wv"].rearrange("(k p) n -> p k n", p=P)[:, :, cols]).then_inc(wv_loaded[g], 16)

        norm_stage(m, "linear_norm", first_loads)

        z_ps = m.ps("lv_z_ps", [P, NT, HB], F32, ctx)
        keepT_ps = m.ps("lv_keepT_ps", [P, S], F32, ctx)
        v_ps = m.ps("lv_v_ps", [P, 4, HALF], F32, ctx)
        hi_done, lo_done = sem("hi_done"), sem("lo_done")
        padded, zT_done, zT_sb = sem("padded"), sem("zT_done"), sem("zT_sb")
        z_done, z_sb, ez_done, soft, keepT_done, keepT_sb, prod_done = (
            sem("z_done"), sem("z_sb"), sem("ez_done"), sem("soft"), sem("keepT_done"), sem("keepT_sb"), sem("prod_done"))
        v_done, v_out = sem("v_done"), sem("v_out")
        units = [(g, t) for g in range(NGV) for t in range(NT)]

        with nc.Block() as block:

            @block.sync
            def _(sp):
                prefetch(sp)
                sp.wait_ge(keepT_sb, 1)
                sp.dma_start(rows_dram[0], keepT[:, :]).then_inc(rows_stored, 16)
                sp.wait_ge(prod_done, NT)
                sp.dma_start(rows_dram[1], prodT[:, :]).then_inc(rows_stored, 16)
                sp.wait_ge(rows_stored, 32)

            @block.tensor
            def _(pe):
                pe.wait_ge(lo_done, 1)
                for half in range(2):
                    tok = slice(half * HALF, (half + 1) * HALF)
                    for k in range(KD):
                        last = mm3(pe, keepT_ps[:, tok], (wb_hi[:, k, :], wb_lo[:, k, :]),
                                   (m.h_hi[:, k, tok], m.h_lo[:, k, tok]), k == 0, k == KD - 1)
                    last.then_inc(zT_done, 1)

                def value(n):
                    g, t = units[n]
                    tok = slice(t * P, (t + 1) * P)
                    if t == 0:
                        pe.wait_ge(lo_done, g + 2)
                    if n >= 4:
                        pe.wait_ge(v_out, n - 3)
                    for k in range(KD):
                        last = mm3(pe, v_ps[:, n % 4, :], (m.h_hi[:, k, tok], m.h_lo[:, k, tok]),
                                   [p[:, k, g * HALF:(g + 1) * HALF] for p in (wv_hi, wv_lo)], k == 0, k == KD - 1)
                    last.then_inc(v_done, 1)

                for n in range(len(units)):
                    if n == 1:
                        for t in range(NT):
                            if t % (NT // 2) == 0:
                                pe.wait_ge(zT_sb, t // (NT // 2) + 1)
                            last = pe.transpose(z_ps[:, t, :], zT[:, t * P:(t + 1) * P], m.ident[0:HB, 0:HB])
                        last.then_inc(z_done, 1)
                    if n == 4:
                        pe.wait_ge(soft, 4)
                        for t in range(NT):
                            last = pe.transpose(keepT_ps[0:HB, t * P:(t + 1) * P], keep[:, t, :], m.ident[:, :])
                        last.then_inc(keepT_done, 1)
                    value(n)

            @block.scalar
            def _(act):
                act.wait_ge(wb_loaded, 32)
                act.wait_ge(padded, 2)
                act.activation(wb_hi[:, :, 0:HB], wb[:, :, :], ACT.Copy).then_inc(hi_done, 1)

                def split(g):
                    cols = slice(g * HALF, (g + 1) * HALF)
                    act.wait_ge(wv_loaded[g], 16)
                    act.activation(wv_hi[:, :, cols], wv[:, :, cols], ACT.Copy).then_inc(hi_done, 1)

                split(0)
                for half in range(2):
                    tok = slice(half * HALF, (half + 1) * HALF)
                    act.wait_ge(zT_done, half + 1)
                    act.activation(zT[:, tok], keepT_ps[0:HB, tok], ACT.Copy).then_inc(zT_sb, 1)
                act.wait_ge(z_sb, 1)
                act.activation(ez[:, 0, :, :], z[:, :, :], ACT.Exp, scale=-1.0)
                act.activation(ez[:, 1, :, :], z[:, :, :], ACT.Exp).then_inc(ez_done, 1)
                for g in range(1, NGV):
                    split(g)
                act.wait_ge(keepT_done, 1)
                act.activation(keepT[:, :], keepT_ps[0:HB, :], ACT.Copy).then_inc(keepT_sb, 1)

            @block.vector
            def _(dve):
                dve.memset(wb_hi[:, :, :].bitcast(F32), 0.0).then_inc(padded, 1)
                dve.memset(wb_lo[:, :, :].bitcast(F32), 0.0).then_inc(padded, 1)
                dve.memset(zeros[:, :], 0.0)
                dve.wait_ge(hi_done, 1)
                dve.tensor_tensor(wb_lo[:, :, 0:HB], wb[:, :, :], wb_hi[:, :, 0:HB].bitcast(F32), ALU.subtract).then_inc(lo_done, 1)

                def split(g):
                    cols = slice(g * HALF, (g + 1) * HALF)
                    dve.wait_ge(hi_done, g + 2)
                    dve.tensor_tensor(wv_lo[:, :, cols], wv[:, :, cols], wv_hi[:, :, cols].bitcast(F32),
                                      ALU.subtract).then_inc(lo_done, 1)

                split(0)
                dve.wait_ge(z_done, 1)
                dve.tensor_tensor(z[:, :, :], z_ps[:, :, :], bb[:, :].unsqueeze(1).to_broadcast([P, NT, HB]),
                                  ALU.add).then_inc(z_sb, 1)
                dve.wait_ge(ez_done, 1)
                for n, out in enumerate((beta, keep)):
                    dve.tensor_scalar(ez[:, n, :, :], ez[:, n, :, :], 1.0, None, ALU.add).then_inc(soft, 1)
                for n, out in enumerate((beta, keep)):
                    dve.wait_ge(soft, n + 1)
                    dve.reciprocal(out[:, :, :], ez[:, n, :, :]).then_inc(soft, 1)
                dve.wait_ge(soft, 3)
                for n, (g, t) in enumerate(units):
                    if t == 4 and g + 1 < NGV:
                        split(g + 1)
                    if n == 6:
                        dve.wait_ge(keepT_sb, 1)
                        for c in range(NT):
                            at = slice(c * P, (c + 1) * P)
                            dve.tensor_tensor_scan(prodT[:, at], keepT[:, at], zeros[:, :], 1.0, ALU.mult,
                                                   ALU.add).then_inc(prod_done, 1)
                    dve.wait_ge(v_done, n + 1)
                    dve.tensor_tensor(v_all[:, g * GV:(g + 1) * GV, t * P:(t + 1) * P],
                                      v_ps[:, n % 4, :].rearrange("p (h v) -> p h v", v=DV),
                                      beta[:, t, g * GV:(g + 1) * GV].unsqueeze(2).to_broadcast([P, GV, DV]),
                                      ALU.mult).then_inc(v_out, 1)


class HeadWeights:

    def __init__(self, m, a, ctx):
        def sb(name, shape):
            return m.sb(f"lh_{name}", shape, F32, ctx)

        self.a = a
        self.raw_qk, self.raw_g = sb("raw_qk", [P, 2, KD, DK]), sb("raw_g", [P, KD, DK])
        self.conv = [sb(f"conv{b}", [P, 2, TAPS + 1]) for b in range(2)]
        self.norm = sb("norm", [P, 4])
        self.qk_in, self.g_in, self.norm_in = m.sem("lh_qk_in"), m.sem("lh_g_in"), m.sem("lh_norm_in")

    def load_qk(self, sp, h, b):
        for n, name in enumerate(("b_Wq", "b_Wk")):
            sp.dma_start(self.raw_qk[:, n, :, :],
                         self.a[name].rearrange("(k p) n -> p k n", p=P)[:, :, ds(h * DK, DK)]).then_inc(self.qk_in, 16)
        sp.dma_start(self.conv[b][:, :, :].rearrange("p z c -> p (z c)"),
                     self.a["conv"][ds(h, 1), :, :].rearrange("a p c -> p (a c)")).then_inc(self.qk_in, 16)

    def load_g(self, sp, h):
        sp.dma_start(self.raw_g[:, :, :],
                     self.a["b_Wg"].rearrange("(k p) n -> p k n", p=P)[:, :, ds(h * DK, DK)]).then_inc(self.g_in, 16)

    def first_loads(self, sp):
        self.load_qk(sp, 0, 0)
        self.load_g(sp, 0)
        sp.dma_start(self.norm[:, :], self.a["norm"]).then_inc(self.norm_in, 16)


def head_stage(m, heads, v_all, rows_dram):
    nc = m.nc
    with ExitStack() as ctx:
        def sb(name, shape, dt=F32):
            return m.sb(f"lh_{name}", shape, dt, ctx)

        def sem(name):
            return m.sem(f"lh_{name}")

        raw_qk, raw_g, conv, norm = heads.raw_qk, heads.raw_g, heads.conv, heads.norm
        qk_in, g_in, norm_in = heads.qk_in, heads.g_in, heads.norm_in
        qk_hi = [sb(f"qk_hi{b}", [P, 2, KD, DK], F32R) for b in range(2)]
        qk_lo = [sb(f"qk_lo{b}", [P, 2, KD, DK], F32R) for b in range(2)]
        g_hi = [sb(f"g_hi{b}", [P, KD, DK], F32R) for b in range(2)]
        g_lo = [sb(f"g_lo{b}", [P, KD, DK], F32R) for b in range(2)]
        PAD = TAPS - 1
        pre = sb("pre", [P, 2, PAD + S])
        y = [sb(f"y{b}", [P, 2, S]) for b in range(2)]
        yn = sb("yn", [P, 2, 4, DK])
        qT = [sb(f"qT{b}", [P, S]) for b in range(2)]
        kT = [sb(f"kT{b}", [P, S]) for b in range(2)]
        ktok = [sb(f"ktok{b}", [P, NT, DK]) for b in range(2)]
        gate = [sb(f"gate{b}", [P, S]) for b in range(2)]
        v = [sb(f"v{b}", [P, NT, DV]) for b in range(2)]
        prod = [sb(f"prod{b}", [P, S]) for b in range(2)]
        keep = sb("keep", [P, S])
        stats, mv = sb("stats", [P, 4, 6]), sb("mv", [P, 2, 4, 2])
        ve, rstd, nbias = sb("ve", [P, 2, 4]), sb("rstd", [P, 2, 4]), sb("nbias", [P, 2, 4])
        decay, probs, qg = sb("decay", [P, S]), sb("probs", [P, S]), sb("qg", [P, S])
        vd = sb("vd", [P, NT, DV])
        state = sb("state", [P, NT, DV])

        proj_ps = m.ps("lh_proj_ps", [P, 2, HALF], F32, ctx)
        tok_ps = m.ps("lh_tok_ps", [P, 2, HALF], F32, ctx)
        back_ps = m.ps("lh_back_ps", [P, HALF], F32, ctx)
        ds_ps = m.ps("lh_ds_ps", [P, HALF], F32, ctx)
        so_ps = m.ps("lh_so_ps", [P, 2, HALF], F32, ctx)

        padded, keep_in = sem("padded"), sem("keep_in")
        v_in = [sem(f"v_in{b}") for b in range(2)]
        qk_hi_done, qk_lo_done, g_hi_done, g_lo_done = sem("qk_hi_done"), sem("qk_lo_done"), sem("g_hi_done"), sem("g_lo_done")
        qk_proj_done, g_proj_done, qk_out, g_out = sem("qk_proj_done"), sem("g_proj_done"), sem("qk_out"), sem("g_out")
        tap_done, silu_done, tok_done = sem("tap_done"), sem("silu_done"), sem("tok_done")
        stats_done, aggr_done, ve_done, rstd_done, nbias_done = (
            sem("stats_done"), sem("aggr_done"), sem("ve_done"), sem("rstd_done"), sem("nbias_done"))
        aggr_begun = sem("aggr_begun")
        yn_done, back_done, hat_done, keys_turned, ktok_done = (
            sem("yn_done"), sem("back_done"), sem("hat_done"), sem("keys_turned"), sem("ktok_done"))
        decay_done, sc_done, probs_done, vd_done, qg_done = (
            sem("decay_done"), sem("sc_done"), sem("probs_done"), sem("vd_done"), sem("qg_done"))
        ds_done, state_done, o_done, og_done = sem("ds_done"), sem("state_done"), sem("o_done"), sem("og_done")
        C_QKPROJ, C_GPROJ, C_GOUT, C_TAP, C_TOK, C_YN, C_BACK, C_HAT, C_KTOK = 5, 3, 4, 12, 5, 2, 2, 1, 2
        C_VD, C_DS, C_STATE, C_O, C_OG = 2, 2, 7, 3, 3
        BLK = NT // 2
        LOOPED = (HB - 4) // 2

        def half_of(half):
            return slice(half * HALF, (half + 1) * HALF)

        def chunk(c):
            return slice(c * P, (c + 1) * P)

        def does(h):
            heads = {"project": h + 2, "normalise": h + 1, "attend": h, "split qk": h + 3, "split g": h + 2,
                     "load qk": h + 4, "load g": h + 3, "load values": h + 1 if h >= 0 else -1}
            return {part for part, head in heads.items() if 0 <= head < HB}

        def all_steps(engine, step):
            for h in (-2, -1):
                step(h, h % 2, h // 2, does(h))
            with engine.Fori(0, LOOPED) as i:
                step(2 * i, 0, i, does(0))
                step(2 * i + 1, 1, i, does(0))
            for h in range(2 * LOOPED, HB):
                step(h, h % 2, h // 2, does(h))

        with nc.Block() as block:

            @block.sync
            def _(sp):
                def load_values(h, b):
                    sp.dma_start(v[b][:, :, :].rearrange("p c v -> p (c v)"),
                                 v_all[:, ds(h, 1), :].rearrange("p a s -> p (a s)")).then_inc(v_in[b], 16)
                    sp.dma_start(prod[b][:, :], rows_dram[1, ds(h, 1), :].to_broadcast([P, S])).then_inc(v_in[b], 16)

                def load_keep(h):
                    sp.dma_start(keep[:, :], rows_dram[0, ds(h, 1), :].to_broadcast([P, S])).then_inc(keep_in, 16)

                def step(h, b, turn, parts):
                    if "load values" in parts:
                        sp.wait_ge(o_done, 2 * h + C_O)
                        load_values(h + 1, 1 - b)
                        sp.wait_ge(decay_done, NT * (h + 1))
                        load_keep(h + 1)
                    if "load g" in parts:
                        sp.wait_ge(g_lo_done, h + 3)
                        heads.load_g(sp, h + 3)
                    if "load qk" in parts:
                        sp.wait_ge(qk_lo_done, h + 4)
                        sp.wait_ge(tap_done, 12 * (h + 3) + C_TAP)
                        heads.load_qk(sp, h + 4, b)

                load_values(0, 0)
                load_keep(0)
                sp.wait_ge(qk_lo_done, 1)
                heads.load_qk(sp, 1, 1)
                all_steps(sp, step)

            @block.tensor
            def _(pe):
                pe.sem_inc(qk_proj_done, C_QKPROJ)
                pe.sem_inc(g_proj_done, C_GPROJ)
                pe.sem_inc(tok_done, C_TOK)
                pe.sem_inc(back_done, C_BACK)
                pe.sem_inc(ds_done, C_DS)
                pe.sem_inc(o_done, C_O)

                def project(h, b, n):
                    kind, half = n // 2, n % 2
                    pe.wait_ge(qk_lo_done, h + 1)
                    if kind == 0:
                        pe.wait_ge(g_out, 2 * (h - 2) + half + 1 + C_GOUT)
                    else:
                        pe.wait_ge(qk_out, 4 * h + half + 1)
                    for k in range(KD):
                        last = mm3(pe, proj_ps[:, n % 2, :], (qk_hi[b][:, kind, k, :], qk_lo[b][:, kind, k, :]),
                                   (m.h_hi[:, k, half_of(half)], m.h_lo[:, k, half_of(half)]), k == 0, k == KD - 1)
                    last.then_inc(qk_proj_done, 1)

                def project_gate(h, b, half, after_keys):
                    pe.wait_ge(g_lo_done, h + 1)
                    if after_keys:
                        pe.wait_ge(qk_out, 4 * (h + 1) + 2 + half + 1)
                    else:
                        pe.wait_ge(g_out, 2 * (h - 1) + half + 1 + C_GOUT)
                    for k in range(KD):
                        last = mm3(pe, proj_ps[:, half, :], (g_hi[b][:, k, :], g_lo[b][:, k, :]),
                                   (m.h_hi[:, k, half_of(half)], m.h_lo[:, k, half_of(half)]), k == 0, k == KD - 1)
                    last.then_inc(g_proj_done, 1)

                def to_tokens(h, b, p):
                    pe.wait_ge(silu_done, 4 * h + p + 1)
                    pe.wait_ge(yn_done, 4 * h + p + 1)
                    for c in range(BLK):
                        at = chunk((p % 2) * BLK + c)
                        last = pe.transpose(tok_ps[:, p % 2, chunk(c)], y[b][:, p // 2, at], m.ident[:, :])
                    last.then_inc(tok_done, 1)

                def to_features(h, p):
                    pe.wait_ge(yn_done, 4 * h + p + 1 + C_YN)
                    pe.wait_ge(hat_done, 4 * h + p + 1)
                    if p == 0:
                        pe.wait_ge(ktok_done, 2 * h + C_KTOK)
                    for c in range(BLK):
                        last = pe.transpose(back_ps[:, chunk(c)], yn[:, p % 2, c, :], m.ident[:, :])
                    last.then_inc(back_done, 1)

                def keys(h, b, half):
                    pe.wait_ge(hat_done, 4 * h + 4 + C_HAT)
                    pe.wait_ge(ktok_done, 2 * h + half + C_KTOK)
                    for c in range(BLK):
                        last = pe.transpose(back_ps[:, chunk(c)], kT[b][:, chunk(half * BLK + c)], m.ident[:, :])
                    last.then_inc(keys_turned, 1)

                def scores(h, b, half):
                    pe.wait_ge(hat_done, 4 * h + 4 + C_HAT)
                    pe.wait_ge(og_done, 2 * h + half - 1 + C_OG)
                    for c in range(BLK):
                        at = chunk(half * BLK + c)
                        last = pe.matmul(so_ps[:, half, chunk(c)], kT[b][:, at], qT[b][:, at], start=True, stop=True)
                    last.then_inc(sc_done, 1)

                def state_change(h, b, half):
                    pe.wait_ge(ktok_done, 2 * h + 2 + C_KTOK)
                    pe.wait_ge(vd_done, 2 * h + half + 1 + C_VD)
                    pe.wait_ge(state_done, 7 * h + 4 * half + C_STATE)
                    for c in range(BLK):
                        n = half * BLK + c
                        if n < NT - 1:
                            last = pe.matmul(ds_ps[:, chunk(c)], ktok[b][:, n, :], vd[:, n, :], start=True, stop=True)
                    last.then_inc(ds_done, 1)

                def output(h, b, half):
                    pe.wait_ge(probs_done, 2 * h + half + 1)
                    pe.wait_ge(qg_done, 2 * h + half + 1)
                    pe.wait_ge(state_done, 7 * h + (3 if half == 0 else 7) + C_STATE)
                    for c in range(BLK):
                        n = half * BLK + c
                        last = pe.matmul(so_ps[:, half, chunk(c)], v[b][:, n, :], probs[:, chunk(n)], start=True, stop=n == 0)
                        if n:
                            last = pe.matmul(so_ps[:, half, chunk(c)], state[:, n, :], qg[:, chunk(n)], start=False, stop=True)
                    last.then_inc(o_done, 1)

                def step(h, b, turn, parts):
                    def new(n):
                        if "project" in parts:
                            project(h + 2, b, n)

                    if "normalise" in parts:
                        to_tokens(h + 1, 1 - b, 0)
                        to_tokens(h + 1, 1 - b, 1)
                    new(0)
                    if "attend" in parts:
                        keys(h, b, 0)
                        scores(h, b, 0)
                        scores(h, b, 1)
                        keys(h, b, 1)
                    new(1)
                    if "normalise" in parts:
                        to_features(h + 1, 0)
                        to_tokens(h + 1, 1 - b, 2)
                    if "attend" in parts:
                        state_change(h, b, 0)
                    new(2)
                    if "normalise" in parts:
                        to_features(h + 1, 1)
                        to_tokens(h + 1, 1 - b, 3)
                    if "attend" in parts:
                        state_change(h, b, 1)
                    new(3)
                    if "attend" in parts:
                        output(h, b, 0)
                    if "normalise" in parts:
                        project_gate(h + 1, 1 - b, 0, "project" in parts)
                        to_features(h + 1, 2)
                    if "attend" in parts:
                        output(h, b, 1)
                    if "normalise" in parts:
                        project_gate(h + 1, 1 - b, 1, "project" in parts)
                        to_features(h + 1, 3)

                all_steps(pe, step)

            @block.scalar
            def _(act):
                act.sem_inc(g_out, C_GOUT)
                act.sem_inc(yn_done, C_YN)
                act.sem_inc(hat_done, C_HAT)
                act.sem_inc(ktok_done, C_KTOK)

                def split_qk(h, b):
                    act.wait_ge(qk_in, 48 * (h + 1))
                    act.wait_ge(qk_proj_done, 4 * (h - 1) + C_QKPROJ)
                    act.activation(qk_hi[b][:, :, :, :], raw_qk[:, :, :, :], ACT.Copy).then_inc(qk_hi_done, 1)

                def split_g(h, b):
                    act.wait_ge(g_in, 16 * (h + 1))
                    act.wait_ge(g_proj_done, 2 * (h - 1) + C_GPROJ)
                    act.activation(g_hi[b][:, :, :], raw_g[:, :, :], ACT.Copy).then_inc(g_hi_done, 1)

                def take(h, b, n):
                    kind, half = n // 2, n % 2
                    act.wait_ge(qk_proj_done, 4 * h + n + 1 + C_QKPROJ)
                    act.wait_ge(tap_done, 12 * h + C_TAP)
                    act.wait_ge(tok_done, 4 * (h - 1) + C_TOK)
                    act.activation(pre[:, kind, PAD + half * HALF:PAD + (half + 1) * HALF], proj_ps[:, n % 2, :], ACT.Copy)
                    act.activation(y[b][:, kind, half_of(half)], proj_ps[:, n % 2, :], ACT.Identity,
                                   bias=conv[b][:, kind, TAPS:TAPS + 1],
                                   scale=conv[b][:, kind, TAPS - 1:TAPS]).then_inc(qk_out, 1)

                def take_gate(h, b, half):
                    act.wait_ge(g_proj_done, 2 * h + half + 1 + C_GPROJ)
                    act.wait_ge(og_done, 2 * (h - 1) + C_OG)
                    act.activation(gate[b][:, half_of(half)], proj_ps[:, half, :], ACT.Silu).then_inc(g_out, 1)

                def silu(h, b, p):
                    z, half = p // 2, p % 2
                    act.wait_ge(tap_done, 12 * h + 6 * z + 5 + half + C_TAP)
                    act.activation(y[b][:, z, half_of(half)], y[b][:, z, half_of(half)], ACT.Silu).then_inc(silu_done, 1)

                def normalise(h, p):
                    act.wait_ge(nbias_done, 4 * h + p + 1)
                    act.wait_ge(back_done, 4 * h + p + 1)
                    for c in range(BLK):
                        last = act.activation(yn[:, p % 2, c, :], tok_ps[:, p % 2, chunk(c)], ACT.Identity,
                                              bias=nbias[:, p % 2, c:c + 1], scale=rstd[:, p % 2, c:c + 1])
                    last.then_inc(yn_done, 1)

                def hat(h, b, p):
                    z, half = p // 2, p % 2
                    act.wait_ge(back_done, 4 * h + p + 1 + C_BACK)
                    act.wait_ge(o_done, 2 * (h - 1) + C_O)
                    act.activation((qT, kT)[z][b][:, half_of(half)], back_ps[:, :], ACT.Identity,
                                   bias=norm[:, 2 * z + 1:2 * z + 2], scale=norm[:, 2 * z:2 * z + 1]).then_inc(hat_done, 1)

                def keys(h, b, half):
                    act.wait_ge(keys_turned, 2 * h + half + 1)
                    act.activation(ktok[b][:, half * BLK:(half + 1) * BLK, :].rearrange("p c k -> p (c k)"), back_ps[:, :],
                                   ACT.Copy).then_inc(ktok_done, 1)

                def step(h, b, turn, parts):
                    nh, nb = h + 1, 1 - b
                    new, middle = "project" in parts, "normalise" in parts
                    if "attend" in parts:
                        keys(h, b, 0)
                    if new:
                        take(h + 2, b, 0)
                    if middle:
                        normalise(nh, 0)
                    if "attend" in parts:
                        keys(h, b, 1)
                    if new:
                        take(h + 2, b, 1)
                    if middle:
                        normalise(nh, 1)
                        hat(nh, nb, 0)
                    if new:
                        take(h + 2, b, 2)
                    if middle:
                        hat(nh, nb, 1)
                    if "split qk" in parts:
                        split_qk(h + 3, nb)
                    if middle:
                        normalise(nh, 2)
                    if new:
                        take(h + 2, b, 3)
                    if "split g" in parts:
                        split_g(h + 2, b)
                    if middle:
                        hat(nh, nb, 2)
                    if new:
                        silu(h + 2, b, 0)
                    if middle:
                        normalise(nh, 3)
                    if new:
                        silu(h + 2, b, 1)
                    if middle:
                        take_gate(nh, nb, 0)
                        hat(nh, nb, 3)
                        take_gate(nh, nb, 1)
                    if new:
                        silu(h + 2, b, 2)
                        silu(h + 2, b, 3)

                act.preload_act_table(ACT.Silu)
                split_qk(0, 0)
                act.wait_ge(norm_in, 16)
                act.wait_ge(padded, 1)
                all_steps(act, step)

            @block.vector
            def _(dve):
                dve.sem_inc(tap_done, C_TAP)
                dve.sem_inc(state_done, C_STATE)
                dve.sem_inc(og_done, C_OG)
                dve.memset(pre[:, :, 0:PAD], 0.0).then_inc(padded, 1)

                def convolve(h, b, z, tap):
                    for half in range(2):
                        if tap == 0:
                            dve.wait_ge(qk_out, 4 * h + 2 * z + half + 1)
                        else:
                            dve.wait_ge(tap_done, 12 * h + 6 * z + 2 * tap + half - 1 + C_TAP)
                        lag = half * HALF + tap
                        dve.scalar_tensor_tensor(y[b][:, z, half_of(half)], pre[:, z, lag:lag + HALF],
                                                 conv[b][:, z, tap:tap + 1], y[b][:, z, half_of(half)],
                                                 ALU.mult, ALU.add).then_inc(tap_done, 1)

                def moments(h, p):
                    dve.wait_ge(tok_done, 4 * h + p + 1 + C_TOK)
                    for c in range(BLK):
                        dve.bn_stats(stats[:, c, :], tok_ps[:, p % 2, chunk(c)]).then_inc(stats_done, 1)
                    dve.wait_ge(stats_done, 16 * h + 4 * p + 4)
                    dve.sem_inc(aggr_begun, 1)
                    for c in range(BLK):
                        dve.bn_aggr(mv[:, p % 2, c, :], stats[:, c, :]).then_inc(aggr_done, 1)
                    dve.wait_ge(aggr_done, 16 * h + 4 * p + 4)
                    dve.tensor_scalar(ve[:, p % 2, :], mv[:, p % 2, :, 1], EPS, None, ALU.add).then_inc(ve_done, 1)

                def bias(h, p):
                    dve.wait_ge(rstd_done, 4 * h + p + 1)
                    dve.wait_ge(yn_done, 4 * h + p + 1)
                    dve.scalar_tensor_tensor(nbias[:, p % 2, :], mv[:, p % 2, :, 0], -1.0, rstd[:, p % 2, :],
                                             ALU.mult, ALU.mult).then_inc(nbias_done, 1)

                def decays(h, half):
                    if half == 0:
                        dve.wait_ge(keep_in, 16 * (h + 1))
                        dve.wait_ge(vd_done, 2 * h + C_VD)
                    for c in range(half * BLK, (half + 1) * BLK):
                        dve.tensor_tensor_scan(decay[:, chunk(c)], keep[:, chunk(c)], m.ident[:, :], 0.0,
                                               ALU.mult, ALU.add).then_inc(decay_done, 1)

                def weigh(h, half):
                    dve.wait_ge(sc_done, 2 * h + half + 1)
                    dve.wait_ge(decay_done, NT * h + BLK * (half + 1))
                    dve.wait_ge(o_done, 2 * h + half - 1 + C_O)
                    dve.tensor_tensor(probs[:, half_of(half)], so_ps[:, half, :], decay[:, half_of(half)],
                                      ALU.mult).then_inc(probs_done, 1)

                def states(h, b, turn, half):
                    dve.wait_ge(ds_done, 2 * h + half + 1 + C_DS)
                    if half == 0:
                        dve.wait_ge(v_in[b], 32 * (turn + 1))
                        dve.wait_ge(o_done, 2 * h + C_O)
                    for c in range(BLK):
                        n = half * BLK + c
                        if n == 0:
                            dve.tensor_copy(state[:, 1, :], ds_ps[:, chunk(0)]).then_inc(state_done, 1)
                        elif n < NT - 1:
                            dve.wait_ge(state_done, 7 * h + n + C_STATE)
                            dve.scalar_tensor_tensor(state[:, n + 1, :], state[:, n, :],
                                                     prod[b][:, n * P + P - 1:n * P + P], ds_ps[:, chunk(c)],
                                                     ALU.mult, ALU.add).then_inc(state_done, 1)

                def gated(h, b, half):
                    dve.wait_ge(o_done, 2 * h + half + 1 + C_O)
                    dve.wait_ge(g_out, 2 * (h + 1) + C_GOUT)
                    dve.tensor_tensor(v_all[:, ds(h, 1), half_of(half)].rearrange("p a s -> p (a s)"), so_ps[:, half, :],
                                      gate[b][:, half_of(half)], ALU.mult).then_inc(og_done, 1)

                def step(h, b, turn, parts):
                    nh = h + 1
                    new, middle, attend = "project" in parts, "normalise" in parts, "attend" in parts
                    if middle:
                        moments(nh, 0)
                    if attend:
                        decays(h, 0)
                    if middle:
                        bias(nh, 0)
                        moments(nh, 1)
                    if attend:
                        decays(h, 1)
                        weigh(h, 0)
                    if middle:
                        bias(nh, 1)
                    if new:
                        convolve(h + 2, b, 0, 0)
                    if attend:
                        weigh(h, 1)
                        states(h, b, turn, 0)
                    if middle:
                        moments(nh, 2)
                    if new:
                        convolve(h + 2, b, 0, 1)
                    if middle:
                        bias(nh, 2)
                    if attend:
                        states(h, b, turn, 1)
                    if middle:
                        moments(nh, 3)
                    if new:
                        convolve(h + 2, b, 0, 2)
                    if middle:
                        bias(nh, 3)
                    if new:
                        convolve(h + 2, b, 1, 0)
                        convolve(h + 2, b, 1, 1)
                    if attend:
                        gated(h, b, 0)
                    if new:
                        convolve(h + 2, b, 1, 2)
                    if attend:
                        gated(h, b, 1)

                all_steps(dve, step)

            @block.gpsimd
            def _(pool):
                pool.sem_inc(vd_done, C_VD)

                def split_qk(h, b):
                    pool.wait_ge(qk_hi_done, h + 1)
                    pool.tensor_tensor(qk_lo[b][:, :, :, :], raw_qk[:, :, :, :], qk_hi[b][:, :, :, :].bitcast(F32),
                                      ALU.subtract).then_inc(qk_lo_done, 1)

                def split_g(h, b):
                    pool.wait_ge(g_hi_done, h + 1)
                    pool.tensor_tensor(g_lo[b][:, :, :], raw_g[:, :, :], g_hi[b][:, :, :].bitcast(F32),
                                      ALU.subtract).then_inc(g_lo_done, 1)

                def decayed_values(h, b, turn, half):
                    if half == 0:
                        pool.wait_ge(v_in[b], 32 * (turn + 1))
                    pool.wait_ge(decay_done, NT * h + BLK * (half + 1))
                    pool.wait_ge(ds_done, 2 * h + half - 1 + C_DS)
                    at = slice(half * BLK, (half + 1) * BLK)
                    to_end = decay[:, :].rearrange("p (c t) -> p c t", t=P)[:, at, P - 1:P].to_broadcast([P, BLK, DV])
                    pool.tensor_tensor(vd[:, at, :], v[b][:, at, :], to_end, ALU.mult).then_inc(vd_done, 1)

                def decayed_queries(h, b, half):
                    pool.wait_ge(hat_done, 4 * h + 4 + C_HAT)
                    pool.wait_ge(o_done, 2 * h + half - 1 + C_O)
                    pool.tensor_tensor(qg[:, half_of(half)], qT[b][:, half_of(half)], prod[b][:, half_of(half)],
                                       ALU.mult).then_inc(qg_done, 1)

                def rstds(h, p):
                    pool.wait_ge(ve_done, 4 * h + p + 1)
                    pool.wait_ge(yn_done, 4 * h + p + 1)
                    pool.tensor_tensor(rstd[:, p % 2, :], ve[:, p % 2, :], m.neghalf[:, 0:4], ALU.pow).then_inc(rstd_done, 1)

                def step(h, b, turn, parts):
                    middle, attend = "normalise" in parts, "attend" in parts
                    if middle:
                        rstds(h + 1, 0)
                    if attend:
                        decayed_values(h, b, turn, 0)
                    if middle:
                        rstds(h + 1, 1)
                    if attend:
                        decayed_values(h, b, turn, 1)
                        decayed_queries(h, b, 0)
                    if middle:
                        rstds(h + 1, 2)
                    if attend:
                        decayed_queries(h, b, 1)
                    if "split qk" in parts:
                        split_qk(h + 3, 1 - b)
                    if middle:
                        rstds(h + 1, 3)
                    if "split g" in parts:
                        split_g(h + 2, b)

                split_qk(0, 0)
                all_steps(pool, step)


def linear_stage(m, a):
    with ExitStack() as ctx:
        v_all = m.sb("li_v_all", [P, HB, S], F32, ctx)
        rows_dram = m.rows_dram
        with ExitStack() as inner:
            heads = HeadWeights(m, a, inner)
            value_stage(m, a, v_all, rows_dram, heads.first_loads)
            head_stage(m, heads, v_all, rows_dram)
        w_hi = m.sb("li_wo_hi", [P, HB, D], F32R, ctx)
        w_lo = m.sb("li_wo_lo", [P, HB, D], F32R, ctx)
        output_stage(m, "lo", v_all, w_hi, w_lo, HB, a["b_Wo"].rearrange("(h p) n -> p h n", p=DV))


def build(nc, a, out, stages=None):
    with ExitStack() as ctx:
        m = Memory(nc, ctx)
        m.wT_dram = {tag: nc.dram_tensor(f"{tag}_wT_dram", (E, S), F32, kind="Internal").ap() for tag in ("moe1", "moe2")}
        m.rows_dram = nc.dram_tensor("linear_rows_dram", (2, HB, S), F32, kind="Internal").ap()
        stages = stages or ["attn", "moe1", "linear", "moe2"]
        load_stage(m, a)
        for stage in stages:
            if stage == "attn":
                attn_stage(m, a)
            elif stage == "linear":
                linear_stage(m, a)
            else:
                moe_stage(m, a, stage)
            m.recycle()
        stored = m.sem("stored")
        with nc.Block() as block:

            @block.sync
            def _(sp):
                sp.dma_start(out.rearrange("b (t p) d -> p (b t) d", p=P), m.x[:, :, :]).then_inc(stored, 16)
                sp.wait_ge(stored, 16)


def constants():
    pos = np.arange(S, dtype=np.float32)
    inv = (np.float32(1.0) / np.float32(10000.0) ** (np.arange(ROPE // 2, dtype=np.float32) * np.float32(2.0 / ROPE)))
    angle = (pos[:, None] * inv.astype(np.float32)[None, :]).astype(np.float32)
    cos, sin = np.cos(angle), np.sin(angle)
    q, k = np.arange(P)[:, None], np.arange(P)[None, :]
    return {
        "owner": (np.arange(P)[None, :] // INNER == np.arange(GE)[:, None]).astype(np.float32),
        "ident": np.eye(P, dtype=np.float32),
        "rope_cos": np.repeat(cos, 2, axis=1).astype(np.float32),
        "rope_sin": np.stack([-sin, sin], axis=2).reshape(S, ROPE).astype(np.float32),
        "mask_qk": np.where(k > q, NEG, 0.0).astype(np.float32),
        "mask_kq": np.where(k > q, NEG, 0.0).astype(np.float32).T,
    }


def kernel(**inputs):
    import concourse.bacc as bacc
    from concourse.bass_utils import run_bass_kernel_spmd

    nc = bacc.Bacc("TRN2", target_bir_lowering=False, num_devices=1)
    arrays, a = {}, {}
    names = {"L0_attn_a_hidden_states": "x", "L0_ffn_router_w": "router_w", "L0_ffn_w_gate": "w_gate",
             "L0_ffn_w_up": "w_up", "L0_ffn_w_down": "w_down"}
    data = {names.get(k, k.removeprefix("L0_attn_")): v for k, v in inputs.items()}
    data["conv"] = np.concatenate([np.concatenate([np.asarray(data[f"b_{z}conv_w"]).reshape(HB, DK, TAPS),
                                                   np.asarray(data[f"b_{z}conv_b"]).reshape(HB, DK, 1)], 2)
                                   for z in "qk"], 2)
    data["norm"] = np.stack([np.asarray(data[f"b_{z}n_{p}"]) for z in "qk" for p in "wb"], 1)
    for name in ("qconv_w", "qconv_b", "kconv_w", "kconv_b", "qn_w", "qn_b"):
        del data[f"b_{name}"]
    for name, v in {**data, **constants()}.items():
        v = np.ascontiguousarray(v)
        arrays[f"in_{name}_dram"] = v
        a[name] = nc.dram_tensor(f"in_{name}_dram", v.shape, mybir.dt.from_np(v.dtype), kind="ExternalInput").ap()
    out = nc.dram_tensor("out_dram", (1, S, D), F32, kind="ExternalOutput").ap()
    build(nc, a, out)
    return run_bass_kernel_spmd(nc, [arrays], core_ids=[0]).results[0]["out_dram"]
```
